# Optimizing a Trainium2 kernel written in Bass

```python
import numpy as np
import jax
import jax.numpy as jnp

def _softmax(x, axis=-1):
    return jax.nn.softmax(x, axis=axis)

def _gelu(x):
    return jax.nn.gelu(x, approximate=True)

def _silu(x):
    return jax.nn.silu(x)

def _sigmoid(x):
    return jax.nn.sigmoid(x)

def _layernorm(x, axis=-1, eps=1e-05):
    m = jnp.mean(x, axis=axis, keepdims=True)
    v = jnp.var(x, axis=axis, keepdims=True)
    return (x - m) / jnp.sqrt(v + eps)

def _scatter_add(tgt, idx, src, axis=0):
    return tgt.at[idx].add(src)

def _segment_sum(src, seg, n):
    return jax.ops.segment_sum(src, seg, n)
kernel_name = 'mk_adaln_ffn_d1_seqx_r8_d5fad7'

def setup_inputs(seed: int=0):
    np.random.seed(seed)
    _w = jnp.asarray

    def _rec_inputs():
        import jax
        import jax.numpy as jnp
        _rk = jax.random.key(seed)
        x = -0.0002928 + 1 * jax.random.normal(jax.random.fold_in(_rk, 1), (16, 128, 128), jnp.float32)
        _lenS = 128 - jax.random.randint(jax.random.fold_in(_rk, 7), (16,), 0, max(1, 128 // 4) + 1, jnp.int32)
        _lenS2 = 128 - jax.random.randint(jax.random.fold_in(_rk, 8), (16,), 0, max(1, 128 // 4) + 1, jnp.int32)
        cond_64 = -0.0184271 + 1.00439 * jax.random.normal(jax.random.fold_in(_rk, 12), (16, 64), jnp.float32)
        _validS = jnp.arange(128)[None, :] < _lenS[:, None]
        _validS2 = jnp.arange(128)[None, :] < _lenS2[:, None]
        _causal = jnp.tril(jnp.ones((128, 128), dtype=bool))
        mask_BxS_bf1 = jnp.ones((16, 128), dtype=bool)
        return (x, cond_64, mask_BxS_bf1)
    x, cond_64, mask_BxS_bf1 = _rec_inputs()

    def _L0_cond_setup():
        import jax, jax.numpy as jnp
        import numpy as np
        DIM = 128
        HEADS = 16
        DIM_HEAD = 64
        SCALE = 8.0

        def ln(x, g, eps=1e-05):
            mean = x.mean(axis=-1, keepdims=True)
            var = ((x - mean) ** 2).mean(axis=-1, keepdims=True)
            return (x - mean) * jax.lax.rsqrt(var + eps) * g

        def l2norm(t):
            n = jnp.maximum(jnp.linalg.norm(t, axis=-1, keepdims=True), 1e-12)
            return t / n

        def rel_pos_bias(n, w0, b0, g0, w1, b1, g1, w2, b2, dtype):
            pos = jnp.arange(-n + 1, n, dtype=dtype)[:, None]
            h = jax.nn.silu(ln(pos @ w0 + b0, g0))
            h = jax.nn.silu(ln(h @ w1 + b1, g1))
            h = h @ w2 + b2
            i = jnp.arange(n)
            idx = i[:, None] - i[None, :] + n - 1
            bias = h[idx]
            return jnp.transpose(bias, (2, 0, 1))
        key = jax.random.key(seed)
        ks = jax.random.split(key, 16)
        b, n = (2, 256)
        inner = HEADS * DIM_HEAD
        s = 0.02
        return {'x': jax.random.normal(ks[0], (b, n, DIM), jnp.float32), 'mask': jnp.ones((b, n), dtype=bool), 'g_norm': jnp.ones((DIM,), jnp.float32), 'Wq': jax.random.normal(ks[1], (DIM, inner), jnp.float32) * s, 'Wkv': jax.random.normal(ks[2], (DIM, 2 * DIM_HEAD), jnp.float32) * s, 'q_scale': jnp.ones((DIM_HEAD,), jnp.float32), 'k_scale': jnp.ones((DIM_HEAD,), jnp.float32), 'null_kv': jax.random.normal(ks[3], (2, DIM_HEAD), jnp.float32), 'null_attn_bias': jax.random.normal(ks[4], (HEADS,), jnp.float32), 'w0': jax.random.normal(ks[5], (1, DIM), jnp.float32) * s, 'b0': jnp.zeros((DIM,), jnp.float32), 'g0': jnp.ones((DIM,), jnp.float32), 'w1': jax.random.normal(ks[6], (DIM, DIM), jnp.float32) * s, 'b1': jnp.zeros((DIM,), jnp.float32), 'g1': jnp.ones((DIM,), jnp.float32), 'w2': jax.random.normal(ks[7], (DIM, HEADS), jnp.float32) * s, 'b2': jnp.zeros((HEADS,), jnp.float32), 'Wout': jax.random.normal(ks[8], (inner, DIM), jnp.float32) * s, 'g_out': jnp.ones((DIM,), jnp.float32)}
    _L0_cond_all = _L0_cond_setup()
    _L0_cond_in = {k: v for k, v in _L0_cond_all.items() if k in ('g_norm', 'Wq', 'Wkv', 'q_scale', 'k_scale', 'null_attn_bias', 'w0', 'b0', 'g0', 'w1', 'b1', 'g1', 'w2', 'b2', 'Wout', 'g_out')}
    del _L0_cond_all

    def _L0_ffn_setup():
        import jax, jax.numpy as jnp
        import numpy as np
        H, I, E_ROUTED, TOP_K = (128, 352, 7, 2)
        B, S = (4, 256)

        def _expert(h, g, u, d):
            return jnp.einsum('...i,hi->...h', jax.nn.silu(h @ g.T) * (h @ u.T), d)
        key = jax.random.key(seed)
        ks = jax.random.split(key, 10)
        sc = 0.02
        return {'x': jax.random.normal(ks[0], (B, S, H), dtype=jnp.float32), 'sg': jax.random.normal(ks[1], (I, H), dtype=jnp.float32) * sc, 'su': jax.random.normal(ks[2], (I, H), dtype=jnp.float32) * sc, 'sd': jax.random.normal(ks[3], (H, I), dtype=jnp.float32) * sc, 'rg': jax.random.normal(ks[4], (E_ROUTED, I, H), dtype=jnp.float32) * sc, 'ru': jax.random.normal(ks[5], (E_ROUTED, I, H), dtype=jnp.float32) * sc, 'rd': jax.random.normal(ks[6], (E_ROUTED, H, I), dtype=jnp.float32) * sc, 'wr': jax.random.normal(ks[7], (E_ROUTED, H), dtype=jnp.float32) * sc, 'rb': jnp.zeros((E_ROUTED,), dtype=jnp.float32)}
    _L0_ffn_all = _L0_ffn_setup()
    _L0_ffn_in = {k: v for k, v in _L0_ffn_all.items() if k in ('sg', 'su', 'sd', 'rg', 'ru', 'rd', 'wr', 'rb')}
    del _L0_ffn_all
    return {'x': x, 'cond_64': cond_64, 'mask_BxS_bf1': mask_BxS_bf1, 'L0_cond_g_norm': _L0_cond_in['g_norm'], 'L0_cond_Wq': _L0_cond_in['Wq'], 'L0_cond_Wkv': _L0_cond_in['Wkv'], 'L0_cond_q_scale': _L0_cond_in['q_scale'], 'L0_cond_k_scale': _L0_cond_in['k_scale'], 'L0_cond_null_attn_bias': _L0_cond_in['null_attn_bias'], 'L0_cond_w0': _L0_cond_in['w0'], 'L0_cond_b0': _L0_cond_in['b0'], 'L0_cond_g0': _L0_cond_in['g0'], 'L0_cond_w1': _L0_cond_in['w1'], 'L0_cond_b1': _L0_cond_in['b1'], 'L0_cond_g1': _L0_cond_in['g1'], 'L0_cond_w2': _L0_cond_in['w2'], 'L0_cond_b2': _L0_cond_in['b2'], 'L0_cond_Wout': _L0_cond_in['Wout'], 'L0_cond_g_out': _L0_cond_in['g_out'], 'L0_ffn_sg': _L0_ffn_in['sg'], 'L0_ffn_su': _L0_ffn_in['su'], 'L0_ffn_sd': _L0_ffn_in['sd'], 'L0_ffn_rg': _L0_ffn_in['rg'], 'L0_ffn_ru': _L0_ffn_in['ru'], 'L0_ffn_rd': _L0_ffn_in['rd'], 'L0_ffn_wr': _L0_ffn_in['wr'], 'L0_ffn_rb': _L0_ffn_in['rb']}

def reference(x, cond_64, mask_BxS_bf1, L0_cond_g_norm, L0_cond_Wq, L0_cond_Wkv, L0_cond_q_scale, L0_cond_k_scale, L0_cond_null_attn_bias, L0_cond_w0, L0_cond_b0, L0_cond_g0, L0_cond_w1, L0_cond_b1, L0_cond_g1, L0_cond_w2, L0_cond_b2, L0_cond_Wout, L0_cond_g_out, L0_ffn_sg, L0_ffn_su, L0_ffn_sd, L0_ffn_rg, L0_ffn_ru, L0_ffn_rd, L0_ffn_wr, L0_ffn_rb):
    import jax
    import jax.numpy as jnp

    def _L0_cond_ref(x, mask, g_norm, Wq, Wkv, q_scale, k_scale, null_kv, null_attn_bias, w0, b0, g0, w1, b1, g1, w2, b2, Wout, g_out):
        import jax, jax.numpy as jnp
        import numpy as np
        DIM = 128
        HEADS = 16
        DIM_HEAD = 64
        SCALE = 8.0

        def ln(x, g, eps=1e-05):
            mean = x.mean(axis=-1, keepdims=True)
            var = ((x - mean) ** 2).mean(axis=-1, keepdims=True)
            return (x - mean) * jax.lax.rsqrt(var + eps) * g

        def l2norm(t):
            n = jnp.maximum(jnp.linalg.norm(t, axis=-1, keepdims=True), 1e-12)
            return t / n

        def rel_pos_bias(n, w0, b0, g0, w1, b1, g1, w2, b2, dtype):
            pos = jnp.arange(-n + 1, n, dtype=dtype)[:, None]
            h = jax.nn.silu(ln(pos @ w0 + b0, g0))
            h = jax.nn.silu(ln(h @ w1 + b1, g1))
            h = h @ w2 + b2
            i = jnp.arange(n)
            idx = i[:, None] - i[None, :] + n - 1
            bias = h[idx]
            return jnp.transpose(bias, (2, 0, 1))
        b, n, _ = x.shape
        xn = ln(x, g_norm)
        q = (xn @ Wq).reshape(b, n, HEADS, DIM_HEAD).transpose(0, 2, 1, 3)
        kv = xn @ Wkv
        k, v = (kv[..., :DIM_HEAD], kv[..., DIM_HEAD:])
        nk = jnp.broadcast_to(null_kv[0], (b, 1, DIM_HEAD))
        nv = jnp.broadcast_to(null_kv[1], (b, 1, DIM_HEAD))
        k = jnp.concatenate([nk, k], axis=1)
        v = jnp.concatenate([nv, v], axis=1)
        q = l2norm(q) * q_scale
        k = l2norm(k) * k_scale
        sim = jnp.einsum('bhid,bjd->bhij', q, k) * SCALE
        bias = rel_pos_bias(n, w0, b0, g0, w1, b1, g1, w2, b2, q.dtype)
        null_bias = jnp.broadcast_to(null_attn_bias[:, None, None], (HEADS, n, 1))
        attn_bias = jnp.concatenate([null_bias, bias], axis=-1)
        sim = sim + attn_bias
        neg = -jnp.finfo(sim.dtype).max
        causal = jnp.triu(jnp.ones((n, n + 1), dtype=bool), k=2)
        sim = jnp.where(causal, neg, sim)
        m = jnp.pad(mask, ((0, 0), (1, 0)), constant_values=True)[:, None, None, :]
        sim = jnp.where(m, sim, neg)
        attn = jax.nn.softmax(sim, axis=-1)
        out = jnp.einsum('bhij,bjd->bhid', attn, v)
        out = out.transpose(0, 2, 1, 3).reshape(b, n, HEADS * DIM_HEAD)
        return ln(out @ Wout, g_out)

    def _L0_ffn_ref(x, sg, su, sd, rg, ru, rd, wr, rb):
        import jax, jax.numpy as jnp
        import numpy as np
        H, I, E_ROUTED, TOP_K = (128, 352, 7, 2)
        B, S = (4, 256)

        def _expert(h, g, u, d):
            return jnp.einsum('...i,hi->...h', jax.nn.silu(h @ g.T) * (h @ u.T), d)
        shared_out = _expert(x, sg, su, sd)
        logits = x @ wr.T + rb
        probs = jax.nn.softmax(logits, axis=-1)
        scores, idx = jax.lax.top_k(probs, TOP_K)
        scores = scores / scores.sum(axis=-1, keepdims=True)
        w = jnp.sum(scores[..., None] * jax.nn.one_hot(idx, E_ROUTED, dtype=x.dtype), axis=-2)
        out = shared_out
        for e in range(E_ROUTED):
            out = out + w[..., e:e + 1] * _expert(x, rg[e], ru[e], rd[e])
        return out
    x = x + _L0_ffn_ref(_L0_cond_ref(x, mask_BxS_bf1, L0_cond_g_norm, L0_cond_Wq, L0_cond_Wkv, L0_cond_q_scale, L0_cond_k_scale, cond_64, L0_cond_null_attn_bias, L0_cond_w0, L0_cond_b0, L0_cond_g0, L0_cond_w1, L0_cond_b1, L0_cond_g1, L0_cond_w2, L0_cond_b2, L0_cond_Wout, L0_cond_g_out), L0_ffn_sg, L0_ffn_su, L0_ffn_sd, L0_ffn_rg, L0_ffn_ru, L0_ffn_rd, L0_ffn_wr, L0_ffn_rb)
    return x

_drawn_inputs = setup_inputs


def setup_inputs(seed=0):
    import zlib

    import numpy as np

    out = dict(_drawn_inputs(seed))
    spreads = {'L0_cond_g_norm': (1.0, 0.6),
     'L0_cond_q_scale': (1.0, 0.6),
     'L0_cond_k_scale': (1.0, 0.6),
     'L0_cond_b0': (0.0, 0.8),
     'L0_cond_g0': (1.0, 0.6),
     'L0_cond_b1': (0.0, 0.8),
     'L0_cond_g1': (1.0, 0.6),
     'L0_cond_b2': (0.0, 0.8),
     'L0_cond_g_out': (1.0, 0.6),
     'L0_ffn_rb': (0.0, 0.8)}
    factors = {'cond_64': 5.284,
     'L0_cond_Wq': 4.954,
     'L0_cond_Wkv': 4.99,
     'L0_cond_null_attn_bias': 7.435,
     'L0_cond_w0': 8.0,
     'L0_cond_w1': 8.0,
     'L0_cond_w2': 8.0,
     'L0_cond_Wout': 4.501,
     'L0_ffn_sg': 5.387,
     'L0_ffn_su': 5.578,
     'L0_ffn_sd': 5.518,
     'L0_ffn_rg': 7.768,
     'L0_ffn_ru': 7.69,
     'L0_ffn_rd': 7.66,
     'L0_ffn_wr': 8.0}
    for name, (base, spread) in spreads.items():
        noise = np.random.default_rng([zlib.crc32(name.encode()), seed]).standard_normal(out[name].shape)
        drawn = base * np.exp(spread * noise) if base else spread * noise
        out[name] = jnp.asarray(drawn.astype(out[name].dtype))
    for name, factor in factors.items():
        out[name] = (out[name] * factor).astype(out[name].dtype)
    return out
```

```python
from contextlib import ExitStack

import concourse.bass as bass
from concourse import mybir

ALU = mybir.AluOpType
ACT = mybir.ActivationFunctionType
AX_X = mybir.AxisListType.X
F32 = mybir.dt.float32
F32R = mybir.dt.float32r
I32 = mybir.dt.int32
U32 = mybir.dt.uint32

P = 128
NEG = -1e30
EPS = 1e-5
NORM_GUARD_SQ = 1e-24
RSQRT_MAGIC = float(0x5F3759DF)


def need(eng, sem, value):
    if not isinstance(value, int) or value > 0:
        eng.wait_ge(sem, value)


def adaln_ffn_kernel(nc: bass.Bass, x, cond, mask, g_norm, wq, wkv, q_scale, k_scale, null_bias, w0, b0, g0,
                     w1, b1, g1, w2, b2, wout, g_out, shared_gate, shared_up, shared_down, routed_gate, routed_up, routed_down, router_w, router_bias, out):
    NB, S, D = x.shape
    H = null_bias.shape[0]
    DH = cond.shape[1]
    HD = H * DH
    NE, I, _ = routed_gate.shape
    assert S == P and D == P and 2 * DH == P
    SCALE = 8.0
    KEYS = S + 1
    VW = DH + 1
    HC = 4
    NCH = H // HC
    QT = HD // P
    HALF = QT // 2
    STAGES = 4
    PEEL = 4
    CHAIN = 11
    SMALL_DMAS, MLP_DMAS, EXPERT_DMAS = 4, 13, 5
    ICH = 3
    IC = -(-I // ICH)
    E = NE + 1

    ctx = ExitStack()
    with ctx:
        def sb(name, shape, dt=F32):
            return ctx.enter_context(nc.sbuf_tensor(name, shape, dt))

        def sem(name):
            return ctx.enter_context(nc.semaphore(name))

        def shared(tile, at, *shape, parts=P):
            n = 1
            for k in shape:
                n *= k
            dims = " ".join(f"d{k}" for k in range(len(shape)))
            return tile[0:parts, at:at + n].rearrange(f"p ({dims}) -> p {dims}", **{f"d{k}": v for k, v in enumerate(shape)})

        bank = [ctx.enter_context(nc.psum_tensor(f"bank{i}", [P, 512], F32)) for i in range(8)]

        bias_dram = nc.dram_tensor("bias_rows", (H, P, 2 * P), F32, kind="Internal").ap()

        ident = sb("ident", [P, P])
        xs = sb("xs", [P, NB, D])
        xn = sb("xn", [P, NB, D])
        xnT = sb("xnT", [P, NB * S])
        wq_sb = sb("wq_sb", [P, HD])
        wkv_sb = sb("wkv_sb", [P, 2 * DH])
        wo_sb = sb("wo_sb", [P, QT, D])
        gcol = sb("gcol", [P, 1])
        kq = sb("kq", [P, 3, DH])
        stat = sb("stat", [P, 8, 32])
        kraw = sb("kraw", [P, NB + 1, DH])
        KB = sb("KB", [P, NB, 2, KEYS])
        V1 = sb("V1", [P, NB, VW])
        NV = sb("NV", [H, H, VW])
        bias = sb("bias", [P, H, KEYS])
        biasm_space = sb("biasm_space", [P, 2 * H * KEYS])
        biasm = shared(biasm_space, 0, 2, H, KEYS)
        kdup = shared(biasm_space, 0, NB + 1, 2, DH)
        madd = sb("madd", [P, NB, KEYS])
        b2r = sb("b2r", [P, H])
        nullb = sb("nullb", [P, H])
        w2_sb = sb("w2_sb", [P, H])
        pos = sb("pos", [P, 1])
        bst = sb("bst", [P, 6])
        bmv = sb("bmv", [P, 2])
        brs = sb("brs", [P, 4])
        hrev = sb("hrev", [P, H])
        hrevT = sb("hrevT", [H, 2 * P])

        q_space = sb("q_space", [P, 2 * QT * P])
        qT = shared(q_space, 0, 2, QT * P)
        mlp_w = shared(q_space, 0, 1, P)
        mlp_r = shared(q_space, P, 5, P)
        hA = shared(q_space, 6 * P, P)
        hB = shared(q_space, 7 * P, P)
        sq = sb("sq", [P, QT * P])
        mask_u8 = sq[:, 0:NB * S // 4].bitcast(mask.dtype).rearrange("p (b s) -> p b s", b=NB)
        hsel = sb("hsel", [P, QT, H])
        rn = sb("rn", [P, 2, H])
        rt = sb("rt", [P, 3, 32])
        p_space = sb("p_space", [P, 2 * H * KEYS])
        Pb = shared(p_space, 0, 2, H, KEYS)
        squares = shared(p_space, 0, NB, D)
        ksq = shared(p_space, H * KEYS, NB + 1, DH)
        mx = sb("mx", [P, 2, H])
        pT = sb("pT", [P, 2, HC * P])
        pnT = sb("pnT", [H, P])
        inv_den = sb("inv_den", [P, HC])
        o_space = sb("o_space", [P, 2 * HD])
        o_sb = shared(o_space, 0, 2, HD)
        draw = shared(o_space, 0, 2, ICH * IC)
        oT_space = sb("oT_space", [P, 2 * QT * P])
        oT = shared(oT_space, 0, 2, QT * P)
        graw = shared(oT_space, 0, 2, 2, ICH, D, parts=IC)
        y_sb = xn

        GH = sb("GH", [P, E, 2, I], F32R)
        GL = sb("GL", [P, E, 2, I], F32R)
        DT = sb("DT", [IC, E, ICH, D])


        YT = xnT
        yh = sb("yh", [P, 2, P], F32R)
        yl = sb("yl", [P, 2, P], F32R)
        act_sb = shared(biasm_space, 0, 2, I)
        h_sb = shared(biasm_space, 2 * I, 2, ICH * IC)
        hT = shared(biasm_space, 2 * I + 2 * ICH * IC, 2, ICH * P, parts=IC)
        W = sb("W", [P, NB, E])
        router_sb = sb("router_sb", [NE, D])
        router_wT = sb("router_wT", [P, NE + 1])
        rbr = sb("rbr", [P, NE])
        L = shared(o_space, 0, NB, NE + 1)
        top = shared(o_space, NB * (NE + 1), NB, 8)
        topi = sb("topi", [P, NB, 8], U32)
        share = sb("share", [P, 6, NB])
        iota7 = sb("iota7", [P, NE])
        oh = shared(o_space, 2 * NB * (NE + 1), 2, NB, NE)
        gor = sb("gor", [P, D])

        dma_x, dma_wq, dma_small, dma_mask, dma_mlp, dma_wo, dma_wr = (sem(n) for n in (
            "dma_x", "dma_wq", "dma_small", "dma_mask", "dma_mlp", "dma_wo", "dma_wr"))
        dma_expert = [sem(f"dma_expert{i}") for i in range(2)]
        bias_stored, bias_loaded, out_stored = sem("bias_stored"), sem("bias_loaded"), sem("out_stored")
        const_made, pool_step, dve_step, act_step, pe_step = (sem(n) for n in (
            "const_made", "pool_step", "dve_step", "act_step", "pe_step"))
        mask_made = sem("mask_made")
        expert_turned, expert_high, expert_low, expert_down = (sem(n) for n in (
            "expert_turned", "expert_high", "expert_low", "expert_down"))
        q_made, q_kept, q_squared, sumsq_made, rnorm_step, rnorm_made = (sem(n) for n in (
            "q_made", "q_kept", "q_squared", "sumsq_made", "rnorm_step", "rnorm_made"))
        biasm_made, scored, biased, maxed, shifted, exped = (sem(n) for n in (
            "biasm_made", "scored", "biased", "maxed", "shifted", "exped"))
        p_turned, p_kept, pn_turned, pn_kept, mixed, den_made, o_kept = (sem(n) for n in (
            "p_turned", "p_kept", "pn_turned", "pn_kept", "mixed", "den_made", "o_kept"))
        o_turned, oT_kept, y_made, y_kept = (sem(n) for n in ("o_turned", "oT_kept", "y_made", "y_kept"))
        yh_made, yl_made, gate_made, up_made, silu_made, h_made, h_turned, hT_kept, down_made, fin_made = (
            sem(n) for n in ("yh_made", "yl_made", "gate_made", "up_made", "silu_made", "h_made", "h_turned",
                             "hT_kept", "down_made", "fin_made"))

        (mlp_normed, mlp_active, mlp_turned, mlp_kept, mlp_made, hrev_made, w_scaled, x_centred, x_squared, x_normed,
         x_turned, xT_kept, kv_made, k_kept, k_squared, k_normed, k_turned, kT_kept, y_centred, y_squared, y_normed,
         y_turned, yT_kept, router_turned, router_kept, logits_made, gap_made, gap_exped) = (sem(n) for n in (
             "mlp_normed mlp_active mlp_turned mlp_kept mlp_made hrev_made w_scaled x_centred x_squared x_normed "
             "x_turned xT_kept kv_made k_kept k_squared k_normed k_turned kT_kept y_centred y_squared y_normed "
             "y_turned yT_kept router_turned router_kept logits_made gap_made gap_exped").split())

        block = ctx.enter_context(nc.Block())

        def spread(ap, n):
            return ap.unsqueeze(2).to_broadcast([ap.shape[0], ap.shape[1], n])

        def row(v, n=P):
            return bass.AP(v.tensor, v.offset, [[0, n], [1, v.shape[-1]]])

        def run_steps(eng, step):
            for t in range(PEEL):
                step(t, t % 2, lambda k, t=t: 0 <= t - k < NB)
            with eng.Fori(0, (NB - PEEL) // 2) as i:
                for p in range(2):
                    step(2 * i + (PEEL + p), p, lambda k: True)
            for t in range(NB, NB + STAGES):
                step(t, t % 2, lambda k, t=t: 0 <= t - k < NB)

        def load_expert(sp, e, p):
            full = (ICH - 1) * IC
            if isinstance(e, int) and e == 0:
                ups, down = (shared_gate, shared_up), shared_down
            else:
                ups = tuple(w[bass.ds(e - 1, 1), :, :].rearrange("a i d -> (a i) d") for w in (routed_gate, routed_up))
                down = routed_down[bass.ds(e - 1, 1), :, :].rearrange("a h i -> (a h) i")
            for k, src in enumerate(ups):
                sp.dma_start(graw[:, p, k, 0:ICH - 1, :],
                             src[0:full, :].rearrange("(c p) d -> p c d", p=IC)).then_inc(dma_expert[p], 16)
                sp.dma_start(graw[0:I - full, p, k, ICH - 1, :], src[full:I, :]).then_inc(dma_expert[p], 16)
            sp.dma_start(draw[:, p, 0:I], down).then_inc(dma_expert[p], 16)

        @block.sync
        def _(sp):
            sp.dma_start(xs[:, :, :], x.rearrange("b s d -> s b d")).then_inc(dma_x, 16)
            sp.dma_start(wq_sb[:, :], wq).then_inc(dma_wq, 16)
            sp.dma_start(wkv_sb[:, :], wkv).then_inc(dma_wq, 16)
            sp.dma_start(gcol[:, :], g_norm.rearrange("(p a) -> p a", a=1)).then_inc(dma_wq, 16)
            sp.dma_start(kq[:, 0, :], row(q_scale)).then_inc(dma_small, 16)
            sp.dma_start(kq[:, 1, :], row(k_scale)).then_inc(dma_small, 16)
            sp.dma_start(kraw[:, NB, :], row(cond[0, :])).then_inc(dma_small, 16)
            sp.dma_start(NV[:, :, 0:DH], bass.AP(cond.tensor, cond[1, :].offset, [[0, H], [0, H], [1, DH]])).then_inc(dma_small, 16)
            for w in range(2):
                load_expert(sp, w, w)
            with sp.Fori(0, (E - 2) // 2) as j:
                for p in range(2):
                    sp.wait_ge(expert_turned, 3 * (2 * j + p) + 3)
                    load_expert(sp, 2 * j + (2 + p), p)
            sp.wait_ge(hrev_made, 1)
            sp.dma_start(bias_dram, hrevT[:, :].unsqueeze(1).to_broadcast([H, P, 2 * P])).then_inc(bias_stored, 16)
            sp.wait_ge(bias_stored, 16)
            sp.dma_start(bias[:, :, 0:S], bass.AP(bias_dram.tensor, P - 1, [[2 * P - 1, P], [2 * P * P, H], [1, S]])).then_inc(bias_loaded, 16)
            with sp.Fori(0, NB) as b:
                sp.wait_ge(fin_made, b + 1)
                sp.dma_start(out[bass.ds(b, 1), :, :].rearrange("a s d -> s (a d)"),
                             xs[:, bass.ds(b, 1), :].rearrange("p a d -> p (a d)")).then_inc(out_stored, 16)
            sp.wait_ge(out_stored, 16 * NB)

        @block.gpsimd
        def _(pool):
            done = 0

            def own(ins):
                nonlocal done
                done += 1
                ins.then_inc(pool_step, 1)
                pool.wait_ge(pool_step, done)

            own(nc.gpsimd.memset(ident[:, :], 0.0))
            nc.gpsimd.affine_select(out=ident[:, :], in_=ident[:, :], compare_op=ALU.not_equal, fill=1.0, base=0,
                                    pattern=[[-1, P]], channel_multiplier=1).then_inc(const_made, 1)
            own(nc.gpsimd.memset(hsel[:, :, :], 1.0))
            own(nc.gpsimd.affine_select(out=hsel[:, :, :], in_=hsel[:, :, :], compare_op=ALU.is_ge, fill=0.0, base=0,
                                        pattern=[[2 * DH, QT], [-DH, H]], channel_multiplier=1))
            nc.gpsimd.affine_select(out=hsel[:, :, :], in_=hsel[:, :, :], compare_op=ALU.is_ge, fill=0.0, base=DH - 1,
                                    pattern=[[-2 * DH, QT], [DH, H]], channel_multiplier=-1).then_inc(const_made, 1)
            nc.gpsimd.iota(pos[:, :], pattern=[[0, 1]], base=P - 1, channel_multiplier=-1,
                           allow_small_or_imprecise_dtypes=True).then_inc(const_made, 1)
            nc.gpsimd.iota(iota7[:, :], pattern=[[1, NE]], base=0, channel_multiplier=0,
                           allow_small_or_imprecise_dtypes=True).then_inc(const_made, 1)
            nc.gpsimd.memset(V1[:, :, DH:VW], 1.0).then_inc(const_made, 1)
            nc.gpsimd.memset(draw[:, :, I:ICH * IC], 0.0).then_inc(const_made, 1)
            nc.gpsimd.memset(KB[:, :, :, :], 0.0).then_inc(const_made, 1)
            nc.gpsimd.memset(hrevT[:, P:2 * P], NEG).then_inc(const_made, 1)
            nc.gpsimd.memset(W[:, :, 0:1], 1.0).then_inc(const_made, 1)
            nc.gpsimd.memset(madd[:, :, S:KEYS], 0.0).then_inc(const_made, 1)
            nc.gpsimd.memset(NV[:, :, DH:VW], 1.0).then_inc(const_made, 1)
            pool.wait_ge(dma_small, 16 * SMALL_DMAS)
            pool.wait_ge(const_made, 11)
            nc.gpsimd.affine_select(out=NV[:, :, :], in_=NV[:, :, :], compare_op=ALU.is_equal, fill=0.0, base=0,
                                    pattern=[[-1, H], [0, VW]], channel_multiplier=1).then_inc(const_made, 1)
            pool.wait_ge(mask_made, 2)
            pool.wait_ge(k_turned, NB // 4 + 1)
            pool.wait_ge(bias_loaded, 16)
            pool.wait_ge(dma_mlp, 16 * MLP_DMAS)

            def step(t, p, on):
                if on(0):
                    need(pool, biased, NCH * (t - 1))
                    nc.gpsimd.tensor_tensor(biasm[:, p, :, :], bias[:, :, :],
                                            madd[:, bass.ds(t, 1), :].to_broadcast([P, H, KEYS]),
                                            ALU.add).then_inc(biasm_made, 1)
                if on(1):
                    for c in range(NCH):
                        pool.wait_ge(maxed, NCH * (t - 1) + c + 1)
                        v = Pb[:, 1 - p, c * HC:(c + 1) * HC, :]
                        nc.gpsimd.tensor_tensor(v, v, spread(mx[:, 1 - p, c * HC:(c + 1) * HC], KEYS),
                                                ALU.subtract).then_inc(shifted, 1)

            run_steps(pool, step)

        def high_y(act, b, p):
            nc.scalar.activation(yh[:, p, :], YT[:, bass.ds(b * P, P)], ACT.Copy).then_inc(yh_made, 1)

        def keep_hT(act, n, q):
            act.wait_ge(h_turned, n + 1)
            nc.scalar.activation(hT[:, q, :], bank[4 + q][0:IC, 0:ICH * P], ACT.Copy).then_inc(hT_kept, 1)

        def keep_expert(act, e):
            for k in range(2):
                act.wait_ge(expert_turned, 3 * e + k + 1)
                nc.scalar.activation(GH[:, bass.ds(e, 1), k, :].rearrange("p a i -> p (a i)"), bank[4 + k][:, 0:I],
                                     ACT.Copy).then_inc(expert_high, 1)
            act.wait_ge(expert_turned, 3 * e + 3)
            nc.scalar.activation(DT[:, bass.ds(e, 1), :, :].rearrange("p a c d -> p (a c d)"),
                                 bank[6][0:IC, 0:ICH * P], ACT.Copy).then_inc(expert_down, 1)

        @block.scalar
        def _(act):
            act.dma_start(mask_u8[:, :, :], bass.AP(mask.tensor, 0, [[0, P], [S, NB], [1, S]])).then_inc(dma_mask, 16)
            for k, v in enumerate((b0, g0, b1, g1)):
                act.dma_start(mlp_r[:, k, :], row(v)).then_inc(dma_mlp, 16)
            act.dma_start(mlp_r[:, 4, :], row(w0[0, :])).then_inc(dma_mlp, 16)
            act.dma_start(mlp_w[:, 0, :], w1).then_inc(dma_mlp, 16)
            act.dma_start(w2_sb[:, :], w2).then_inc(dma_mlp, 16)
            act.dma_start(b2r[:, :], row(b2)).then_inc(dma_mlp, 16)
            act.dma_start(nullb[:, :], row(null_bias)).then_inc(dma_mlp, 16)
            act.dma_start(gor[:, :], row(g_out)).then_inc(dma_mlp, 16)
            act.dma_start(rbr[:, :], row(router_bias)).then_inc(dma_mlp, 16)
            act.dma_start(router_sb[:, :], router_w).then_inc(dma_mlp, 16)
            act.dma_start(wo_sb[:, :, :], wout.rearrange("(t p) n -> p t n", p=P)).then_inc(dma_mlp, 16)
            act.wait_ge(mlp_normed, 1)
            nc.scalar.activation(hA[:, :], hA[:, :], ACT.Silu).then_inc(mlp_active, 1)
            act.wait_ge(mlp_normed, 2)
            nc.scalar.activation(hA[:, :], hA[:, :], ACT.Silu).then_inc(mlp_active, 1)
            act.wait_ge(x_centred, 1)
            nc.scalar.activation(squares[:, :, :], xn[:, :, :], ACT.Square).then_inc(x_squared, 1)
            for g in range(NB // 4):
                act.wait_ge(x_turned, g + 1)
                nc.scalar.activation(xnT[:, g * 512:(g + 1) * 512], bank[g % 4][:, :], ACT.Copy).then_inc(xT_kept, 1)
            act.wait_ge(k_kept, 4)
            act.wait_ge(dma_small, 16 * SMALL_DMAS)
            nc.scalar.activation(ksq[:, :, :], kraw[:, :, :], ACT.Square).then_inc(k_squared, 1)
            for e in range(2):
                keep_expert(act, e)
            with act.Fori(0, (E - 2) // 2) as j:
                for p in range(2):
                    keep_expert(act, 2 * j + (2 + p))

            def step(t, p, on):
                q = 1 - p
                if on(2):
                    act.wait_ge(pn_turned, t - 1)
                    need(act, mixed, NCH * (t - 2))
                    nc.scalar.activation(pnT[:, :], bank[7][0:H, 0:P], ACT.Copy).then_inc(pn_kept, 1)
                for c in range(NCH):
                    if on(2):
                        n = NCH * (t - 2) + c
                        act.wait_ge(p_turned, n + 1)
                        need(act, mixed, n - 1)
                        nc.scalar.activation(pT[:, c % 2, :], bank[5][:, :], ACT.Copy).then_inc(p_kept, 1)
                    if c < 2 and on(0):
                        half = slice(c * HALF * P, (c + 1) * HALF * P)
                        act.wait_ge(q_made, 2 * t + c + 1)
                        need(act, scored, NCH * (t - 1))
                        nc.scalar.activation(qT[:, p, half], bank[4][:, :], ACT.Copy).then_inc(q_kept, 1)
                        act.wait_ge(q_kept, 2 * t + c + 1)
                        need(act, sumsq_made, t)
                        nc.scalar.activation(sq[:, half], qT[:, p, half], ACT.Square).then_inc(q_squared, 1)
                    if c >= 2 and on(3):
                        act.wait_ge(o_turned, 2 * (t - 3) + c - 1)
                        need(act, y_made, t - 3)
                        nc.scalar.activation(oT[:, q, (c - 2) * HALF * P:(c - 1) * HALF * P], bank[4][:, :],
                                             ACT.Copy).then_inc(oT_kept, 1)
                    if on(1):
                        act.wait_ge(shifted, NCH * (t - 1) + c + 1)
                        v = Pb[:, q, c * HC:(c + 1) * HC, :]
                        nc.scalar.activation(v, v, ACT.Exp).then_inc(exped, 1)

            run_steps(act, step)

            act.wait_ge(y_centred, 1)
            nc.scalar.activation(squares[:, :, :], y_sb[:, :, :], ACT.Square).then_inc(y_squared, 1)
            for g in range(NB // 4):
                act.wait_ge(y_turned, g + 1)
                nc.scalar.activation(YT[:, g * 512:(g + 1) * 512], bank[g % 4][:, :], ACT.Copy).then_inc(yT_kept, 1)
            act.wait_ge(gap_made, 1)
            nc.scalar.activation(share[:, 1, :], share[:, 0, :], ACT.Exp).then_inc(gap_exped, 1)

            with act.Fori(0, NB // 2) as i:
                for p in range(2):
                    b = 2 * i + p
                    for e in range(E):
                        if e == 0 and p == 0:
                            high_y(act, b, 0)
                            high_y(act, b + 1, 1)
                        n = E * b + e
                        act.wait_ge(gate_made, n + 1)
                        if p or e > 1:
                            act.wait_ge(h_made, n - 1)
                        nc.scalar.activation(act_sb[:, e % 2, :], bank[2 * (e % 2)][:, 0:I], ACT.Silu).then_inc(silu_made, 1)
                        if p or e >= 1:
                            keep_hT(act, n - 1, (e - 1) % 2)
                    if p:
                        keep_hT(act, E * b + E - 1, (E - 1) % 2)

        @block.vector
        def _(dve):
            done = 0

            def own(ins):
                nonlocal done
                done += 1
                ins.then_inc(dve_step, 1)
                dve.wait_ge(dve_step, done)

            def rsqrt(y, v, tmp, own):
                own(nc.vector.tensor_scalar(tmp.bitcast(I32), v.bitcast(I32), 1, None, ALU.logical_shift_right))
                own(nc.vector.tensor_scalar(y.bitcast(I32), tmp.bitcast(I32), -1.0, RSQRT_MAGIC, ALU.mult, ALU.add))
                for k in range(3):
                    own(nc.vector.tensor_tensor(tmp, y, y, ALU.mult))
                    own(nc.vector.scalar_tensor_tensor(tmp, tmp, -0.5, v, ALU.mult, ALU.mult))
                    last = nc.vector.scalar_tensor_tensor(y, tmp, 1.5, y, ALU.add, ALU.mult)
                    if k < 2:
                        own(last)
                return last

            dve.wait_ge(dma_mask, 16)
            nc.vector.tensor_scalar(madd[:, :, 0:S], mask_u8[:, :, :], 1.0, -NEG, ALU.subtract, ALU.mult).then_inc(mask_made, 1)

            def layer_norm_small(g):
                own(nc.vector.bn_stats(bst[:, :], hA[:, :]))
                own(nc.vector.bn_aggr(bmv[:, :], bst[:, :]))
                own(nc.vector.tensor_scalar(brs[:, 0:1], bmv[:, 1:2], EPS, None, ALU.add))
                own(rsqrt(brs[:, 1:2], brs[:, 0:1], brs[:, 2:3], own))
                own(nc.vector.tensor_scalar(hA[:, :], hA[:, :], bmv[:, 0:1], brs[:, 1:2], ALU.subtract, ALU.mult))
                nc.vector.tensor_tensor(hA[:, :], hA[:, :], mlp_r[:, g, :], ALU.mult).then_inc(mlp_normed, 1)

            dve.wait_ge(dma_mlp, 16 * MLP_DMAS)
            nc.vector.tensor_copy(bias[:, :, S], nullb[:, :]).then_inc(mask_made, 1)
            dve.wait_ge(dma_mlp, 16 * MLP_DMAS)
            dve.wait_ge(const_made, 11)
            own(nc.vector.scalar_tensor_tensor(hA[:, :], mlp_r[:, 4, :], pos[:, 0:1], mlp_r[:, 0, :], ALU.mult, ALU.add))
            layer_norm_small(1)
            dve.wait_ge(mlp_turned, 1)
            nc.vector.tensor_copy(hB[:, :], bank[7][:, 0:P]).then_inc(mlp_kept, 1)
            dve.wait_ge(mlp_made, 1)
            own(nc.vector.tensor_tensor(hA[:, :], bank[7][:, 0:P], mlp_r[:, 2, :], ALU.add))
            layer_norm_small(3)
            dve.wait_ge(mlp_turned, 2)
            nc.vector.tensor_copy(hB[:, :], bank[7][:, 0:P]).then_inc(mlp_kept, 1)
            dve.wait_ge(mlp_made, 2)
            nc.vector.tensor_tensor(hrev[:, :], bank[7][:, 0:H], b2r[:, :], ALU.add).then_inc(mlp_kept, 1)
            dve.wait_ge(mlp_turned, 3)
            nc.vector.tensor_copy(hrevT[:, 0:P], bank[7][0:H, 0:P]).then_inc(hrev_made, 1)

            dve.wait_ge(dma_wq, 48)
            nc.vector.tensor_scalar(wq_sb[:, :], wq_sb[:, :], gcol[:, 0:1], None, ALU.mult).then_inc(w_scaled, 1)
            nc.vector.tensor_scalar(wkv_sb[:, :], wkv_sb[:, :], gcol[:, 0:1], None, ALU.mult).then_inc(w_scaled, 1)
            dve.wait_ge(dma_small, 16 * SMALL_DMAS)
            own(nc.vector.tensor_tensor(kq[:, 2, :], kq[:, 0, :], kq[:, 1, :], ALU.mult))

            ma, va, ta, ra = (stat[:, k, 0:NB] for k in range(4))
            dve.wait_ge(dma_x, 16)
            own(nc.vector.tensor_reduce(ma, xs[:, :, :], AX_X, ALU.add))
            own(nc.vector.tensor_scalar(ma, ma, 1.0 / D, None, ALU.mult))
            nc.vector.tensor_tensor(xn[:, :, :], xs[:, :, :], spread(ma, D), ALU.subtract).then_inc(x_centred, 1)
            dve.wait_ge(x_squared, 1)
            own(nc.vector.tensor_reduce(va, squares[:, :, :], AX_X, ALU.add))
            own(nc.vector.tensor_scalar(va, va, 1.0 / D, EPS, ALU.mult, ALU.add))
            own(rsqrt(ra, va, ta, own))
            nc.vector.tensor_tensor(xn[:, :, :], xn[:, :, :], spread(ra, D), ALU.mult).then_inc(x_normed, 1)

            for g in range(NB // 4):
                dve.wait_ge(kv_made, g + 1)
                kv = bank[g % 4][:, :].rearrange("p (b n) -> p b n", b=4)
                nc.vector.tensor_copy(kraw[:, 4 * g:4 * g + 4, :], kv[:, :, 0:DH])
                nc.vector.tensor_copy(V1[:, 4 * g:4 * g + 4, 0:DH], kv[:, :, DH:2 * DH]).then_inc(k_kept, 1)
            dve.wait_ge(k_squared, 1)
            vk, tk, rk = (stat[:, 4 + k, 0:NB + 1] for k in range(3))
            own(nc.vector.tensor_reduce(vk, ksq[:, :, :], AX_X, ALU.add))
            own(nc.vector.tensor_scalar(vk, vk, NORM_GUARD_SQ, None, ALU.max))
            own(rsqrt(rk, vk, tk, own))
            own(nc.vector.tensor_tensor(kraw[:, :, :], kraw[:, :, :], spread(rk, DH), ALU.mult))
            for k in range(2):
                last = nc.vector.scalar_tensor_tensor(kdup[:, :, k, :], kraw[:, :, :], SCALE,
                                                      kq[:, 2:3, :].to_broadcast([P, NB + 1, DH]), ALU.mult, ALU.mult)
            last.then_inc(k_normed, 1)
            for g in range(NB // 4):
                dve.wait_ge(k_turned, g + 1)
                for k in range(2):
                    rows = slice(k * DH, (k + 1) * DH)
                    last = nc.vector.tensor_copy(KB[rows, 4 * g:4 * g + 4, k, 0:S],
                                                 bank[g % 4][rows, :].rearrange("p (b n) -> p b n", b=4))
                last.then_inc(kT_kept, 1)
            dve.wait_ge(k_turned, NB // 4 + 1)
            for k in range(2):
                rows = slice(k * DH, (k + 1) * DH)
                last = nc.vector.tensor_copy(KB[rows, :, k, S], bank[0][rows, 0:1].to_broadcast([DH, NB]))
            last.then_inc(kT_kept, 1)

            def low_expert(e):
                for k in range(2):
                    dve.wait_ge(expert_high, 2 * e + k + 1)
                    nc.vector.tensor_tensor(GL[:, bass.ds(e, 1), k, :].rearrange("p a i -> p (a i)"),
                                            bank[4 + k][:, 0:I],
                                            GH[:, bass.ds(e, 1), k, :].rearrange("p a i -> p (a i)").bitcast(F32),
                                            ALU.subtract).then_inc(expert_low, 1)

            for e in range(2):
                low_expert(e)
            with dve.Fori(0, (E - 2) // 2) as j:
                for p in range(2):
                    low_expert(2 * j + (2 + p))

            def step(t, p, on):
                q = 1 - p
                for c in range(NCH):
                    if on(1):
                        n = NCH * (t - 1) + c
                        dve.wait_ge(scored, n + 1)
                        if c == 0:
                            dve.wait_ge(rnorm_made, t)
                            dve.wait_ge(biasm_made, t)
                            need(dve, p_turned, NCH * (t - 2))
                            need(dve, pn_turned, t - 2)
                            need(dve, shifted, NCH * (t - 2))
                        for k in range(HC):
                            h = c * HC + k
                            src = bank[2 * (c % 2) + k // 2][:, (k % 2) * KEYS:(k % 2 + 1) * KEYS]
                            last = nc.vector.scalar_tensor_tensor(Pb[:, q, h, :], src, rn[:, q, h:h + 1],
                                                                  biasm[:, q, h, :], ALU.mult, ALU.add)
                        last.then_inc(biased, 1)
                        dve.wait_ge(biased, n + 1)
                        nc.vector.tensor_reduce(mx[:, q, c * HC:(c + 1) * HC], Pb[:, q, c * HC:(c + 1) * HC, :],
                                                AX_X, ALU.max).then_inc(maxed, 1)
                    if on(2):
                        n = NCH * (t - 2) + c
                        dve.wait_ge(mixed, n + 1)
                        av = bank[6][:, 0:HC * VW].rearrange("p (h d) -> p h d", h=HC)
                        need(dve, o_kept, n)
                        nc.vector.reciprocal(inv_den[:, :], av[:, :, DH]).then_inc(den_made, 1)
                        dve.wait_ge(den_made, n + 1)
                        if c == 0:
                            need(dve, o_turned, 2 * (t - 3))
                        nc.vector.tensor_tensor(o_sb[:, p, c * HC * DH:(c + 1) * HC * DH].rearrange("p (h d) -> p h d", h=HC),
                                                av[:, :, 0:DH], spread(inv_den[:, :], DH), ALU.mult).then_inc(o_kept, 1)
                    if c == 1 and on(4):
                        dve.wait_ge(y_made, t - 3)
                        nc.vector.tensor_copy(y_sb[:, bass.ds(t - 4, 1), :].rearrange("p a d -> p (a d)"),
                                              bank[7][:, 0:D]).then_inc(y_kept, 1)
                    if c == 2 and on(0):
                        links = 0

                        def link(ins):
                            nonlocal links
                            links += 1
                            ins.then_inc(rnorm_step, 1)
                            dve.wait_ge(rnorm_step, CHAIN * t + links)

                        dve.wait_ge(sumsq_made, t + 1)
                        link(nc.vector.tensor_scalar(rt[:, 0, 0:H], bank[7][:, 0:H], NORM_GUARD_SQ, None, ALU.max))
                        rsqrt(rn[:, p, :], rt[:, 0, 0:H], rt[:, 1, 0:H], link).then_inc(rnorm_made, 1)
                        assert links == CHAIN

            run_steps(dve, step)

            dve.wait_ge(y_kept, NB)
            own(nc.vector.tensor_reduce(ma, y_sb[:, :, :], AX_X, ALU.add))
            own(nc.vector.tensor_scalar(ma, ma, 1.0 / D, None, ALU.mult))
            nc.vector.tensor_tensor(y_sb[:, :, :], y_sb[:, :, :], spread(ma, D), ALU.subtract).then_inc(y_centred, 1)
            dve.wait_ge(y_squared, 1)
            own(nc.vector.tensor_reduce(va, squares[:, :, :], AX_X, ALU.add))
            own(nc.vector.tensor_scalar(va, va, 1.0 / D, EPS, ALU.mult, ALU.add))
            own(rsqrt(ra, va, ta, own))
            own(nc.vector.tensor_tensor(y_sb[:, :, :], y_sb[:, :, :], spread(ra, D), ALU.mult))
            nc.vector.tensor_tensor(y_sb[:, :, :], y_sb[:, :, :], gor[:, :].unsqueeze(1).to_broadcast([P, NB, D]),
                                    ALU.mult).then_inc(y_normed, 1)

            own(nc.vector.memset(L[:, :, NE:NE + 1], NEG))
            dve.wait_ge(router_turned, 1)
            nc.vector.tensor_copy(router_wT[:, 0:NE], bank[4][:, 0:NE]).then_inc(router_kept, 1)
            dve.wait_ge(logits_made, 1)
            own(nc.vector.tensor_tensor(L[:, :, 0:NE], bank[5][:, 0:NB * NE].rearrange("p (b e) -> p b e", b=NB),
                                        rbr[:, :].unsqueeze(1).to_broadcast([P, NB, NE]), ALU.add))
            for b in range(NB):
                last = nc.vector.max(top[:, b, :], L[:, b, :])
            own(last)
            for b in range(NB):
                last = nc.vector.max_index(topi[:, b, :], top[:, b, :], L[:, b, :])
            own(last)
            nc.vector.tensor_tensor(share[:, 0, :], top[:, :, 1], top[:, :, 0], ALU.subtract).then_inc(gap_made, 1)
            nc.vector.tensor_copy(share[:, 4, :], topi[:, :, 0])
            own(nc.vector.tensor_copy(share[:, 5, :], topi[:, :, 1]))
            for k in range(2):
                last = nc.vector.tensor_tensor(oh[:, k, :, :], spread(share[:, 4 + k, :], NE),
                                               iota7[:, :].unsqueeze(1).to_broadcast([P, NB, NE]), ALU.is_equal)
            own(last)
            dve.wait_ge(gap_exped, 1)
            own(nc.vector.tensor_scalar(share[:, 2, :], share[:, 1, :], 1.0, None, ALU.add))
            own(nc.vector.reciprocal(share[:, 2, :], share[:, 2, :]))
            own(nc.vector.tensor_tensor(share[:, 3, :], share[:, 2, :], share[:, 1, :], ALU.mult))
            for k in range(2):
                last = nc.vector.tensor_tensor(oh[:, k, :, :], oh[:, k, :, :], spread(share[:, 2 + k, :], NE), ALU.mult)
            own(last)
            own(nc.vector.tensor_tensor(W[:, :, 1:E], oh[:, 0, :, :], oh[:, 1, :, :], ALU.add))

            own(nc.vector.memset(h_sb[:, :, I:ICH * IC], 0.0))
            with dve.Fori(0, NB // 2) as i:
                for p in range(2):
                    b = 2 * i + p
                    if p == 0:
                        for k in range(2):
                            dve.wait_ge(yh_made, b + k + 1)
                            nc.vector.tensor_tensor(yl[:, k, :], YT[:, bass.ds((b + k) * P, P)], yh[:, k, :].bitcast(F32),
                                                    ALU.subtract).then_inc(yl_made, 1)
                    for e in range(E):
                        n = E * b + e
                        dve.wait_ge(silu_made, n + 1)
                        dve.wait_ge(up_made, n + 1)
                        if p or e > 1:
                            dve.wait_ge(h_turned, n - 1)
                        nc.vector.scalar_tensor_tensor(h_sb[:, e % 2, 0:I], act_sb[:, e % 2, :],
                                                       W[:, bass.ds(b, 1), e], bank[2 * (e % 2) + 1][:, 0:I],
                                                       ALU.mult, ALU.mult).then_inc(h_made, 1)
                    dve.wait_ge(down_made, b + 1)
                    xb = xs[:, bass.ds(b, 1), :].rearrange("p a d -> p (a d)")
                    nc.vector.tensor_tensor(xb, bank[6 + p][:, 0:D], xb, ALU.add).then_inc(fin_made, 1)

        @block.tensor
        def _(pe):
            def turn(out, in_):
                n = in_.shape[0]
                return nc.tensor.transpose(out, in_, ident[0:n, 0:n])

            def mm(out, a, b, start, stop):
                return nc.tensor.matmul(out, a, b, start=start, stop=stop, skip_group_check=True)

            pe.wait_ge(const_made, 11)
            pe.wait_ge(dma_mlp, 16 * MLP_DMAS)
            for k, w in enumerate((mlp_w[:, 0, :], w2_sb[:, :])):
                pe.wait_ge(mlp_active, k + 1)
                turn(bank[7][:, 0:P], hA[:, :]).then_inc(mlp_turned, 1)
                pe.wait_ge(mlp_kept, k + 1)
                mm(bank[7][:, 0:w.shape[1]], hB[:, :], w, True, True).then_inc(mlp_made, 1)
            pe.wait_ge(mlp_kept, 3)
            turn(bank[7][0:H, 0:P], hrev[:, :]).then_inc(mlp_turned, 1)

            pe.wait_ge(x_normed, 1)
            for b in range(NB):
                last = turn(bank[b // 4][:, (b % 4) * P:(b % 4 + 1) * P], xn[:, b, :])
                if b % 4 == 3:
                    last.then_inc(x_turned, 1)
            pe.wait_ge(w_scaled, 2)
            for b in range(NB):
                if b % 4 == 0:
                    pe.wait_ge(xT_kept, b // 4 + 1)
                last = mm(bank[b // 4][:, (b % 4) * P:(b % 4 + 1) * P], xnT[:, b * P:(b + 1) * P], wkv_sb[:, :], True, True)
                if b % 4 == 3:
                    last.then_inc(kv_made, 1)
            pe.wait_ge(k_normed, 1)
            for b in range(NB + 1):
                if b == NB:
                    pe.wait_ge(kT_kept, 1)
                last = turn(bank[b // 4 % 4][:, (b % 4) * P:(b % 4 + 1) * P], kdup[:, b, :, :].rearrange("p a d -> p (a d)"))
                if b % 4 == 3 or b == NB:
                    last.then_inc(k_turned, 1)

            def expert(n, p, first):
                for k in range(2):
                    if not first:
                        pe.wait_ge(expert_low, 2 * (n - 1) + k + 1)
                    for c in range(ICH):
                        w = min(IC, I - c * IC)
                        last = turn(bank[4 + k][:, c * IC:c * IC + w], graw[0:w, p, k, c, :])
                    last.then_inc(expert_turned, 1)
                if not first:
                    pe.wait_ge(expert_down, n)
                for c in range(ICH):
                    last = turn(bank[6][0:IC, c * P:(c + 1) * P], draw[:, p, c * IC:(c + 1) * IC])
                last.then_inc(expert_turned, 1)

            for e in range(2):
                pe.wait_ge(dma_expert[e], 16 * EXPERT_DMAS)
                expert(e, e, e == 0)
            with pe.Fori(0, (E - 2) // 2) as j:
                for p in range(2):
                    pe.wait_ge(dma_expert[p], 16 * EXPERT_DMAS * (j + 2))
                    expert(2 * j + (2 + p), p, False)

            pe.wait_ge(kT_kept, NB // 4 + 1)
            pe.wait_ge(const_made, 12)
            pe.wait_ge(expert_down, E)
            pe.wait_ge(expert_low, 2 * E)

            def step(t, p, on):
                q = 1 - p
                if isinstance(t, int) and t > NB:
                    pe.wait_ge(y_kept, t - 4)
                if on(2):
                    pe.wait_ge(exped, NCH * (t - 1))
                    need(pe, rnorm_made, min(t, NB) if isinstance(t, int) else t)
                    turn(bank[7][0:H, 0:P], Pb[:, p, :, S]).then_inc(pn_turned, 1)
                for c in range(NCH):
                    if on(1):
                        n = NCH * (t - 1) + c
                        pe.wait_ge(q_kept, 2 * t)
                        need(pe, biased, n - 1)
                        for k in range(2):
                            tile = 2 * c + k
                            last = mm(bank[2 * (c % 2) + k][:, 0:2 * KEYS], qT[:, q, tile * P:(tile + 1) * P],
                                      KB[:, bass.ds(t - 1, 1), :, :].rearrange("p a k n -> p (a k n)"), True, True)
                        last.then_inc(scored, 1)
                    if on(2):
                        n = NCH * (t - 2) + c
                        need(pe, p_kept, n)
                        for k in range(HC):
                            last = turn(bank[5][:, k * P:(k + 1) * P], Pb[:, p, c * HC + k, 0:S])
                        last.then_inc(p_turned, 1)
                    if c < 2 and on(0):
                        if c == 0:
                            need(pe, oT_kept, 2 * (t - 3))
                        else:
                            pe.wait_ge(q_kept, 2 * t + 1)
                        for k in range(HALF):
                            tile = c * HALF + k
                            last = mm(bank[4][:, k * P:(k + 1) * P], wq_sb[:, tile * P:(tile + 1) * P],
                                      xnT[:, bass.ds(t * P, P)], True, True)
                        last.then_inc(q_made, 1)
                    if c >= 2 and on(3):
                        if c == 2:
                            pe.wait_ge(o_kept, NCH * (t - 2))
                            pe.wait_ge(q_kept, 2 * t + 2 if not isinstance(t, int) or t < NB else 2 * NB)
                        else:
                            pass
                        need(pe, oT_kept, 2 * (t - 3) + c - 2)
                        for k in range(HALF):
                            tile = (c - 2) * HALF + k
                            last = turn(bank[4][:, k * P:(k + 1) * P], o_sb[:, q, tile * P:(tile + 1) * P])
                        last.then_inc(o_turned, 1)
                    if on(2):
                        n = NCH * (t - 2) + c
                        pe.wait_ge(p_kept, n + 1)
                        pe.wait_ge(pn_kept, t - 1)
                        need(pe, o_kept, n)
                        mm(bank[6][:, 0:HC * VW], pnT[:, :],
                           NV[:, c * HC:(c + 1) * HC, :].rearrange("p h d -> p (h d)"), True, False)
                        for k in range(HC):
                            last = mm(bank[6][:, k * VW:(k + 1) * VW], pT[:, c % 2, k * P:(k + 1) * P],
                                      V1[:, bass.ds(t - 2, 1), :].rearrange("p a d -> p (a d)"), False, k == HC - 1)
                        last.then_inc(mixed, 1)
                    if c == 0 and on(4):
                        if not isinstance(t, int) or t - 2 < NB:
                            pe.wait_ge(pn_kept, t - 1)
                        pe.wait_ge(oT_kept, 2 * (t - 3))
                        for k in range(QT):
                            last = mm(bank[7][:, 0:D], oT[:, p, k * P:(k + 1) * P], wo_sb[:, k, :], k == 0, k == QT - 1)
                        last.then_inc(y_made, 1)
                    if c == 1 and on(0):
                        pe.wait_ge(q_squared, 2 * t + 2)
                        need(pe, y_kept, t - 3)
                        if not isinstance(t, int) or t >= 2:
                            pe.wait_ge(pn_kept, t - 1)
                        for k in range(QT):
                            last = mm(bank[7][:, 0:H], sq[:, k * P:(k + 1) * P], hsel[:, k, :], k == 0, k == QT - 1)
                        last.then_inc(sumsq_made, 1)

            run_steps(pe, step)

            turn(bank[4][:, 0:NE], router_sb[:, :]).then_inc(router_turned, 1)
            pe.wait_ge(y_normed, 1)
            for b in range(NB):
                last = turn(bank[b // 4][:, (b % 4) * P:(b % 4 + 1) * P], y_sb[:, b, :])
                if b % 4 == 3:
                    last.then_inc(y_turned, 1)
            pe.wait_ge(router_kept, 1)
            for b in range(NB):
                if b % 4 == 0:
                    pe.wait_ge(yT_kept, b // 4 + 1)
                last = mm(bank[5][:, b * NE:(b + 1) * NE], YT[:, b * P:(b + 1) * P], router_wT[:, 0:NE], True, True)
            last.then_inc(logits_made, 1)

            def gate_up(b, e, p, n, guard):
                pe.wait_ge(yl_made, b + 1)
                if guard:
                    pe.wait_ge(h_made, n - 1)
                for k, made in ((0, gate_made), (1, up_made)):
                    o = bank[2 * (e % 2) + k][:, 0:I]
                    mm(o, yh[:, p, :], GH[:, e, k, :], True, False)
                    mm(o, yh[:, p, :], GL[:, e, k, :], False, False)
                    mm(o, yl[:, p, :], GH[:, e, k, :], False, True).then_inc(made, 1)

            def turn_h(n, q, guard):
                pe.wait_ge(h_made, n + 1)
                if guard:
                    pe.wait_ge(hT_kept, n - 1)
                for c in range(ICH):
                    last = turn(bank[4 + q][0:IC, c * P:(c + 1) * P], h_sb[:, q, c * IC:(c + 1) * IC])
                last.then_inc(h_turned, 1)

            def down(n, e, p, guard):
                pe.wait_ge(hT_kept, n + 1)
                if guard:
                    pe.wait_ge(fin_made, guard)
                for c in range(ICH):
                    last = mm(bank[6 + p][:, 0:D], hT[:, e % 2, c * P:(c + 1) * P], DT[:, e, c, :],
                              e == 0 and c == 0, e == E - 1 and c == ICH - 1)
                return last

            with pe.Fori(0, NB // 2) as i:
                for m in range(2 * E + 2):
                    if m < 2 * E:
                        p, e = divmod(m, E)
                        gate_up(2 * i + p, e, p, 2 * E * i + m, m > 1)
                    if m >= 2:
                        p, e = divmod(m - 2, E)
                        last = down(2 * E * i + (m - 2), e, p, None)
                        if e == E - 1:
                            last.then_inc(down_made, 1)
                    if 1 <= m <= 2 * E:
                        turn_h(2 * E * i + (m - 1), (m - 1) % 2, m > 2)


_INS = ['x', 'cond_64', 'mask_BxS_bf1', 'L0_cond_g_norm', 'L0_cond_Wq', 'L0_cond_Wkv', 'L0_cond_q_scale',
        'L0_cond_k_scale', 'L0_cond_null_attn_bias', 'L0_cond_w0', 'L0_cond_b0', 'L0_cond_g0', 'L0_cond_w1',
        'L0_cond_b1', 'L0_cond_g1', 'L0_cond_w2', 'L0_cond_b2', 'L0_cond_Wout', 'L0_cond_g_out', 'L0_ffn_sg',
        'L0_ffn_su', 'L0_ffn_sd', 'L0_ffn_rg', 'L0_ffn_ru', 'L0_ffn_rd', 'L0_ffn_wr', 'L0_ffn_rb']
_OUTS = [((16, 128, 128), 'float32')]


def kernel(**inputs):
    import numpy as _np
    import concourse.bacc as _bacc
    from concourse import mybir as _mybir
    from concourse.bass_utils import run_bass_kernel_spmd as _run

    nc = _bacc.Bacc("TRN2", target_bir_lowering=False, num_devices=1)
    arrays, args = {}, []
    for name in _INS:
        a = _np.ascontiguousarray(inputs[name])
        arrays[f"in_{name}_dram"] = a
        args.append(nc.dram_tensor(f"in_{name}_dram", a.shape, _mybir.dt.from_np(a.dtype), kind="ExternalInput").ap())
    for i, (shape, dtype) in enumerate(_OUTS):
        dt = _mybir.dt.from_np(_np.dtype(dtype))
        args.append(nc.dram_tensor(f"out_{i}_dram", shape, dt, kind="ExternalOutput").ap())
    adaln_ffn_kernel(nc, *args)
    r = _run(nc, [arrays], core_ids=[0])
    got = tuple(r.results[0][f"out_{i}_dram"] for i in range(len(_OUTS)))
    return got[0]
```

```python
from contextlib import ExitStack

import concourse.bass as bass
from concourse import mybir

ALU = mybir.AluOpType
ACT = mybir.ActivationFunctionType
AX_X = mybir.AxisListType.X
F32 = mybir.dt.float32
F32R = mybir.dt.float32r
I32 = mybir.dt.int32
U32 = mybir.dt.uint32

P = 128
NEG = -1e30
EPS = 1e-5
NORM_GUARD_SQ = 1e-24
RSQRT_MAGIC = float(0x5F3759DF)


def need(eng, sem, value):
    if not isinstance(value, int) or value > 0:
        eng.wait_ge(sem, value)


def adaln_ffn_kernel(nc: bass.Bass, x, cond, mask, g_norm, wq, wkv, q_scale, k_scale, null_bias, w0, b0, g0,
                     w1, b1, g1, w2, b2, wout, g_out, shared_gate, shared_up, shared_down, routed_gate, routed_up, routed_down, router_w, router_bias, out):
    NB, S, D = x.shape
    H = null_bias.shape[0]
    DH = cond.shape[1]
    HD = H * DH
    NE, I, _ = routed_gate.shape
    assert S == P and D == P and 2 * DH == P
    SCALE = 8.0
    KEYS = S + 1
    VW = DH + 1
    HC = 4
    NCH = H // HC
    QT = HD // P
    HALF = QT // 2
    STAGES = 4
    PEEL = 4
    CHAIN = 11
    SMALL_DMAS, MLP_DMAS, EXPERT_DMAS = 4, 13, 5
    NULL_ROWS = 5 * H
    ICH = 3
    IC = -(-I // ICH)
    E = NE + 1
    TOP = 2
    ROUTED = (TOP * NB * S + NE * (P - 1)) // P
    TILES = NB + ROUTED
    SHARE_AT, DEST_AT, ROW = D, D + 1, D + 2
    NOWHERE = 1 << 20
    RING = 4
    LAPS = (TILES - NB - RING) // RING

    ctx = ExitStack()
    with ctx:
        def sb(name, shape, dt=F32):
            return ctx.enter_context(nc.sbuf_tensor(name, shape, dt))

        def sem(name):
            return ctx.enter_context(nc.semaphore(name))

        def shared(tile, at, *shape, parts=P):
            n = 1
            for k in shape:
                n *= k
            dims = " ".join(f"d{k}" for k in range(len(shape)))
            return tile[0:parts, at:at + n].rearrange(f"p ({dims}) -> p {dims}", **{f"d{k}": v for k, v in enumerate(shape)})

        bank = [ctx.enter_context(nc.psum_tensor(f"bank{i}", [P, 512], F32)) for i in range(8)]

        bias_dram = nc.dram_tensor("bias_rows", (H, P, 2 * P), F32, kind="Internal").ap()
        sent_dram = nc.dram_tensor("sent_rows", (ROUTED * P, ROW), F32, kind="Internal").ap()
        result_dram = nc.dram_tensor("result_rows", (TOP * NB * S, D), F32, kind="Internal").ap()

        ident = sb("ident", [P, P])
        xs = sb("xs", [P, NB, D])
        xn = sb("xn", [P, NB, D])
        xnT = sb("xnT", [P, NB * S])
        wq_sb = sb("wq_sb", [P, HD])
        wkv_sb = sb("wkv_sb", [P, 2 * DH])
        wo_sb = sb("wo_sb", [P, QT, D])
        gcol = sb("gcol", [P, 1])
        kq = sb("kq", [P, 3, DH])
        stat = sb("stat", [P, 8, 32])
        kraw = sb("kraw", [P, NB + 1, DH])
        KB = sb("KB", [P, NB, 2, KEYS])
        V1 = sb("V1", [P, NB, VW])
        NV = sb("NV", [NULL_ROWS, H, VW], F32R)
        bias = sb("bias", [P, H, KEYS])
        biasm_space = sb("biasm_space", [P, 2 * H * KEYS])
        BIASM_FREE = 2 * ICH * IC + 2 * ICH * P
        biasm = shared(biasm_space, 0, 2, H, KEYS)
        kdup = shared(biasm_space, 0, NB + 1, 2, DH)
        madd = sb("madd", [P, NB, KEYS])
        b2r = sb("b2r", [P, H])
        nullb = sb("nullb", [P, H])
        w2_sb = sb("w2_sb", [P, H])
        pos = sb("pos", [P, 1])
        bst = sb("bst", [P, 6])
        bmv = sb("bmv", [P, 2])
        brs = sb("brs", [P, 4])
        hrev = sb("hrev", [P, H])
        hrevT = sb("hrevT", [H, 2 * P])

        q_space = sb("q_space", [P, 2 * QT * P])
        qT = shared(q_space, 0, 2, QT * P)
        mlp_w = shared(q_space, 0, 1, P)
        mlp_r = shared(q_space, P, 5, P)
        hA = shared(q_space, 6 * P, P)
        hB = shared(q_space, 7 * P, P)
        sq = sb("sq", [P, QT * P])
        mask_u8 = sq[:, 0:NB * S // 4].bitcast(mask.dtype).rearrange("p (b s) -> p b s", b=NB)
        hsel = sb("hsel", [P, QT, H])
        rn = sb("rn", [P, 2, H])
        norm_in = sb("norm_in", [P, 2, 32])
        p_space = sb("p_space", [P, 2 * H * KEYS])
        Pb = shared(p_space, 0, 2, H, KEYS)
        squares = shared(p_space, 0, NB, D)
        ksq = shared(p_space, H * KEYS, NB + 1, DH)
        null_v = shared(p_space, 0, H, VW, parts=NULL_ROWS)
        mx = sb("mx", [P, 2, H])
        pT = sb("pT", [P, 2, HC * P])
        pnT = sb("pnT", [NULL_ROWS, P], F32R)
        pn3 = sb("pn3", [P, NULL_ROWS // H, H], F32R)
        inv_den = sb("inv_den", [P, HC])
        o_space = sb("o_space", [P, 2 * HD])
        o_sb = shared(o_space, 0, 2, HD)
        draw = shared(o_space, 0, 2, ICH * IC)
        oT_space = sb("oT_space", [P, 2 * QT * P])
        oT = shared(oT_space, 0, 2, QT * P)
        graw = shared(oT_space, 0, 2, 2, ICH, D, parts=IC)
        y_sb = xn
        send = (shared(p_space, 0, NB, ROW), shared(biasm_space, BIASM_FREE, NB, ROW))

        GH = sb("GH", [P, E, 2, I], F32R)
        GL = sb("GL", [P, E, 2, I], F32R)
        DT = sb("DT", [IC, E, ICH, D])


        YT = xnT
        yh = sb("yh", [P, 2, P], F32R)
        yl = sb("yl", [P, 2, P], F32R)
        act_sb = shared(sq, 0, 2, I)
        h_sb = shared(biasm_space, 0, 2, ICH * IC)
        hT = shared(biasm_space, 2 * ICH * IC, 2, ICH * P, parts=IC)
        router_sb = sb("router_sb", [NE, D])
        router_wT = sb("router_wT", [P, NE + 1])
        rbr = sb("rbr", [P, NE])
        iota7 = sb("iota7", [P, NE])
        iota_tile = sb("iota_tile", [P, ROUTED])
        fill_row = sb("fill_row", [P, ROW])
        dest = sb("dest", [P, TOP, NB], I32)
        share = sb("share", [P, 4, NB])
        PAD = NB // 2
        EPAD = 4
        L = shared(o_space, 0, NB, NE)
        equal = shared(o_space, NB * NE, NB, NE)
        chosen = shared(o_space, 2 * NB * NE, TOP, NB, NE)
        load = shared(o_space, 4 * NB * NE, NB, NE)
        totals = shared(o_space, 5 * NB * NE, NB, NE)
        place = shared(o_space, 6 * NB * NE, NB, NE)
        placed = shared(o_space, 7 * NB * NE, TOP, NB, NE)
        run_up = shared(o_space, 9 * NB * NE, 2, PAD + NB, NE)
        tiles_up = shared(o_space, 12 * NB * NE, 2, EPAD + NE)
        best = sb("best", [P, 2, NB])
        tiles_of = sb("tiles_of", [P, NE])
        tiles_int = sb("tiles_int", [P, 2, NE], I32)
        row_of = sb("row_of", [P, TOP, NB])
        row_index = sb("row_index", [P, TOP, NB], U32)
        passed = shared(q_space, 0, ROUTED, NE - 1)
        before = shared(q_space, 2 * P, P)
        ones = shared(q_space, 3 * P, P)
        tile_float = shared(q_space, 4 * P + RING * ROW + 2 * ROUTED, ROUTED)
        TABLE = -(-ROUTED // RING) * RING + 2 * RING
        tile_expert = sb("tile_expert", [P, TABLE], I32)
        rows_in = shared(q_space, 4 * P, RING, ROW)
        share_of = shared(q_space, 4 * P + RING * ROW, ROUTED)
        dest_of = shared(q_space, 4 * P + RING * ROW + ROUTED, ROUTED).bitcast(U32)
        dest_ring = sb("dest_ring", [P, RING], U32)
        result = shared(oT_space, 0, RING, D)
        result_in = (xn, xnT[:, :].rearrange("p (b d) -> p b d", b=NB))
        gor = sb("gor", [P, D])

        dma_x, dma_wq, dma_small, dma_mask, dma_mlp, dma_wo, dma_wr = (sem(n) for n in (
            "dma_x", "dma_wq", "dma_small", "dma_mask", "dma_mlp", "dma_wo", "dma_wr"))
        dma_expert = [sem(f"dma_expert{i}") for i in range(2)]
        bias_stored, bias_loaded, out_stored = sem("bias_stored"), sem("bias_loaded"), sem("out_stored")
        const_made, pool_step, dve_step, act_step, pe_step = (sem(n) for n in (
            "const_made", "pool_step", "dve_step", "act_step", "pe_step"))
        mask_made, null_made, null_split, pn_high, pn_split = (sem(n) for n in (
            "mask_made", "null_made", "null_split", "pn_high", "pn_split"))
        expert_turned, expert_high, expert_low, expert_down = (sem(n) for n in (
            "expert_turned", "expert_high", "expert_low", "expert_down"))
        q_made, q_kept, q_squared, sumsq_made, rnorm_step, rnorm_made = (sem(n) for n in (
            "q_made", "q_kept", "q_squared", "sumsq_made", "rnorm_step", "rnorm_made"))
        biasm_made, scored, biased, maxed, shifted, exped = (sem(n) for n in (
            "biasm_made", "scored", "biased", "maxed", "shifted", "exped"))
        p_turned, p_kept, pn_turned, pn_kept, mixed, den_made, o_kept = (sem(n) for n in (
            "p_turned", "p_kept", "pn_turned", "pn_kept", "mixed", "den_made", "o_kept"))
        o_turned, oT_kept, y_made, y_kept = (sem(n) for n in ("o_turned", "oT_kept", "y_made", "y_kept"))
        yh_made, yl_made, gate_made, up_made, silu_made, h_made, h_turned, hT_kept, down_made, down_kept, fin_made = (
            sem(n) for n in ("yh_made", "yl_made", "gate_made", "up_made", "silu_made", "h_made", "h_turned",
                             "hT_kept", "down_made", "down_kept", "fin_made"))
        (rows_filled, rows_sent, sort_consts, load_made, ranks_made, table_made, row_index_made, send0_made, send1_made,
         tile_turned, dest_kept) = (sem(n) for n in (
             "rows_filled rows_sent sort_consts load_made ranks_made table_made row_index_made send0_made send1_made "
             "tile_turned dest_kept").split())
        rows_loaded = [sem(f"rows_loaded{m}") for m in range(RING)]
        result_sent = [sem(f"result_sent{m}") for m in range(RING)]
        result_loaded = [sem(f"result_loaded{g}") for g in range(NB // 4)]

        (mlp_normed, mlp_active, mlp_turned, mlp_kept, mlp_made, hrev_made, w_scaled, x_centred, x_squared, x_normed,
         x_turned, xT_kept, kv_made, k_kept, k_squared, k_normed, k_turned, kT_kept, y_centred, y_squared,
         y_turned, yT_kept, router_turned, router_kept, logits_made, gap_made, gap_exped) = (sem(n) for n in (
             "mlp_normed mlp_active mlp_turned mlp_kept mlp_made hrev_made w_scaled x_centred x_squared x_normed "
             "x_turned xT_kept kv_made k_kept k_squared k_normed k_turned kT_kept y_centred y_squared "
             "y_turned yT_kept router_turned router_kept logits_made gap_made gap_exped").split())

        block = ctx.enter_context(nc.Block())

        def spread(ap, n):
            return ap.unsqueeze(2).to_broadcast([ap.shape[0], ap.shape[1], n])

        def row(v, n=P):
            return bass.AP(v.tensor, v.offset, [[0, n], [1, v.shape[-1]]])

        def run_steps(eng, step):
            for t in range(PEEL):
                step(t, t % 2, lambda k, t=t: 0 <= t - k < NB)
            with eng.Fori(0, (NB - PEEL) // 2) as i:
                for p in range(2):
                    step(2 * i + (PEEL + p), p, lambda k: True)
            for t in range(NB, NB + STAGES):
                step(t, t % 2, lambda k, t=t: 0 <= t - k < NB)

        def run_tiles(eng, step):
            def single(u):
                step(u, u % RING, u // RING, lambda k: None if not 0 <= u - k < TILES else
                     "shared" if u - k < NB else "routed")

            for u in range(RING):
                single(u)
            with eng.Fori(0, NB // RING - 1) as i:
                for m in range(RING):
                    step(RING * i + (RING + m), m, i + 1, lambda k: "shared")
            for u in range(NB, NB + RING):
                single(u)
            with eng.Fori(0, LAPS) as i:
                for m in range(RING):
                    step(RING * i + (NB + RING + m), m, i + (NB // RING + 1), lambda k: "routed")
            for u in range(NB + RING + LAPS * RING, TILES + 3):
                single(u)

        def load_expert(sp, e, p):
            full = (ICH - 1) * IC
            if isinstance(e, int) and e == 0:
                ups, down = (shared_gate, shared_up), shared_down
            else:
                ups = tuple(w[bass.ds(e - 1, 1), :, :].rearrange("a i d -> (a i) d") for w in (routed_gate, routed_up))
                down = routed_down[bass.ds(e - 1, 1), :, :].rearrange("a h i -> (a h) i")
            for k, src in enumerate(ups):
                sp.dma_start(graw[:, p, k, 0:ICH - 1, :],
                             src[0:full, :].rearrange("(c p) d -> p c d", p=IC)).then_inc(dma_expert[p], 16)
                sp.dma_start(graw[0:I - full, p, k, ICH - 1, :], src[full:I, :]).then_inc(dma_expert[p], 16)
            sp.dma_start(draw[:, p, 0:I], down).then_inc(dma_expert[p], 16)

        @block.sync
        def _(sp):
            sp.dma_start(xs[:, :, :], x.rearrange("b s d -> s b d")).then_inc(dma_x, 16)
            sp.dma_start(wq_sb[:, :], wq).then_inc(dma_wq, 16)
            sp.dma_start(wkv_sb[:, :], wkv).then_inc(dma_wq, 16)
            sp.dma_start(gcol[:, :], g_norm.rearrange("(p a) -> p a", a=1)).then_inc(dma_wq, 16)
            sp.dma_start(kq[:, 0, :], row(q_scale)).then_inc(dma_small, 16)
            sp.dma_start(kq[:, 1, :], row(k_scale)).then_inc(dma_small, 16)
            sp.dma_start(kraw[:, NB, :], row(cond[0, :])).then_inc(dma_small, 16)
            sp.dma_start(null_v[:, :, 0:DH], bass.AP(cond.tensor, cond[1, :].offset,
                                                     [[0, NULL_ROWS], [0, H], [1, DH]])).then_inc(dma_small, 16)
            for w in range(2):
                load_expert(sp, w, w)
            with sp.Fori(0, (E - 2) // 2) as j:
                for p in range(2):
                    sp.wait_ge(expert_turned, 3 * (2 * j + p) + 3)
                    load_expert(sp, 2 * j + (2 + p), p)
            sp.wait_ge(hrev_made, 1)
            sp.dma_start(bias_dram, hrevT[:, :].unsqueeze(1).to_broadcast([H, P, 2 * P])).then_inc(bias_stored, 16)
            sp.wait_ge(bias_stored, 16)
            sp.dma_start(bias[:, :, 0:S], bass.AP(bias_dram.tensor, P - 1, [[2 * P - 1, P], [2 * P * P, H], [1, S]])).then_inc(bias_loaded, 16)
            sp.wait_ge(const_made, 19)
            sp.dma_start(sent_dram.rearrange("(t p) c -> p t c", p=P),
                         fill_row[:, :].unsqueeze(1).to_broadcast([P, ROUTED, ROW])).then_inc(rows_filled, 16)

            def load_rows(r, m):
                sp.dma_start(rows_in[:, m, :], sent_dram[bass.ds(r * P, P), :]).then_inc(rows_loaded[m], 16)

            sp.wait_ge(rows_sent, 16 * TOP * NB)
            for r in range(RING):
                load_rows(r, r)
            with sp.Fori(0, (ROUTED - RING) // RING) as i:
                for m in range(RING):
                    sp.wait_ge(dest_kept, RING * i + (m + 1))
                    load_rows(RING * i + (RING + m), m)
            for r in range(ROUTED - ROUTED % RING, ROUTED):
                sp.wait_ge(dest_kept, r - RING + 1)
                load_rows(r, r % RING)
            for m in range(RING):
                sp.wait_ge(result_sent[m], 16 * (ROUTED // RING + (m < ROUTED % RING)))
            for g in range(NB // 4):
                for k in range(TOP):
                    sp.dma_start(result_in[k][:, 4 * g:4 * g + 4, :],
                                 result_dram[(k * NB + 4 * g) * P:(k * NB + 4 * g + 4) * P, :].rearrange(
                                     "(b p) d -> p b d", p=P)).then_inc(result_loaded[g], 16)
            for g in range(NB // 4):
                sp.wait_ge(fin_made, g + 1)
                sp.dma_start(out[4 * g:4 * g + 4, :, :].rearrange("b s d -> s b d"),
                             xs[:, 4 * g:4 * g + 4, :]).then_inc(out_stored, 16)
            sp.wait_ge(out_stored, 16 * (NB // 4))

        @block.gpsimd
        def _(pool):
            done = 0

            def own(ins):
                nonlocal done
                done += 1
                ins.then_inc(pool_step, 1)
                pool.wait_ge(pool_step, done)

            own(nc.gpsimd.memset(ident[:, :], 0.0))
            nc.gpsimd.affine_select(out=ident[:, :], in_=ident[:, :], compare_op=ALU.not_equal, fill=1.0, base=0,
                                    pattern=[[-1, P]], channel_multiplier=1).then_inc(const_made, 1)
            own(nc.gpsimd.memset(hsel[:, :, :], 1.0))
            own(nc.gpsimd.affine_select(out=hsel[:, :, :], in_=hsel[:, :, :], compare_op=ALU.is_ge, fill=0.0, base=0,
                                        pattern=[[2 * DH, QT], [-DH, H]], channel_multiplier=1))
            nc.gpsimd.affine_select(out=hsel[:, :, :], in_=hsel[:, :, :], compare_op=ALU.is_ge, fill=0.0, base=DH - 1,
                                    pattern=[[-2 * DH, QT], [DH, H]], channel_multiplier=-1).then_inc(const_made, 1)
            nc.gpsimd.iota(pos[:, :], pattern=[[0, 1]], base=P - 1, channel_multiplier=-1,
                           allow_small_or_imprecise_dtypes=True).then_inc(const_made, 1)
            nc.gpsimd.iota(iota7[:, :], pattern=[[1, NE]], base=0, channel_multiplier=0,
                           allow_small_or_imprecise_dtypes=True).then_inc(const_made, 1)
            nc.gpsimd.memset(V1[:, :, DH:VW], 1.0).then_inc(const_made, 1)
            nc.gpsimd.memset(draw[:, :, I:ICH * IC], 0.0).then_inc(const_made, 1)
            nc.gpsimd.memset(KB[:, :, :, :], 0.0).then_inc(const_made, 1)
            nc.gpsimd.memset(hrevT[:, P:2 * P], NEG).then_inc(const_made, 1)
            nc.gpsimd.memset(fill_row[:, 0:DEST_AT], 0.0).then_inc(const_made, 1)
            nc.gpsimd.memset(madd[:, :, S:KEYS], 0.0).then_inc(const_made, 1)
            nc.gpsimd.memset(null_v[:, :, DH:VW], 1.0).then_inc(const_made, 1)
            nc.gpsimd.memset(NV[:, :, :].bitcast(F32), 0.0).then_inc(const_made, 1)
            nc.gpsimd.memset(pn3[:, :, :].bitcast(F32), 0.0).then_inc(const_made, 1)
            nc.gpsimd.memset(fill_row[:, DEST_AT:ROW].bitcast(I32), NOWHERE).then_inc(const_made, 1)
            nc.gpsimd.iota(iota_tile[:, :], pattern=[[1, ROUTED]], base=0, channel_multiplier=0,
                           allow_small_or_imprecise_dtypes=True).then_inc(const_made, 1)
            nc.gpsimd.iota(dest[:, :, :], pattern=[[NB * S, TOP], [S, NB]], base=0, channel_multiplier=1).then_inc(const_made, 1)
            nc.gpsimd.memset(row_index[:, :, :], 0).then_inc(const_made, 1)
            nc.gpsimd.memset(dest_ring[:, :], 0).then_inc(const_made, 1)
            nc.gpsimd.memset(tile_expert[:, :], 1).then_inc(const_made, 1)
            pool.wait_ge(dma_small, 16 * SMALL_DMAS)
            pool.wait_ge(const_made, 19)
            for at in (0, 2 * H, 4 * H):
                rows = slice(at, at + H)
                nc.gpsimd.affine_select(out=null_v[rows, :, :], in_=null_v[rows, :, :], compare_op=ALU.is_equal, fill=0.0,
                                        base=0, pattern=[[-1, H], [0, VW]], channel_multiplier=1).then_inc(null_made, 1)
            pool.wait_ge(mask_made, 2)
            pool.wait_ge(k_turned, NB // 4 + 1)
            pool.wait_ge(bias_loaded, 16)
            pool.wait_ge(dma_mlp, 16 * MLP_DMAS)

            def step(t, p, on):
                for c in range(NCH):
                    heads = slice(c * HC, (c + 1) * HC)
                    if on(1):
                        pool.wait_ge(maxed, NCH * (t - 1) + c + 1)
                        v = Pb[:, 1 - p, heads, :]
                        nc.gpsimd.tensor_tensor(v, v, spread(mx[:, 1 - p, heads], KEYS),
                                                ALU.subtract).then_inc(shifted, 1)
                    if on(0):
                        nc.gpsimd.tensor_tensor(biasm[:, p, heads, :], bias[:, heads, :],
                                                madd[:, bass.ds(t, 1), :].to_broadcast([P, HC, KEYS]),
                                                ALU.add).then_inc(biasm_made, 1)

            run_steps(pool, step)

            pool.wait_ge(y_kept, NB)
            nc.gpsimd.memset(ones[:, :], 1.0).then_inc(sort_consts, 1)
            nc.gpsimd.memset(run_up[:, :, :, :], 0.0).then_inc(sort_consts, 1)
            nc.gpsimd.memset(tiles_up[:, :, :], 0.0).then_inc(sort_consts, 1)
            pool.wait_ge(sort_consts, 3)
            nc.gpsimd.affine_select(out=before[:, :], in_=ones[:, :], compare_op=ALU.is_gt, fill=0.0, base=0,
                                    pattern=[[1, P]], channel_multiplier=-1).then_inc(sort_consts, 1)
            pool.wait_ge(rows_filled, 16)
            pool.wait_ge(row_index_made, 1)
            for k, made in ((0, send0_made), (1, send1_made)):
                pool.wait_ge(made, 3)
                for b in range(NB):
                    nc.gpsimd.indirect_dma_start(
                        out=sent_dram[:, :], out_offset=bass.IndirectOffsetOnAxis(ap=row_index[:, k, b:b + 1], axis=0),
                        in_=send[k][:, b, :], in_offset=None).then_inc(rows_sent, 16)

            def send_result(r, m):
                pool.wait_ge(down_kept, r + (NB + 1))
                nc.gpsimd.indirect_dma_start(
                    out=result_dram[:, :], out_offset=bass.IndirectOffsetOnAxis(ap=dest_ring[:, m:m + 1], axis=0),
                    in_=result[:, m, :], in_offset=None, bounds_check=TOP * NB * S - 1,
                    oob_is_err=False).then_inc(result_sent[m], 16)

            for r in range(ROUTED):
                send_result(r, r % RING)

        def keep_expert(act, e):
            for k in range(2):
                act.wait_ge(expert_turned, 3 * e + k + 1)
                nc.scalar.activation(GH[:, bass.ds(e, 1), k, :].rearrange("p a i -> p (a i)"), bank[4 + k][:, 0:I],
                                     ACT.Copy).then_inc(expert_high, 1)
            act.wait_ge(expert_turned, 3 * e + 3)
            nc.scalar.activation(DT[:, bass.ds(e, 1), :, :].rearrange("p a c d -> p (a c d)"),
                                 bank[6][0:IC, 0:ICH * P], ACT.Copy).then_inc(expert_down, 1)

        @block.scalar
        def _(act):
            act.dma_start(mask_u8[:, :, :], bass.AP(mask.tensor, 0, [[0, P], [S, NB], [1, S]])).then_inc(dma_mask, 16)
            for k, v in enumerate((b0, g0, b1, g1)):
                act.dma_start(mlp_r[:, k, :], row(v)).then_inc(dma_mlp, 16)
            act.dma_start(mlp_r[:, 4, :], row(w0[0, :])).then_inc(dma_mlp, 16)
            act.dma_start(mlp_w[:, 0, :], w1).then_inc(dma_mlp, 16)
            act.dma_start(w2_sb[:, :], w2).then_inc(dma_mlp, 16)
            act.dma_start(b2r[:, :], row(b2)).then_inc(dma_mlp, 16)
            act.dma_start(nullb[:, :], row(null_bias)).then_inc(dma_mlp, 16)
            act.dma_start(gor[:, :], row(g_out)).then_inc(dma_mlp, 16)
            act.dma_start(rbr[:, :], row(router_bias)).then_inc(dma_mlp, 16)
            act.dma_start(router_sb[:, :], router_w).then_inc(dma_mlp, 16)
            act.dma_start(wo_sb[:, :, :], wout.rearrange("(t p) n -> p t n", p=P)).then_inc(dma_mlp, 16)
            act.wait_ge(mlp_normed, 1)
            nc.scalar.activation(hA[:, :], hA[:, :], ACT.Silu).then_inc(mlp_active, 1)
            act.wait_ge(mlp_normed, 2)
            nc.scalar.activation(hA[:, :], hA[:, :], ACT.Silu).then_inc(mlp_active, 1)
            act.wait_ge(x_centred, 1)
            nc.scalar.activation(squares[:, :, :], xn[:, :, :], ACT.Square).then_inc(x_squared, 1)
            for g in range(NB // 4):
                act.wait_ge(x_turned, g + 1)
                nc.scalar.activation(xnT[:, g * 512:(g + 1) * 512], bank[g % 4][:, :], ACT.Copy).then_inc(xT_kept, 1)
            act.wait_ge(k_kept, 4)
            act.wait_ge(dma_small, 16 * SMALL_DMAS)
            nc.scalar.activation(ksq[:, :, :], kraw[:, :, :], ACT.Square).then_inc(k_squared, 1)
            for e in range(2):
                keep_expert(act, e)
            with act.Fori(0, (E - 2) // 2) as j:
                for p in range(2):
                    keep_expert(act, 2 * j + (2 + p))

            def step(t, p, on):
                q = 1 - p

                def keep_q(c):
                    if on(0):
                        half = slice(c * HALF * P, (c + 1) * HALF * P)
                        act.wait_ge(q_made, 2 * t + c + 1)
                        need(act, scored, NCH * (t - 1))
                        nc.scalar.activation(qT[:, p, half], bank[4][:, :], ACT.Copy).then_inc(q_kept, 1)
                        act.wait_ge(q_kept, 2 * t + c + 1)
                        need(act, sumsq_made, t)
                        nc.scalar.activation(sq[:, half], qT[:, p, half], ACT.Square).then_inc(q_squared, 1)

                def exp(c, back=1):
                    if on(back):
                        act.wait_ge(shifted, NCH * (t - back) + c + 1)
                        v = Pb[:, q if back == 1 else p, c * HC:(c + 1) * HC, :]
                        nc.scalar.activation(v, v, ACT.Exp).then_inc(exped, 1)

                def keep_pn():
                    if on(2):
                        act.wait_ge(pn_turned, t - 1)
                        need(act, mixed, NCH * (t - 2))
                        nc.scalar.activation(pnT[:, :], bank[7][0:NULL_ROWS, 0:P], ACT.Copy).then_inc(pn_kept, 1)

                def keep_pT(c):
                    if on(2):
                        n = NCH * (t - 2) + c
                        act.wait_ge(p_turned, n + 1)
                        need(act, mixed, n - 1)
                        nc.scalar.activation(pT[:, c % 2, :], bank[5][:, :], ACT.Copy).then_inc(p_kept, 1)

                def keep_oT(c):
                    if on(3):
                        act.wait_ge(o_turned, 2 * (t - 3) + c + 1)
                        need(act, y_made, t - 3)
                        nc.scalar.activation(oT[:, q, c * HALF * P:(c + 1) * HALF * P], bank[4][:, :],
                                             ACT.Copy).then_inc(oT_kept, 1)

                exp(3, back=2)
                keep_q(0)
                keep_pn()
                keep_pT(0)
                keep_q(1)
                exp(0)
                keep_pT(1)
                exp(1)
                keep_pT(2)
                keep_oT(0)
                keep_pT(3)
                exp(2)
                keep_oT(1)

            run_steps(act, step)

            act.wait_ge(y_centred, 1)
            nc.scalar.activation(squares[:, :, :], y_sb[:, :, :], ACT.Square).then_inc(y_squared, 1)
            for g in range(NB // 4):
                act.wait_ge(y_turned, g + 1)
                nc.scalar.activation(YT[:, g * 512:(g + 1) * 512], bank[g % 4][:, :], ACT.Copy).then_inc(yT_kept, 1)
            act.wait_ge(send0_made, 1)
            nc.scalar.activation(send[1][:, :, 0:D], send[0][:, :, 0:D], ACT.Copy).then_inc(send1_made, 1)
            act.wait_ge(gap_made, 1)
            nc.scalar.activation(share[:, 1, :], share[:, 3, :], ACT.Exp).then_inc(gap_exped, 1)

            def step(u, m, lap, kind):
                if kind(3):
                    n = u - 3
                    act.wait_ge(h_turned, n + 1)
                    need(act, down_made, n - 1)
                    nc.scalar.activation(hT[:, (m - 3) % 2, :], bank[4 + (m - 3) % 2][0:IC, 0:ICH * P],
                                         ACT.Copy).then_inc(hT_kept, 1)
                if kind(0):
                    need(act, up_made, u - 1)
                    if kind(0) == "shared":
                        src = YT[:, bass.ds(u * P, P)]
                    else:
                        act.wait_ge(tile_turned, u - (NB - 1))
                        src = bank[6][:, 0:P]
                    nc.scalar.activation(yh[:, m % 2, :], src, ACT.Copy).then_inc(yh_made, 1)
                if kind(1):
                    n = u - 1
                    act.wait_ge(gate_made, n + 1)
                    need(act, h_made, n - 1)
                    nc.scalar.activation(act_sb[:, (m - 1) % 2, :], bank[2 * ((m - 1) % 2)][:, 0:I], ACT.Silu).then_inc(silu_made, 1)

            run_tiles(act, step)

        @block.vector
        def _(dve):
            done = 0

            def own(ins):
                nonlocal done
                done += 1
                ins.then_inc(dve_step, 1)
                dve.wait_ge(dve_step, done)

            def rsqrt(y, v, tmp, own):
                own(nc.vector.tensor_scalar(tmp.bitcast(I32), v.bitcast(I32), 1, None, ALU.logical_shift_right))
                own(nc.vector.tensor_scalar(y.bitcast(I32), tmp.bitcast(I32), -1.0, RSQRT_MAGIC, ALU.mult, ALU.add))
                for k in range(3):
                    own(nc.vector.tensor_tensor(tmp, y, y, ALU.mult))
                    own(nc.vector.scalar_tensor_tensor(tmp, tmp, -0.5, v, ALU.mult, ALU.mult))
                    last = nc.vector.scalar_tensor_tensor(y, tmp, 1.5, y, ALU.add, ALU.mult)
                    if k < 2:
                        own(last)
                return last

            dve.wait_ge(dma_mask, 16)
            nc.vector.tensor_scalar(madd[:, :, 0:S], mask_u8[:, :, :], 1.0, -NEG, ALU.subtract, ALU.mult).then_inc(mask_made, 1)

            def layer_norm_small(g):
                own(nc.vector.bn_stats(bst[:, :], hA[:, :]))
                own(nc.vector.bn_aggr(bmv[:, :], bst[:, :]))
                own(nc.vector.tensor_scalar(brs[:, 0:1], bmv[:, 1:2], EPS, None, ALU.add))
                own(rsqrt(brs[:, 1:2], brs[:, 0:1], brs[:, 2:3], own))
                own(nc.vector.tensor_scalar(hA[:, :], hA[:, :], bmv[:, 0:1], brs[:, 1:2], ALU.subtract, ALU.mult))
                nc.vector.tensor_tensor(hA[:, :], hA[:, :], mlp_r[:, g, :], ALU.mult).then_inc(mlp_normed, 1)

            dve.wait_ge(dma_mlp, 16 * MLP_DMAS)
            nc.vector.tensor_copy(bias[:, :, S], nullb[:, :]).then_inc(mask_made, 1)
            dve.wait_ge(dma_mlp, 16 * MLP_DMAS)
            dve.wait_ge(const_made, 19)
            own(nc.vector.scalar_tensor_tensor(hA[:, :], mlp_r[:, 4, :], pos[:, 0:1], mlp_r[:, 0, :], ALU.mult, ALU.add))
            layer_norm_small(1)
            dve.wait_ge(mlp_turned, 1)
            nc.vector.tensor_copy(hB[:, :], bank[7][:, 0:P]).then_inc(mlp_kept, 1)
            dve.wait_ge(mlp_made, 1)
            own(nc.vector.tensor_tensor(hA[:, :], bank[7][:, 0:P], mlp_r[:, 2, :], ALU.add))
            layer_norm_small(3)
            dve.wait_ge(mlp_turned, 2)
            nc.vector.tensor_copy(hB[:, :], bank[7][:, 0:P]).then_inc(mlp_kept, 1)
            dve.wait_ge(mlp_made, 2)
            nc.vector.tensor_tensor(hrev[:, :], bank[7][:, 0:H], b2r[:, :], ALU.add).then_inc(mlp_kept, 1)
            dve.wait_ge(mlp_turned, 3)
            nc.vector.tensor_copy(hrevT[:, 0:P], bank[7][0:H, 0:P]).then_inc(hrev_made, 1)

            dve.wait_ge(dma_wq, 48)
            nc.vector.tensor_scalar(wq_sb[:, :], wq_sb[:, :], gcol[:, 0:1], None, ALU.mult).then_inc(w_scaled, 1)
            nc.vector.tensor_scalar(wkv_sb[:, :], wkv_sb[:, :], gcol[:, 0:1], None, ALU.mult).then_inc(w_scaled, 1)
            dve.wait_ge(dma_small, 16 * SMALL_DMAS)
            dve.wait_ge(null_made, 3)
            for at in (0, 2 * H, 4 * H):
                rows = slice(at, at + H)
                nc.vector.tensor_copy(NV[rows, :, :], null_v[rows, :, :]).then_inc(null_split, 1)
            rows = slice(2 * H, 3 * H)
            dve.wait_ge(null_split, 3)
            nc.vector.tensor_tensor(NV[rows, :, :], null_v[rows, :, :], NV[rows, :, :].bitcast(F32), ALU.subtract).then_inc(null_split, 1)
            own(nc.vector.tensor_tensor(kq[:, 2, :], kq[:, 0, :], kq[:, 1, :], ALU.mult))

            ma, va, ta, ra = (stat[:, k, 0:NB] for k in range(4))
            dve.wait_ge(dma_x, 16)
            own(nc.vector.tensor_reduce(ma, xs[:, :, :], AX_X, ALU.add))
            own(nc.vector.tensor_scalar(ma, ma, 1.0 / D, None, ALU.mult))
            nc.vector.tensor_tensor(xn[:, :, :], xs[:, :, :], spread(ma, D), ALU.subtract).then_inc(x_centred, 1)
            dve.wait_ge(x_squared, 1)
            own(nc.vector.tensor_reduce(va, squares[:, :, :], AX_X, ALU.add))
            own(nc.vector.tensor_scalar(va, va, 1.0 / D, EPS, ALU.mult, ALU.add))
            own(rsqrt(ra, va, ta, own))
            nc.vector.tensor_tensor(xn[:, :, :], xn[:, :, :], spread(ra, D), ALU.mult).then_inc(x_normed, 1)

            for g in range(NB // 4):
                dve.wait_ge(kv_made, g + 1)
                kv = bank[g % 4][:, :].rearrange("p (b n) -> p b n", b=4)
                nc.vector.tensor_copy(kraw[:, 4 * g:4 * g + 4, :], kv[:, :, 0:DH])
                nc.vector.tensor_copy(V1[:, 4 * g:4 * g + 4, 0:DH], kv[:, :, DH:2 * DH]).then_inc(k_kept, 1)
            dve.wait_ge(k_squared, 1)
            vk, tk, rk = (stat[:, 4 + k, 0:NB + 1] for k in range(3))
            own(nc.vector.tensor_reduce(vk, ksq[:, :, :], AX_X, ALU.add))
            own(nc.vector.tensor_scalar(vk, vk, NORM_GUARD_SQ, None, ALU.max))
            own(rsqrt(rk, vk, tk, own))
            own(nc.vector.tensor_tensor(kraw[:, :, :], kraw[:, :, :], spread(rk, DH), ALU.mult))
            for k in range(2):
                last = nc.vector.scalar_tensor_tensor(kdup[:, :, k, :], kraw[:, :, :], SCALE,
                                                      kq[:, 2:3, :].to_broadcast([P, NB + 1, DH]), ALU.mult, ALU.mult)
            last.then_inc(k_normed, 1)
            for g in range(NB // 4):
                dve.wait_ge(k_turned, g + 1)
                for k in range(2):
                    rows = slice(k * DH, (k + 1) * DH)
                    last = nc.vector.tensor_copy(KB[rows, 4 * g:4 * g + 4, k, 0:S],
                                                 bank[g % 4][rows, :].rearrange("p (b n) -> p b n", b=4))
                last.then_inc(kT_kept, 1)
            dve.wait_ge(k_turned, NB // 4 + 1)
            for k in range(2):
                rows = slice(k * DH, (k + 1) * DH)
                last = nc.vector.tensor_copy(KB[rows, :, k, S], bank[0][rows, 0:1].to_broadcast([DH, NB]))
            last.then_inc(kT_kept, 1)

            def low_expert(e):
                for k in range(2):
                    dve.wait_ge(expert_high, 2 * e + k + 1)
                    nc.vector.tensor_tensor(GL[:, bass.ds(e, 1), k, :].rearrange("p a i -> p (a i)"),
                                            bank[4 + k][:, 0:I],
                                            GH[:, bass.ds(e, 1), k, :].rearrange("p a i -> p (a i)").bitcast(F32),
                                            ALU.subtract).then_inc(expert_low, 1)

            for e in range(2):
                low_expert(e)
            with dve.Fori(0, (E - 2) // 2) as j:
                for p in range(2):
                    low_expert(2 * j + (2 + p))

            def step(t, p, on):
                q = 1 - p

                def scores(c):
                    if on(1):
                        n = NCH * (t - 1) + c
                        dve.wait_ge(scored, n + 1)
                        dve.wait_ge(biasm_made, n + 1)
                        if c == 0:
                            dve.wait_ge(rnorm_made, t)
                            need(dve, p_turned, NCH * (t - 2))
                            need(dve, pn_split, t - 2)
                            need(dve, shifted, NCH * (t - 2))
                        for k in range(HC):
                            h = c * HC + k
                            src = bank[2 * (c % 2) + k // 2][:, (k % 2) * KEYS:(k % 2 + 1) * KEYS]
                            last = nc.vector.scalar_tensor_tensor(Pb[:, q, h, :], src, rn[:, q, h:h + 1],
                                                                  biasm[:, q, h, :], ALU.mult, ALU.add)
                        last.then_inc(biased, 1)
                        dve.wait_ge(biased, n + 1)
                        nc.vector.tensor_reduce(mx[:, q, c * HC:(c + 1) * HC], Pb[:, q, c * HC:(c + 1) * HC, :],
                                                AX_X, ALU.max).then_inc(maxed, 1)

                def split_pn():
                    if on(2):
                        dve.wait_ge(exped, NCH * (t - 1))
                        need(dve, pn_turned, t - 2)
                        nc.vector.tensor_copy(pn3[:, 0, :], Pb[:, p, :, S]).then_inc(pn_high, 1)
                        dve.wait_ge(pn_high, t - 1)
                        nc.vector.tensor_copy(pn3[:, 2, :], pn3[:, 0, :].bitcast(F32))
                        nc.vector.tensor_tensor(pn3[:, 4, :], Pb[:, p, :, S], pn3[:, 0, :].bitcast(F32),
                                                ALU.subtract).then_inc(pn_split, 1)

                def keep_o(c):
                    if on(2):
                        n = NCH * (t - 2) + c
                        dve.wait_ge(mixed, n + 1)
                        av = bank[6][:, 0:HC * VW].rearrange("p (h d) -> p h d", h=HC)
                        need(dve, o_kept, n)
                        nc.vector.reciprocal(inv_den[:, :], av[:, :, DH]).then_inc(den_made, 1)
                        dve.wait_ge(den_made, n + 1)
                        if c == 0:
                            need(dve, o_turned, 2 * (t - 3))
                        nc.vector.tensor_tensor(o_sb[:, p, c * HC * DH:(c + 1) * HC * DH].rearrange("p (h d) -> p h d", h=HC),
                                                av[:, :, 0:DH], spread(inv_den[:, :], DH), ALU.mult).then_inc(o_kept, 1)

                def keep_y():
                    if on(4):
                        dve.wait_ge(y_made, t - 3)
                        nc.vector.tensor_copy(y_sb[:, bass.ds(t - 4, 1), :].rearrange("p a d -> p (a d)"),
                                              bank[7][:, 0:D]).then_inc(y_kept, 1)

                def norms():
                    if on(0):
                        links = 0

                        def link(ins):
                            nonlocal links
                            links += 1
                            ins.then_inc(rnorm_step, 1)
                            dve.wait_ge(rnorm_step, CHAIN * t + links)

                        dve.wait_ge(sumsq_made, t + 1)
                        link(nc.vector.tensor_scalar(norm_in[:, 0, 0:H], bank[7][:, 0:H], NORM_GUARD_SQ, None, ALU.max))
                        rsqrt(rn[:, p, :], norm_in[:, 0, 0:H], norm_in[:, 1, 0:H], link).then_inc(rnorm_made, 1)
                        assert links == CHAIN

                split_pn()
                scores(0)
                scores(1)
                keep_o(0)
                keep_y()
                keep_o(1)
                scores(2)
                norms()
                keep_o(2)
                scores(3)
                keep_o(3)

            run_steps(dve, step)

            dve.wait_ge(y_kept, NB)
            own(nc.vector.tensor_reduce(ma, y_sb[:, :, :], AX_X, ALU.add))
            own(nc.vector.tensor_scalar(ma, ma, 1.0 / D, None, ALU.mult))
            nc.vector.tensor_tensor(y_sb[:, :, :], y_sb[:, :, :], spread(ma, D), ALU.subtract).then_inc(y_centred, 1)
            dve.wait_ge(y_squared, 1)
            own(nc.vector.tensor_reduce(va, squares[:, :, :], AX_X, ALU.add))
            own(nc.vector.tensor_scalar(va, va, 1.0 / D, EPS, ALU.mult, ALU.add))
            own(rsqrt(ra, va, ta, own))
            own(nc.vector.tensor_tensor(send[0][:, :, 0:D], y_sb[:, :, :], spread(ra, D), ALU.mult))
            nc.vector.tensor_tensor(send[0][:, :, 0:D], send[0][:, :, 0:D], gor[:, :].unsqueeze(1).to_broadcast([P, NB, D]),
                                    ALU.mult).then_inc(send0_made, 1)

            dve.wait_ge(router_turned, 1)
            nc.vector.tensor_copy(router_wT[:, 0:NE], bank[4][:, 0:NE]).then_inc(router_kept, 1)
            for k in range(TOP):
                nc.vector.tensor_copy(send[k][:, :, DEST_AT].bitcast(I32), dest[:, k, :]).then_inc((send0_made, send1_made)[k], 1)
            dve.wait_ge(logits_made, 1)
            own(nc.vector.tensor_tensor(L[:, :, :], bank[5][:, 0:NB * NE].rearrange("p (b e) -> p b e", b=NB),
                                        rbr[:, :].unsqueeze(1).to_broadcast([P, NB, NE]), ALU.add))
            for k in range(TOP):
                own(nc.vector.tensor_reduce(best[:, k, :], L[:, :, :], AX_X, ALU.max))
                own(nc.vector.tensor_tensor(equal[:, :, :], L[:, :, :], spread(best[:, k, :], NE), ALU.is_equal))
                own(nc.vector.scalar_tensor_tensor(equal[:, :, :], equal[:, :, :], -float(NE),
                                                   iota7[:, :].unsqueeze(1).to_broadcast([P, NB, NE]), ALU.mult, ALU.add))
                own(nc.vector.tensor_reduce(share[:, 0, :], equal[:, :, :], AX_X, ALU.min))
                own(nc.vector.tensor_tensor(chosen[:, k, :, :], equal[:, :, :], spread(share[:, 0, :], NE), ALU.is_equal))
                if k == 0:
                    own(nc.vector.scalar_tensor_tensor(L[:, :, :], chosen[:, 0, :, :], 2 * NEG, L[:, :, :], ALU.mult, ALU.add))
            nc.vector.tensor_tensor(load[:, :, :], chosen[:, 0, :, :], chosen[:, 1, :, :], ALU.add).then_inc(load_made, 1)
            nc.vector.tensor_tensor(share[:, 3, :], best[:, 1, :], best[:, 0, :], ALU.subtract).then_inc(gap_made, 1)

            dve.wait_ge(sort_consts, 4)
            dve.wait_ge(ranks_made, 1)
            tot = bank[7][:, 0:NB * NE].rearrange("p (b e) -> p b e", b=NB)
            nc.vector.tensor_copy(totals[:, :, :], tot)
            own(nc.vector.tensor_copy(run_up[:, 0, PAD:PAD + NB, :], tot))
            own(nc.vector.tensor_tensor(place[:, :, :], bank[6][:, 0:NB * NE].rearrange("p (b e) -> p b e", b=NB),
                                        totals[:, :, :], ALU.subtract))
            side, far = 0, 1
            while far < NB:
                own(nc.vector.tensor_tensor(run_up[:, 1 - side, PAD:PAD + NB, :], run_up[:, side, PAD:PAD + NB, :],
                                            run_up[:, side, PAD - far:PAD - far + NB, :], ALU.add))
                side, far = 1 - side, 2 * far
            own(nc.vector.tensor_tensor(place[:, :, :], place[:, :, :], run_up[:, side, PAD:PAD + NB, :], ALU.add))
            own(nc.vector.tensor_scalar(tiles_int[:, 0, :], run_up[:, side, PAD + NB - 1, :], float(P - 1), None, ALU.add))
            own(nc.vector.tensor_scalar(tiles_int[:, 1, :], tiles_int[:, 0, :], P.bit_length() - 1, None, ALU.logical_shift_right))
            nc.vector.tensor_copy(tiles_of[:, :], tiles_int[:, 1, :])
            own(nc.vector.tensor_copy(tiles_up[:, 0, EPAD:EPAD + NE], tiles_int[:, 1, :]))
            side, far = 0, 1
            while far < NE:
                own(nc.vector.tensor_tensor(tiles_up[:, 1 - side, EPAD:EPAD + NE], tiles_up[:, side, EPAD:EPAD + NE],
                                            tiles_up[:, side, EPAD - far:EPAD - far + NE], ALU.add))
                side, far = 1 - side, 2 * far
            ends = tiles_up[:, side, EPAD:EPAD + NE]
            own(nc.vector.tensor_tensor(tiles_of[:, :], ends, tiles_of[:, :], ALU.subtract))
            own(nc.vector.scalar_tensor_tensor(place[:, :, :], tiles_of[:, :].unsqueeze(1).to_broadcast([P, NB, NE]), float(P),
                                               place[:, :, :], ALU.mult, ALU.add))
            for k in range(TOP):
                last = nc.vector.tensor_tensor(placed[:, k, :, :], chosen[:, k, :, :], place[:, :, :], ALU.mult)
            own(last)
            own(nc.vector.tensor_reduce(row_of[:, :, :], placed[:, :, :, :], AX_X, ALU.add))
            nc.vector.tensor_copy(row_index[:, :, :], row_of[:, :, :]).then_inc(row_index_made, 1)
            dve.wait_ge(gap_exped, 1)
            own(nc.vector.tensor_scalar(share[:, 2, :], share[:, 1, :], 1.0, None, ALU.add))
            own(nc.vector.reciprocal(share[:, 2, :], share[:, 2, :]))
            nc.vector.tensor_copy(send[0][:, :, SHARE_AT], share[:, 2, :]).then_inc(send0_made, 1)
            nc.vector.tensor_tensor(send[1][:, :, SHARE_AT], share[:, 2, :], share[:, 1, :], ALU.mult).then_inc(send1_made, 1)
            own(nc.vector.tensor_tensor(passed[:, :, :], spread(iota_tile[:, :], NE - 1),
                                        ends[:, 0:NE - 1].unsqueeze(1).to_broadcast([P, ROUTED, NE - 1]), ALU.is_ge))
            own(nc.vector.tensor_reduce(tile_float[:, :], passed[:, :, :], AX_X, ALU.add))
            nc.vector.tensor_scalar(tile_expert[:, RING:RING + ROUTED], tile_float[:, :], 1.0, None, ALU.add).then_inc(table_made, 1)

            own(nc.vector.memset(h_sb[:, :, I:ICH * IC], 0.0))

            def step(u, m, lap, kind):
                if kind(0):
                    if kind(0) == "routed":
                        r = u - NB
                        dve.wait_ge(rows_loaded[m], 16 * (lap - NB // RING + 1))
                        src = bank[6][:, 0:P]
                    else:
                        src = YT[:, bass.ds(u * P, P)]
                    dve.wait_ge(yh_made, u + 1)
                    nc.vector.tensor_tensor(yl[:, m % 2, :], src, yh[:, m % 2, :].bitcast(F32), ALU.subtract).then_inc(yl_made, 1)
                    if kind(0) == "routed":
                        nc.vector.tensor_copy(share_of[:, bass.ds(r, 1)], rows_in[:, m, SHARE_AT:DEST_AT])
                        nc.vector.tensor_copy(dest_of[:, bass.ds(r, 1)], rows_in[:, m, DEST_AT:ROW].bitcast(U32)).then_inc(dest_kept, 1)
                if kind(1):
                    n, q = u - 1, (m - 1) % 2
                    dve.wait_ge(silu_made, n + 1)
                    dve.wait_ge(up_made, n + 1)
                    need(dve, h_turned, n - 1)
                    up = bank[2 * q + 1][:, 0:I]
                    if kind(1) == "shared":
                        ins = nc.vector.tensor_tensor(h_sb[:, q, 0:I], act_sb[:, q, :], up, ALU.mult)
                    else:
                        dve.wait_ge(dest_kept, n - NB + 1)
                        ins = nc.vector.scalar_tensor_tensor(h_sb[:, q, 0:I], act_sb[:, q, :], share_of[:, bass.ds(n - NB, 1)],
                                                             up, ALU.mult, ALU.mult)
                    ins.then_inc(h_made, 1)
                if kind(3):
                    n, q = u - 3, (m - 3) % RING
                    dve.wait_ge(down_made, n + 1)
                    if kind(3) == "shared":
                        xb = xs[:, bass.ds(n, 1), :].rearrange("p a d -> p (a d)")
                        nc.vector.tensor_tensor(xb, bank[7][:, 0:D], xb, ALU.add).then_inc(down_kept, 1)
                    else:
                        lap_n = lap - (1 if m < 3 else 0)
                        need(dve, result_sent[q], 16 * (lap_n - NB // RING))
                        nc.vector.tensor_copy(result[:, q, :], bank[7][:, 0:D])
                        nc.vector.tensor_copy(dest_ring[:, q:q + 1], dest_of[:, bass.ds(n - NB, 1)]).then_inc(down_kept, 1)

            run_tiles(dve, step)

            dve.wait_ge(down_kept, TILES)
            for g in range(NB // 4):
                dve.wait_ge(result_loaded[g], 16 * TOP)
                xg = xs[:, 4 * g:4 * g + 4, :]
                own(nc.vector.tensor_tensor(xg, xg, result_in[0][:, 4 * g:4 * g + 4, :], ALU.add))
                nc.vector.tensor_tensor(xg, xg, result_in[1][:, 4 * g:4 * g + 4, :], ALU.add).then_inc(fin_made, 1)

        @block.tensor
        def _(pe):
            def turn(out, in_):
                n = in_.shape[0]
                return nc.tensor.transpose(out, in_, ident[0:n, 0:n])

            def mm(out, a, b, start, stop):
                return nc.tensor.matmul(out, a, b, start=start, stop=stop, skip_group_check=True)

            pe.wait_ge(const_made, 19)
            pe.wait_ge(dma_mlp, 16 * MLP_DMAS)
            for k, w in enumerate((mlp_w[:, 0, :], w2_sb[:, :])):
                pe.wait_ge(mlp_active, k + 1)
                turn(bank[7][:, 0:P], hA[:, :]).then_inc(mlp_turned, 1)
                pe.wait_ge(mlp_kept, k + 1)
                mm(bank[7][:, 0:w.shape[1]], hB[:, :], w, True, True).then_inc(mlp_made, 1)
            pe.wait_ge(mlp_kept, 3)
            turn(bank[7][0:H, 0:P], hrev[:, :]).then_inc(mlp_turned, 1)

            pe.wait_ge(x_normed, 1)
            for b in range(NB):
                last = turn(bank[b // 4][:, (b % 4) * P:(b % 4 + 1) * P], xn[:, b, :])
                if b % 4 == 3:
                    last.then_inc(x_turned, 1)
            pe.wait_ge(w_scaled, 2)
            for b in range(NB):
                if b % 4 == 0:
                    pe.wait_ge(xT_kept, b // 4 + 1)
                last = mm(bank[b // 4][:, (b % 4) * P:(b % 4 + 1) * P], xnT[:, b * P:(b + 1) * P], wkv_sb[:, :], True, True)
                if b % 4 == 3:
                    last.then_inc(kv_made, 1)
            pe.wait_ge(k_normed, 1)
            for b in range(NB + 1):
                if b == NB:
                    pe.wait_ge(kT_kept, 1)
                last = turn(bank[b // 4 % 4][:, (b % 4) * P:(b % 4 + 1) * P], kdup[:, b, :, :].rearrange("p a d -> p (a d)"))
                if b % 4 == 3 or b == NB:
                    last.then_inc(k_turned, 1)

            def expert(n, p, first):
                for k in range(2):
                    if not first:
                        pe.wait_ge(expert_low, 2 * (n - 1) + k + 1)
                    for c in range(ICH):
                        w = min(IC, I - c * IC)
                        last = turn(bank[4 + k][:, c * IC:c * IC + w], graw[0:w, p, k, c, :])
                    last.then_inc(expert_turned, 1)
                if not first:
                    pe.wait_ge(expert_down, n)
                for c in range(ICH):
                    last = turn(bank[6][0:IC, c * P:(c + 1) * P], draw[:, p, c * IC:(c + 1) * IC])
                last.then_inc(expert_turned, 1)

            for e in range(2):
                pe.wait_ge(dma_expert[e], 16 * EXPERT_DMAS)
                expert(e, e, e == 0)
            with pe.Fori(0, (E - 2) // 2) as j:
                for p in range(2):
                    pe.wait_ge(dma_expert[p], 16 * EXPERT_DMAS * (j + 2))
                    expert(2 * j + (2 + p), p, False)

            pe.wait_ge(kT_kept, NB // 4 + 1)
            pe.wait_ge(null_split, 4)
            pe.wait_ge(expert_down, E)
            pe.wait_ge(expert_low, 2 * E)

            def step(t, p, on):
                q = 1 - p
                if isinstance(t, int) and t > NB:
                    pe.wait_ge(y_kept, t - 4)

                def scores(c):
                    if on(1):
                        n = NCH * (t - 1) + c
                        pe.wait_ge(q_kept, 2 * t)
                        need(pe, biased, n - 1)
                        for k in range(2):
                            tile = 2 * c + k
                            last = mm(bank[2 * (c % 2) + k][:, 0:2 * KEYS], qT[:, q, tile * P:(tile + 1) * P],
                                      KB[:, bass.ds(t - 1, 1), :, :].rearrange("p a k n -> p (a k n)"), True, True)
                        last.then_inc(scored, 1)

                def queries(c):
                    if on(0):
                        if c == 0:
                            need(pe, oT_kept, 2 * (t - 3))
                        else:
                            pe.wait_ge(q_kept, 2 * t + 1)
                        for k in range(HALF):
                            tile = c * HALF + k
                            last = mm(bank[4][:, k * P:(k + 1) * P], wq_sb[:, tile * P:(tile + 1) * P],
                                      xnT[:, bass.ds(t * P, P)], True, True)
                        last.then_inc(q_made, 1)

                def turn_pn():
                    if on(2):
                        pe.wait_ge(pn_split, t - 1)
                        need(pe, rnorm_made, min(t, NB) if isinstance(t, int) else t)
                        turn(bank[7][0:NULL_ROWS, 0:P], pn3[:, :, :].rearrange("p a h -> p (a h)").bitcast(F32)).then_inc(pn_turned, 1)

                def turn_p(c):
                    if on(2):
                        n = NCH * (t - 2) + c
                        pe.wait_ge(exped, n + 1)
                        need(pe, p_kept, n)
                        for k in range(HC):
                            last = turn(bank[5][:, k * P:(k + 1) * P], Pb[:, p, c * HC + k, 0:S])
                        last.then_inc(p_turned, 1)

                def mix(c):
                    if on(2):
                        n = NCH * (t - 2) + c
                        pe.wait_ge(p_kept, n + 1)
                        pe.wait_ge(pn_kept, t - 1)
                        need(pe, o_kept, n)
                        mm(bank[6][:, 0:HC * VW], pnT[:, :],
                           NV[:, c * HC:(c + 1) * HC, :].rearrange("p h d -> p (h d)"), True, False)
                        for k in range(HC):
                            last = mm(bank[6][:, k * VW:(k + 1) * VW], pT[:, c % 2, k * P:(k + 1) * P],
                                      V1[:, bass.ds(t - 2, 1), :].rearrange("p a d -> p (a d)"), False, k == HC - 1)
                        last.then_inc(mixed, 1)

                def project():
                    if on(4):
                        if not isinstance(t, int) or t - 2 < NB:
                            pe.wait_ge(pn_kept, t - 1)
                        pe.wait_ge(oT_kept, 2 * (t - 3))
                        for k in range(QT):
                            last = mm(bank[7][:, 0:D], oT[:, p, k * P:(k + 1) * P], wo_sb[:, k, :], k == 0, k == QT - 1)
                        last.then_inc(y_made, 1)

                def sum_squares():
                    if on(0):
                        pe.wait_ge(q_squared, 2 * t + 2)
                        need(pe, y_kept, t - 3)
                        if not isinstance(t, int) or t >= 2:
                            pe.wait_ge(pn_kept, t - 1)
                        for k in range(QT):
                            last = mm(bank[7][:, 0:H], sq[:, k * P:(k + 1) * P], hsel[:, k, :], k == 0, k == QT - 1)
                        last.then_inc(sumsq_made, 1)

                def turn_o(c):
                    if on(3):
                        if c == 0:
                            pe.wait_ge(o_kept, NCH * (t - 2))
                            pe.wait_ge(q_kept, 2 * t + 2 if not isinstance(t, int) or t < NB else 2 * NB)
                        need(pe, oT_kept, 2 * (t - 3) + c)
                        for k in range(HALF):
                            tile = c * HALF + k
                            last = turn(bank[4][:, k * P:(k + 1) * P], o_sb[:, q, tile * P:(tile + 1) * P])
                        last.then_inc(o_turned, 1)

                scores(0)
                queries(0)
                turn_pn()
                turn_p(0)
                scores(1)
                queries(1)
                mix(0)
                turn_p(1)
                project()
                mix(1)
                scores(2)
                turn_p(2)
                sum_squares()
                mix(2)
                turn_o(0)
                turn_p(3)
                scores(3)
                mix(3)
                turn_o(1)

            run_steps(pe, step)

            turn(bank[4][:, 0:NE], router_sb[:, :]).then_inc(router_turned, 1)
            pe.wait_ge(send0_made, 1)
            for b in range(NB):
                last = turn(bank[b // 4][:, (b % 4) * P:(b % 4 + 1) * P], send[0][:, b, 0:D])
                if b % 4 == 3:
                    last.then_inc(y_turned, 1)
            pe.wait_ge(router_kept, 1)
            for b in range(NB):
                if b % 4 == 0:
                    pe.wait_ge(yT_kept, b // 4 + 1)
                last = mm(bank[5][:, b * NE:(b + 1) * NE], YT[:, b * P:(b + 1) * P], router_wT[:, 0:NE], True, True)
            last.then_inc(logits_made, 1)

            pe.wait_ge(load_made, 1)
            pe.wait_ge(sort_consts, 4)
            load_flat = load[:, :, :].rearrange("p b e -> p (b e)")
            mm(bank[6][:, 0:NB * NE], before[:, :], load_flat, True, True)
            mm(bank[7][:, 0:NB * NE], ones[:, :], load_flat, True, True).then_inc(ranks_made, 1)

            expert_of = {}
            expert_regs = [pe.alloc_register(f"expert_reg{k}") for k in range(2 * RING)]

            def step(u, m, lap, kind):
                if m == 0 and (not isinstance(u, int) or u >= NB) and kind(0) != "shared":
                    pe.load(expert_regs, tile_expert[0:1, bass.ds(u - NB, 2 * RING)])
                    for at in range(-3, RING - 1):
                        expert_of[at] = pe.snap(expert_regs[at + RING], min_val=1, max_val=NE)
                if kind(0) == "routed":
                    r = u - NB
                    pe.wait_ge(rows_loaded[m], 16 * (lap - NB // RING + 1))
                    pe.wait_ge(yl_made, u)
                    turn(bank[6][:, 0:P], rows_in[:, m, 0:D]).then_inc(tile_turned, 1)
                if kind(1):
                    n, q = u - 1, (m - 1) % 2
                    e = 0 if kind(1) == "shared" else expert_of[m - 1]
                    pe.wait_ge(yl_made, n + 1)
                    need(pe, h_made, n - 1)
                    for k, made in ((0, gate_made), (1, up_made)):
                        o = bank[2 * q + k][:, 0:I]
                        high, low = (w[:, bass.ds(e, 1), k, :].rearrange("p a i -> p (a i)") for w in (GH, GL))
                        mm(o, yh[:, q, :], high, True, False)
                        mm(o, yh[:, q, :], low, False, False)
                        mm(o, yl[:, q, :], high, False, True).then_inc(made, 1)
                if kind(3):
                    n, q = u - 3, (m - 3) % 2
                    e = 0 if kind(3) == "shared" else expert_of[m - 3]
                    pe.wait_ge(hT_kept, n + 1)
                    need(pe, down_kept, n)
                    for c in range(ICH):
                        last = mm(bank[7][:, 0:D], hT[:, q, c * P:(c + 1) * P],
                                  DT[:, bass.ds(e, 1), c, :].rearrange("p a d -> p (a d)"), c == 0, c == ICH - 1)
                    last.then_inc(down_made, 1)
                if kind(2):
                    n, q = u - 2, (m - 2) % 2
                    pe.wait_ge(h_made, n + 1)
                    need(pe, hT_kept, n - 1)
                    for c in range(ICH):
                        last = turn(bank[4 + q][0:IC, c * P:(c + 1) * P], h_sb[:, q, c * IC:(c + 1) * IC])
                    last.then_inc(h_turned, 1)

            pe.wait_ge(table_made, 1)
            run_tiles(pe, step)


_INS = ['x', 'cond_64', 'mask_BxS_bf1', 'L0_cond_g_norm', 'L0_cond_Wq', 'L0_cond_Wkv', 'L0_cond_q_scale',
        'L0_cond_k_scale', 'L0_cond_null_attn_bias', 'L0_cond_w0', 'L0_cond_b0', 'L0_cond_g0', 'L0_cond_w1',
        'L0_cond_b1', 'L0_cond_g1', 'L0_cond_w2', 'L0_cond_b2', 'L0_cond_Wout', 'L0_cond_g_out', 'L0_ffn_sg',
        'L0_ffn_su', 'L0_ffn_sd', 'L0_ffn_rg', 'L0_ffn_ru', 'L0_ffn_rd', 'L0_ffn_wr', 'L0_ffn_rb']
_OUTS = [((16, 128, 128), 'float32')]


def kernel(**inputs):
    import numpy as _np
    import concourse.bacc as _bacc
    from concourse import mybir as _mybir
    from concourse.bass_utils import run_bass_kernel_spmd as _run

    nc = _bacc.Bacc("TRN2", target_bir_lowering=False, num_devices=1)
    arrays, args = {}, []
    for name in _INS:
        a = _np.ascontiguousarray(inputs[name])
        arrays[f"in_{name}_dram"] = a
        args.append(nc.dram_tensor(f"in_{name}_dram", a.shape, _mybir.dt.from_np(a.dtype), kind="ExternalInput").ap())
    for i, (shape, dtype) in enumerate(_OUTS):
        dt = _mybir.dt.from_np(_np.dtype(dtype))
        args.append(nc.dram_tensor(f"out_{i}_dram", shape, dt, kind="ExternalOutput").ap())
    adaln_ffn_kernel(nc, *args)
    r = _run(nc, [arrays], core_ids=[0])
    got = tuple(r.results[0][f"out_{i}_dram"] for i in range(len(_OUTS)))
    return got[0]
```

```python
from contextlib import ExitStack

import concourse.bass as bass
from concourse import mybir

ALU = mybir.AluOpType
ACT = mybir.ActivationFunctionType
AX_X = mybir.AxisListType.X
F32 = mybir.dt.float32
F32R = mybir.dt.float32r
I32 = mybir.dt.int32
U32 = mybir.dt.uint32

P = 128
NEG = -1e30
EPS = 1e-5
NORM_GUARD_SQ = 1e-24
RSQRT_MAGIC = float(0x5F3759DF)


def need(eng, sem, value):
    if not isinstance(value, int) or value > 0:
        eng.wait_ge(sem, value)


def adaln_ffn_kernel(nc: bass.Bass, x, cond, mask, g_norm, wq, wkv, q_scale, k_scale, null_bias, w0, b0, g0,
                     w1, b1, g1, w2, b2, wout, g_out, shared_gate, shared_up, shared_down, routed_gate, routed_up, routed_down, router_w, router_bias, out):
    NB, S, D = x.shape
    H = null_bias.shape[0]
    DH = cond.shape[1]
    HD = H * DH
    NE, I, _ = routed_gate.shape
    assert S == P and D == P and 2 * DH == P
    SCALE = 8.0
    KEYS = S + 1
    VW = DH + 1
    HC = 4
    NCH = H // HC
    QT = HD // P
    HALF = QT // 2
    GROUPS = 4
    STAGES = 4
    PEEL = 4
    Y_FIRST = NB - STAGES
    CHAIN = 11
    CONSTS = 21
    SMALL_DMAS, MLP_DMAS, EXPERT_DMAS = 4, 12, 5
    NULL_ROWS = 5 * H
    ICH = 3
    IC = -(-I // ICH)
    E = NE + 1
    FIRST, SECOND, THIRD = range(2), range(2, 5), range(5, NE + 1)
    TOP = 2
    ROUTED = (TOP * NB * S + NE * (P - 1)) // P
    TILES = NB + ROUTED
    SHARE_AT, DEST_AT, ROW = D, D + 1, D + 2
    NOWHERE = 1 << 20
    RING = 4
    LAPS = (TILES - NB - RING) // RING

    ctx = ExitStack()
    with ctx:
        def sb(name, shape, dt=F32):
            return ctx.enter_context(nc.sbuf_tensor(name, shape, dt))

        def sem(name):
            return ctx.enter_context(nc.semaphore(name))

        def shared(tile, at, *shape, parts=P):
            n = 1
            for k in shape:
                n *= k
            dims = " ".join(f"d{k}" for k in range(len(shape)))
            return tile[0:parts, at:at + n].rearrange(f"p ({dims}) -> p {dims}", **{f"d{k}": v for k, v in enumerate(shape)})

        bank = [ctx.enter_context(nc.psum_tensor(f"bank{i}", [P, 512], F32)) for i in range(8)]

        bias_dram = nc.dram_tensor("bias_rows", (H, P, 2 * P), F32, kind="Internal").ap()
        sent_dram = nc.dram_tensor("sent_rows", (ROUTED * P, ROW), F32, kind="Internal").ap()
        result_dram = nc.dram_tensor("result_rows", (TOP * NB * S, D), F32, kind="Internal").ap()

        ident = sb("ident", [P, P])
        xs = sb("xs", [P, NB, D])
        xn = sb("xn", [P, NB, D])
        xnT = sb("xnT", [P, NB * S])
        wq_sb = sb("wq_sb", [P, HD])
        wkv_sb = sb("wkv_sb", [P, 2 * DH])
        wo_sb = sb("wo_sb", [P, QT, D])
        gcol = sb("gcol", [P, 1])
        kq = sb("kq", [P, 3, DH])
        stat = sb("stat", [P, 8, 32])
        kraw = sb("kraw", [P, NB + 1, DH])
        KB = sb("KB", [P, NB, 2, KEYS])
        V1 = sb("V1", [P, NB, VW])
        NV = sb("NV", [NULL_ROWS, H, VW], F32R)
        bias = sb("bias", [P, H, KEYS])
        biasm_space = sb("biasm_space", [P, 2 * H * KEYS])
        BIASM_FREE = 2 * ICH * IC + 2 * ICH * P
        biasm = shared(biasm_space, 0, 2, H, KEYS)
        kdup = shared(biasm_space, 0, NB + 1, 2, DH)
        madd = sb("madd", [P, NB, KEYS])
        b2r = sb("b2r", [P, H])
        nullb = sb("nullb", [P, H])
        w2_sb = sb("w2_sb", [P, H])
        pos = sb("pos", [P, 1])
        bst = sb("bst", [P, 6])
        bmv = sb("bmv", [P, 2])
        brs = sb("brs", [P, 4])
        hrev = sb("hrev", [P, H])
        hrevT = sb("hrevT", [H, 2 * P])

        q_space = sb("q_space", [P, 2 * QT * P])
        qT = shared(q_space, 0, 2, QT * P)
        mlp_w = shared(q_space, 0, 1, P)
        mlp_r = shared(q_space, P, 5, P)
        hA = shared(q_space, 6 * P, P)
        hB = shared(q_space, 7 * P, P)
        sq = sb("sq", [P, QT * P])
        mask_u8 = sq[:, 0:NB * S // 4].bitcast(mask.dtype).rearrange("p (b s) -> p b s", b=NB)
        hsel = sb("hsel", [P, QT // GROUPS, P // GROUPS])
        sums_sb = kraw[:, 0:2, :].rearrange("p a d -> p (a d)")
        rn = sb("rn", [P, 2, H])
        norm_in = sb("norm_in", [P, 2, 32])
        p_space = sb("p_space", [P, 2 * H * KEYS])
        Pb = shared(p_space, 0, 2, H, KEYS)
        squares = shared(p_space, 0, NB, D)
        ksq = shared(p_space, H * KEYS, NB + 1, DH)
        null_v = shared(biasm_space, (NB + 1) * 2 * DH, H, VW, parts=NULL_ROWS)
        mx = sb("mx", [P, 2, H])
        pT = sb("pT", [P, 2, HC * P])
        pnT = sb("pnT", [NULL_ROWS, P], F32R)
        pn3 = sb("pn3", [P, NULL_ROWS // H, H], F32R)
        inv_den = sb("inv_den", [P, HC])
        o_space = sb("o_space", [P, 2 * HD])
        o_sb = shared(o_space, 0, 2, HD)
        oT_space = sb("oT_space", [P, 2 * QT * P])
        oT = shared(oT_space, 0, 2, QT * P)
        GRAW, DRAW = 2 * ICH * D, ICH * IC
        graw = tuple(shared(tile, at, 2, ICH, D, parts=IC) for tile, at in ((oT_space, 0), (oT_space, GRAW), (o_space, 2 * DRAW)))
        draw = tuple(shared(tile, at, DRAW) for tile, at in ((o_space, 0), (o_space, DRAW), (oT_space, 2 * GRAW)))
        y_sb = xn
        y_squares = xnT[:, :].rearrange("p (b d) -> p b d", b=NB)
        send = (shared(p_space, 0, NB, ROW), shared(biasm_space, BIASM_FREE, NB, ROW))

        whole = (shared(p_space, H * KEYS + (NB + 1) * DH, 2, I), shared(biasm_space, (NB + 1) * 2 * DH + H * VW, 2, I))
        GH = sb("GH", [P, E, 2, I], F32R)
        GL = sb("GL", [P, E, 2, I], F32R)
        DT = sb("DT", [IC, E, ICH, D])


        YT = xnT
        yh = sb("yh", [P, 2, P], F32R)
        yl = sb("yl", [P, 2, P], F32R)
        act_sb = shared(sq, 0, 2, I)
        h_sb = shared(biasm_space, 0, 2, ICH * IC)
        hT = shared(biasm_space, 2 * ICH * IC, 2, ICH * P, parts=IC)
        router_sb = sb("router_sb", [NE, D])
        router_wT = sb("router_wT", [P, NE + 1])
        rbr = sb("rbr", [P, NE])
        iota7 = sb("iota7", [P, NE])
        iota_tile = sb("iota_tile", [P, ROUTED])
        fill_row = sb("fill_row", [P, ROW])
        dest = sb("dest", [P, TOP, NB], I32)
        share = sb("share", [P, 4, NB])
        PAD = NB // 2
        EPAD = 4
        L = shared(o_space, 0, NB, NE)
        equal = shared(o_space, NB * NE, NB, NE)
        chosen = shared(o_space, 2 * NB * NE, TOP, NB, NE)
        load = shared(o_space, 4 * NB * NE, NB, NE)
        totals = shared(o_space, 5 * NB * NE, NB, NE)
        place = shared(o_space, 6 * NB * NE, NB, NE)
        placed = shared(o_space, 7 * NB * NE, TOP, NB, NE)
        run_up = shared(o_space, 9 * NB * NE, 2, PAD + NB, NE)
        tiles_up = shared(o_space, 12 * NB * NE, 2, EPAD + NE)
        best = sb("best", [P, 2, NB])
        tiles_of = sb("tiles_of", [P, NE])
        tiles_int = sb("tiles_int", [P, 2, NE], I32)
        row_of = sb("row_of", [P, TOP, NB])
        row_index = sb("row_index", [P, TOP, NB], U32)
        passed = shared(q_space, 0, ROUTED, NE - 1)
        before = shared(q_space, 2 * P, P)
        ones = shared(q_space, 3 * P, P)
        tile_float = shared(q_space, 4 * P + RING * ROW + 2 * ROUTED, ROUTED)
        TABLE = -(-ROUTED // RING) * RING + 2 * RING
        tile_expert = sb("tile_expert", [P, TABLE], I32)
        rows_in = shared(q_space, 4 * P, RING, ROW)
        share_of = shared(q_space, 4 * P + RING * ROW, ROUTED)
        dest_of = shared(q_space, 4 * P + RING * ROW + ROUTED, ROUTED).bitcast(U32)
        dest_ring = sb("dest_ring", [P, RING], U32)
        result = shared(oT_space, 0, RING, D)
        result_in = (xn, xnT[:, :].rearrange("p (b d) -> p b d", b=NB))
        gor = sb("gor", [P, D])

        dma_x, dma_wq, dma_small, dma_mask, dma_mlp, dma_wo = (sem(n) for n in (
            "dma_x", "dma_wq", "dma_small", "dma_mask", "dma_mlp", "dma_wo"))
        dma_expert = [sem(f"dma_expert{i}") for i in range(len(graw))]
        bias_stored, bias_loaded, out_stored = sem("bias_stored"), sem("bias_loaded"), sem("out_stored")
        const_made, pool_step, dve_step = (sem(n) for n in ("const_made", "pool_step", "dve_step"))
        mask_made, null_made, null_split, pn_high, pn_split = (sem(n) for n in (
            "mask_made", "null_made", "null_split", "pn_high", "pn_split"))
        expert_turned, expert_kept, expert_split, expert_low, expert_down = (sem(n) for n in (
            "expert_turned", "expert_kept", "expert_split", "expert_low", "expert_down"))
        q_made, q_kept, q_squared, sumsq_made, rnorm_step, rnorm_made = (sem(n) for n in (
            "q_made", "q_kept", "q_squared", "sumsq_made", "rnorm_step", "rnorm_made"))
        biasm_made, scored, biased, maxed, shifted, exped = (sem(n) for n in (
            "biasm_made", "scored", "biased", "maxed", "shifted", "exped"))
        p_turned, p_kept, pn_turned, pn_kept, mixed, den_made, o_kept = (sem(n) for n in (
            "p_turned", "p_kept", "pn_turned", "pn_kept", "mixed", "den_made", "o_kept"))
        o_turned, oT_kept, y_made, y_kept = (sem(n) for n in ("o_turned", "oT_kept", "y_made", "y_kept"))
        yh_made, yl_made, gate_made, up_made, silu_made, h_made, h_turned, hT_kept, down_made, down_kept, fin_made = (
            sem(n) for n in ("yh_made", "yl_made", "gate_made", "up_made", "silu_made", "h_made", "h_turned",
                             "hT_kept", "down_made", "down_kept", "fin_made"))
        sums_kept, sums_turned = sem("sums_kept"), sem("sums_turned")
        (rows_filled, rows_sent, sort_consts, load_made, ranks_made, table_made, row_index_made, send0_made, send1_made,
         tile_turned, dest_kept) = (sem(n) for n in (
             "rows_filled rows_sent sort_consts load_made ranks_made table_made row_index_made send0_made send1_made "
             "tile_turned dest_kept").split())
        rows_loaded = [sem(f"rows_loaded{m}") for m in range(RING)]
        result_sent = [sem(f"result_sent{m}") for m in range(RING)]
        result_loaded = [sem(f"result_loaded{g}") for g in range(NB // 4)]

        (mlp_normed, mlp_active, mlp_turned, mlp_kept, mlp_made, hrev_made, w_scaled, x_centred, x_squared, x_normed,
         x_turned, xT_kept, kv_made, k_kept, k_squared, k_normed, k_turned, kT_kept, kT_odd_kept, y_centred, y_squared, y_normed,
         y_turned, yT_kept, router_turned, router_kept, logits_made, gap_made, gap_exped) = (sem(n) for n in (
             "mlp_normed mlp_active mlp_turned mlp_kept mlp_made hrev_made w_scaled x_centred x_squared x_normed "
             "x_turned xT_kept kv_made k_kept k_squared k_normed k_turned kT_kept kT_odd_kept y_centred y_squared y_normed "
             "y_turned yT_kept router_turned router_kept logits_made gap_made gap_exped").split())

        block = ctx.enter_context(nc.Block())

        def spread(ap, n):
            return ap.unsqueeze(2).to_broadcast([ap.shape[0], ap.shape[1], n])

        def row(v, n=P):
            return bass.AP(v.tensor, v.offset, [[0, n], [1, v.shape[-1]]])

        def run_steps(eng, step):
            for t in range(PEEL):
                step(t, t % 2, lambda k, t=t: 0 <= t - k < NB)
            with eng.Fori(0, (NB - PEEL) // 2) as i:
                for p in range(2):
                    step(2 * i + (PEEL + p), p, lambda k: True)
            for t in range(NB, NB + STAGES):
                step(t, t % 2, lambda k, t=t: 0 <= t - k < NB)

        def turned_bank(t, c):
            return (5, 0, 1, 2)[c] if isinstance(t, int) and t == NB + 1 else 5

        def run_tiles(eng, step):
            def single(u):
                step(u, u % RING, u // RING, lambda k: None if not 0 <= u - k < TILES else
                     "shared" if u - k < NB else "routed")

            for u in range(RING):
                single(u)
            with eng.Fori(0, NB // RING - 1) as i:
                for m in range(RING):
                    step(RING * i + (RING + m), m, i + 1, lambda k: "shared")
            for u in range(NB, NB + RING):
                single(u)
            with eng.Fori(0, LAPS) as i:
                for m in range(RING):
                    step(RING * i + (NB + RING + m), m, i + (NB // RING + 1), lambda k: "routed")
            for u in range(NB + RING + LAPS * RING, TILES + 3):
                single(u)

        def load_expert(sp, e, p):
            full = (ICH - 1) * IC
            if isinstance(e, int) and e == 0:
                ups, down = (shared_gate, shared_up), shared_down
            else:
                ups = tuple(w[bass.ds(e - 1, 1), :, :].rearrange("a i d -> (a i) d") for w in (routed_gate, routed_up))
                down = routed_down[bass.ds(e - 1, 1), :, :].rearrange("a h i -> (a h) i")
            for k, src in enumerate(ups):
                sp.dma_start(graw[p][:, k, 0:ICH - 1, :],
                             src[0:full, :].rearrange("(c p) d -> p c d", p=IC)).then_inc(dma_expert[p], 16)
                sp.dma_start(graw[p][0:I - full, k, ICH - 1, :], src[full:I, :]).then_inc(dma_expert[p], 16)
            sp.dma_start(draw[p][:, 0:I], down).then_inc(dma_expert[p], 16)

        def load_results(eng, k):
            for m in range(RING):
                eng.wait_ge(result_sent[m], 16 * (ROUTED // RING + (m < ROUTED % RING)))
            for g in range(NB // 4):
                eng.dma_start(result_in[k][:, 4 * g:4 * g + 4, :],
                              result_dram[(k * NB + 4 * g) * P:(k * NB + 4 * g + 4) * P, :].rearrange(
                                  "(b p) d -> p b d", p=P)).then_inc(result_loaded[g], 16)

        @block.sync
        def _(sp):
            sp.dma_start(xs[:, :, :], x.rearrange("b s d -> s b d")).then_inc(dma_x, 16)
            sp.dma_start(wkv_sb[:, :], wkv).then_inc(dma_wq, 16)
            sp.dma_start(wq_sb[:, :], wq).then_inc(dma_wq, 16)
            sp.dma_start(gcol[:, :], g_norm.rearrange("(p a) -> p a", a=1)).then_inc(dma_wq, 16)
            sp.dma_start(kq[:, 0, :], row(q_scale)).then_inc(dma_small, 16)
            sp.dma_start(kq[:, 1, :], row(k_scale)).then_inc(dma_small, 16)
            sp.dma_start(kraw[:, NB, :], row(cond[0, :])).then_inc(dma_small, 16)
            sp.dma_start(null_v[:, :, 0:DH], bass.AP(cond.tensor, cond[1, :].offset,
                                                     [[0, NULL_ROWS], [0, H], [1, DH]])).then_inc(dma_small, 16)
            for e in range(E):
                need(sp, expert_turned, 3 * (e - len(graw) + 1))
                load_expert(sp, e, e % len(graw))
            sp.wait_ge(const_made, CONSTS)
            sp.dma_start(sent_dram.rearrange("(t p) c -> p t c", p=P),
                         fill_row[:, :].unsqueeze(1).to_broadcast([P, ROUTED, ROW])).then_inc(rows_filled, 16)

            def load_rows(r, m):
                sp.dma_start(rows_in[:, m, :], sent_dram[bass.ds(r * P, P), :]).then_inc(rows_loaded[m], 16)

            sp.wait_ge(rows_sent, 16 * TOP * NB)
            for r in range(RING):
                load_rows(r, r)
            with sp.Fori(0, (ROUTED - RING) // RING) as i:
                for m in range(RING):
                    sp.wait_ge(dest_kept, RING * i + (m + 1))
                    load_rows(RING * i + (RING + m), m)
            for r in range(ROUTED - ROUTED % RING, ROUTED):
                sp.wait_ge(dest_kept, r - RING + 1)
                load_rows(r, r % RING)
            load_results(sp, 0)
            for g in range(NB // 4):
                sp.wait_ge(fin_made, g + 1)
                sp.dma_start(out[4 * g:4 * g + 4, :, :].rearrange("b s d -> s b d"),
                             xs[:, 4 * g:4 * g + 4, :]).then_inc(out_stored, 16)
            sp.wait_ge(out_stored, 16 * (NB // 4))

        @block.gpsimd
        def _(pool):
            done = 0

            def own(ins):
                nonlocal done
                done += 1
                ins.then_inc(pool_step, 1)
                pool.wait_ge(pool_step, done)

            own(nc.gpsimd.memset(ident[:, :], 0.0))
            nc.gpsimd.affine_select(out=ident[:, :], in_=ident[:, :], compare_op=ALU.not_equal, fill=1.0, base=0,
                                    pattern=[[-1, P]], channel_multiplier=1).then_inc(const_made, 1)
            own(nc.gpsimd.memset(hsel[:, :, :], 1.0))
            own(nc.gpsimd.affine_select(out=hsel[:, :, :], in_=hsel[:, :, :], compare_op=ALU.is_ge, fill=0.0, base=0,
                                        pattern=[[2 * DH, QT // GROUPS], [-DH, P // GROUPS]], channel_multiplier=1))
            nc.gpsimd.affine_select(out=hsel[:, :, :], in_=hsel[:, :, :], compare_op=ALU.is_ge, fill=0.0, base=DH - 1,
                                    pattern=[[-2 * DH, QT // GROUPS], [DH, P // GROUPS]], channel_multiplier=-1).then_inc(const_made, 1)
            nc.gpsimd.iota(pos[:, :], pattern=[[0, 1]], base=P - 1, channel_multiplier=-1,
                           allow_small_or_imprecise_dtypes=True).then_inc(const_made, 1)
            nc.gpsimd.iota(iota7[:, :], pattern=[[1, NE]], base=0, channel_multiplier=0,
                           allow_small_or_imprecise_dtypes=True).then_inc(const_made, 1)
            nc.gpsimd.memset(V1[:, :, DH:VW], 1.0).then_inc(const_made, 1)
            for d in draw:
                nc.gpsimd.memset(d[:, I:ICH * IC], 0.0).then_inc(const_made, 1)
            nc.gpsimd.memset(KB[:, :, :, :], 0.0).then_inc(const_made, 1)
            nc.gpsimd.memset(hrevT[:, P:2 * P], NEG).then_inc(const_made, 1)
            nc.gpsimd.memset(fill_row[:, 0:DEST_AT], 0.0).then_inc(const_made, 1)
            nc.gpsimd.memset(madd[:, :, S:KEYS], 0.0).then_inc(const_made, 1)
            nc.gpsimd.memset(null_v[:, :, DH:VW], 1.0).then_inc(const_made, 1)
            nc.gpsimd.memset(NV[:, :, :].bitcast(F32), 0.0).then_inc(const_made, 1)
            nc.gpsimd.memset(pn3[:, :, :].bitcast(F32), 0.0).then_inc(const_made, 1)
            nc.gpsimd.memset(fill_row[:, DEST_AT:ROW].bitcast(I32), NOWHERE).then_inc(const_made, 1)
            nc.gpsimd.iota(iota_tile[:, :], pattern=[[1, ROUTED]], base=0, channel_multiplier=0,
                           allow_small_or_imprecise_dtypes=True).then_inc(const_made, 1)
            nc.gpsimd.iota(dest[:, :, :], pattern=[[NB * S, TOP], [S, NB]], base=0, channel_multiplier=1).then_inc(const_made, 1)
            nc.gpsimd.memset(row_index[:, :, :], 0).then_inc(const_made, 1)
            nc.gpsimd.memset(dest_ring[:, :], 0).then_inc(const_made, 1)
            nc.gpsimd.memset(tile_expert[:, :], 1).then_inc(const_made, 1)
            pool.wait_ge(dma_wq, 48)
            nc.gpsimd.tensor_scalar(wkv_sb[:, :], wkv_sb[:, :], gcol[:, 0:1], None, ALU.mult).then_inc(w_scaled, 1)
            nc.gpsimd.tensor_scalar(wq_sb[:, :], wq_sb[:, :], gcol[:, 0:1], None, ALU.mult).then_inc(w_scaled, 1)
            pool.wait_ge(w_scaled, 2)
            pool.wait_ge(dma_small, 16 * SMALL_DMAS)
            pool.wait_ge(const_made, CONSTS)
            for at in (0, 2 * H, 4 * H):
                rows = slice(at, at + H)
                nc.gpsimd.affine_select(out=null_v[rows, :, :], in_=null_v[rows, :, :], compare_op=ALU.is_equal, fill=0.0,
                                        base=0, pattern=[[-1, H], [0, VW]], channel_multiplier=1).then_inc(null_made, 1)

            def split_expert(e):
                for k in range(2):
                    pool.wait_ge(expert_kept, 2 * e + k + 1)
                    nc.gpsimd.tensor_copy(GH[:, e, k, :], whole[e % 2][:, k, :]).then_inc(expert_split, 1)
                    pool.wait_ge(expert_split, 4 * e + 2 * k + 1)
                    nc.gpsimd.tensor_tensor(GL[:, e, k, :], whole[e % 2][:, k, :], GH[:, e, k, :].bitcast(F32), ALU.subtract).then_inc(expert_split, 1)
                    pool.wait_ge(expert_split, 4 * e + 2 * k + 2)

            pool.wait_ge(null_made, 3)
            for e in FIRST:
                split_expert(e)
            pool.wait_ge(hrev_made, 1)
            pool.dma_start(bias_dram, hrevT[:, :].unsqueeze(1).to_broadcast([H, P, 2 * P])).then_inc(bias_stored, 16)
            split_expert(SECOND[0])
            pool.wait_ge(bias_stored, 16)
            pool.dma_start(bias[:, :, 0:S], bass.AP(bias_dram.tensor, P - 1, [[2 * P - 1, P], [2 * P * P, H], [1, S]])).then_inc(bias_loaded, 16)
            for e in SECOND[1:]:
                split_expert(e)
            pool.wait_ge(mask_made, 2)
            pool.wait_ge(null_split, 4)
            pool.wait_ge(k_turned, NB // 4 + 1)
            pool.wait_ge(bias_loaded, 16)
            pool.wait_ge(dma_mlp, 16 * MLP_DMAS)

            def step(t, p, on):
                for c in range(NCH):
                    heads = slice(c * HC, (c + 1) * HC)
                    if on(1):
                        pool.wait_ge(maxed, NCH * (t - 1) + c + 1)
                        v = Pb[:, 1 - p, heads, :]
                        nc.gpsimd.tensor_tensor(v, v, spread(mx[:, 1 - p, heads], KEYS),
                                                ALU.subtract).then_inc(shifted, 1)
                    if on(0):
                        nc.gpsimd.tensor_tensor(biasm[:, p, heads, :], bias[:, heads, :],
                                                madd[:, bass.ds(t, 1), :].to_broadcast([P, HC, KEYS]),
                                                ALU.add).then_inc(biasm_made, 1)

            run_steps(pool, step)

            pool.wait_ge(y_kept, NB)
            nc.gpsimd.memset(ones[:, :], 1.0).then_inc(sort_consts, 1)
            nc.gpsimd.memset(run_up[:, :, :, :], 0.0).then_inc(sort_consts, 1)
            nc.gpsimd.memset(tiles_up[:, :, :], 0.0).then_inc(sort_consts, 1)
            pool.wait_ge(sort_consts, 3)
            nc.gpsimd.affine_select(out=before[:, :], in_=ones[:, :], compare_op=ALU.is_gt, fill=0.0, base=0,
                                    pattern=[[1, P]], channel_multiplier=-1).then_inc(sort_consts, 1)
            pool.wait_ge(sort_consts, 4)
            pool.wait_ge(y_normed, 2)
            nc.gpsimd.tensor_copy(send[0][:, :, 0:D], y_sb[:, :, :]).then_inc(send0_made, 1)
            pool.wait_ge(rows_filled, 16)
            pool.wait_ge(row_index_made, 1)
            for k, made in ((0, send0_made), (1, send1_made)):
                pool.wait_ge(made, 3)
                for b in range(NB):
                    nc.gpsimd.indirect_dma_start(
                        out=sent_dram[:, :], out_offset=bass.IndirectOffsetOnAxis(ap=row_index[:, k, b:b + 1], axis=0),
                        in_=send[k][:, b, :], in_offset=None).then_inc(rows_sent, 16)

            def send_result(r, m):
                pool.wait_ge(down_kept, r + (NB + 1))
                nc.gpsimd.indirect_dma_start(
                    out=result_dram[:, :], out_offset=bass.IndirectOffsetOnAxis(ap=dest_ring[:, m:m + 1], axis=0),
                    in_=result[:, m, :], in_offset=None, bounds_check=TOP * NB * S - 1,
                    oob_is_err=False).then_inc(result_sent[m], 16)

            for r in range(ROUTED):
                send_result(r, r % RING)

        def down_bank(e):
            return 3 if e in THIRD else 4

        def keep_expert(act, e):
            for k in range(2):
                act.wait_ge(expert_turned, 3 * e + k + 1)
                if e in THIRD:
                    to = GH[:, e, k, :]
                else:
                    need(act, expert_split, 4 * (e - 1))
                    to = whole[e % 2][:, k, :]
                nc.scalar.activation(to, bank[5 + k][:, 0:I], ACT.Copy).then_inc(expert_kept, 1)
            act.wait_ge(expert_turned, 3 * e + 3)
            nc.scalar.activation(DT[:, e, :, :].rearrange("p c d -> p (c d)"), bank[down_bank(e)][0:IC, 0:ICH * P],
                                 ACT.Copy).then_inc(expert_down, 1)

        @block.scalar
        def _(act):
            act.dma_start(mask_u8[:, :, :], bass.AP(mask.tensor, 0, [[0, P], [S, NB], [1, S]])).then_inc(dma_mask, 16)
            for k, v in enumerate((b0, g0, b1, g1)):
                act.dma_start(mlp_r[:, k, :], row(v)).then_inc(dma_mlp, 16)
            act.dma_start(mlp_r[:, 4, :], row(w0[0, :])).then_inc(dma_mlp, 16)
            act.dma_start(mlp_w[:, 0, :], w1).then_inc(dma_mlp, 16)
            act.dma_start(w2_sb[:, :], w2).then_inc(dma_mlp, 16)
            act.dma_start(b2r[:, :], row(b2)).then_inc(dma_mlp, 16)
            act.dma_start(nullb[:, :], row(null_bias)).then_inc(dma_mlp, 16)
            act.dma_start(gor[:, :], row(g_out)).then_inc(dma_mlp, 16)
            act.dma_start(rbr[:, :], row(router_bias)).then_inc(dma_mlp, 16)
            act.dma_start(router_sb[:, :], router_w).then_inc(dma_mlp, 16)
            act.dma_start(wo_sb[:, :, :], wout.rearrange("(t p) n -> p t n", p=P)).then_inc(dma_wo, 16)
            act.wait_ge(x_centred, 1)
            nc.scalar.activation(squares[:, :, :], xn[:, :, :], ACT.Square).then_inc(x_squared, 1)
            for e in FIRST:
                keep_expert(act, e)
            act.wait_ge(mlp_normed, 1)
            nc.scalar.activation(hA[:, :], hA[:, :], ACT.Silu).then_inc(mlp_active, 1)
            for g in range(NB // 4):
                act.wait_ge(x_turned, g + 1)
                nc.scalar.activation(xnT[:, g * 512:(g + 1) * 512], bank[g % 4][:, :], ACT.Copy).then_inc(xT_kept, 1)
            act.wait_ge(mlp_normed, 2)
            nc.scalar.activation(hA[:, :], hA[:, :], ACT.Silu).then_inc(mlp_active, 1)
            act.wait_ge(k_kept, 4)
            act.wait_ge(dma_small, 16 * SMALL_DMAS)
            nc.scalar.activation(ksq[:, :, :], kraw[:, :, :], ACT.Square).then_inc(k_squared, 1)
            for e in SECOND:
                keep_expert(act, e)
            for g in range(1, NB // 4, 2):
                act.wait_ge(k_turned, g + 1)
                for k in range(2):
                    rows = slice(k * DH, (k + 1) * DH)
                    last = nc.scalar.activation(KB[rows, 4 * g:4 * g + 4, k, 0:S],
                                                bank[g % 4][rows, :].rearrange("p (b n) -> p b n", b=4), ACT.Copy)
                last.then_inc(kT_odd_kept, 1)

            def square_y(k):
                b = slice(0, Y_FIRST) if k == 0 else slice(Y_FIRST, NB)
                act.wait_ge(y_centred, k + 1)
                nc.scalar.activation(y_squares[:, b, :], y_sb[:, b, :], ACT.Square).then_inc(y_squared, 1)

            def step(t, p, on):
                q = 1 - p

                def keep_q(c):
                    if on(0):
                        half = slice(c * HALF * P, (c + 1) * HALF * P)
                        act.wait_ge(q_made, 2 * t + c + 1)
                        need(act, scored, NCH * (t - 1))
                        nc.scalar.activation(qT[:, p, half], bank[4][:, :], ACT.Copy).then_inc(q_kept, 1)
                        act.wait_ge(q_kept, 2 * t + c + 1)
                        need(act, sumsq_made, t)
                        nc.scalar.activation(sq[:, half], qT[:, p, half], ACT.Square).then_inc(q_squared, 1)

                def exp(c, back=1):
                    if on(back):
                        act.wait_ge(shifted, NCH * (t - back) + c + 1)
                        v = Pb[:, q if back == 1 else p, c * HC:(c + 1) * HC, :]
                        nc.scalar.activation(v, v, ACT.Exp).then_inc(exped, 1)

                def prepare(k):
                    if isinstance(t, int) and t == 0:
                        keep_expert(act, THIRD[k])

                def keep_pn():
                    if on(2):
                        act.wait_ge(pn_turned, t - 1)
                        need(act, mixed, NCH * (t - 2))
                        nc.scalar.activation(pnT[:, :], bank[7][0:NULL_ROWS, 0:P], ACT.Copy).then_inc(pn_kept, 1)

                def keep_pT(c):
                    if on(2):
                        n = NCH * (t - 2) + c
                        act.wait_ge(p_turned, n + 1)
                        need(act, mixed, n - 1)
                        nc.scalar.activation(pT[:, c % 2, :], bank[turned_bank(t, c)][:, :], ACT.Copy).then_inc(p_kept, 1)

                def keep_sums():
                    if on(0):
                        act.wait_ge(sumsq_made, t + 1)
                        nc.scalar.activation(sums_sb[:, :], bank[7][:, 0:P], ACT.Copy).then_inc(sums_kept, 1)

                def keep_oT(c):
                    if on(3):
                        act.wait_ge(o_turned, 2 * (t - 3) + c + 1)
                        need(act, y_made, t - 3)
                        nc.scalar.activation(oT[:, q, c * HALF * P:(c + 1) * HALF * P], bank[4][:, :],
                                             ACT.Copy).then_inc(oT_kept, 1)

                exp(3, back=2)
                keep_q(0)
                keep_pT(0)
                keep_pn()
                prepare(0)
                keep_q(1)
                prepare(1)
                exp(0)
                keep_pT(1)
                if isinstance(t, int) and t == NB + 1:
                    square_y(0)
                exp(1)
                keep_pT(2)
                keep_sums()
                prepare(2)
                keep_pT(3)
                keep_oT(0)
                exp(2)
                keep_oT(1)

            run_steps(act, step)

            for g in range(NB // 4):
                if g == Y_FIRST // 4:
                    square_y(1)
                act.wait_ge(y_turned, g + 1)
                nc.scalar.activation(YT[:, g * 512:(g + 1) * 512], bank[g % 4][:, :], ACT.Copy).then_inc(yT_kept, 1)
            act.wait_ge(y_normed, 2)
            nc.scalar.activation(send[1][:, :, 0:D], y_sb[:, :, :], ACT.Copy).then_inc(send1_made, 1)
            act.wait_ge(gap_made, 1)
            nc.scalar.activation(share[:, 1, :], share[:, 3, :], ACT.Exp).then_inc(gap_exped, 1)

            def step(u, m, lap, kind):
                if kind(3):
                    n = u - 3
                    act.wait_ge(h_turned, n + 1)
                    need(act, down_made, n - 1)
                    nc.scalar.activation(hT[:, (m - 3) % 2, :], bank[4 + (m - 3) % 2][0:IC, 0:ICH * P],
                                         ACT.Copy).then_inc(hT_kept, 1)
                if kind(0):
                    need(act, up_made, u - 1)
                    if kind(0) == "shared":
                        src = YT[:, bass.ds(u * P, P)]
                    else:
                        act.wait_ge(tile_turned, u - (NB - 1))
                        src = bank[6][:, 0:P]
                    nc.scalar.activation(yh[:, m % 2, :], src, ACT.Copy).then_inc(yh_made, 1)
                if kind(1):
                    n = u - 1
                    act.wait_ge(gate_made, n + 1)
                    need(act, h_made, n - 1)
                    nc.scalar.activation(act_sb[:, (m - 1) % 2, :], bank[2 * ((m - 1) % 2)][:, 0:I], ACT.Silu).then_inc(silu_made, 1)

            run_tiles(act, step)
            load_results(act, 1)

        @block.vector
        def _(dve):
            done = 0

            def own(ins):
                nonlocal done
                done += 1
                ins.then_inc(dve_step, 1)
                dve.wait_ge(dve_step, done)

            def rsqrt(y, v, tmp, own):
                own(nc.vector.tensor_scalar(tmp.bitcast(I32), v.bitcast(I32), 1, None, ALU.logical_shift_right))
                own(nc.vector.tensor_scalar(y.bitcast(I32), tmp.bitcast(I32), -1.0, RSQRT_MAGIC, ALU.mult, ALU.add))
                for k in range(3):
                    own(nc.vector.tensor_tensor(tmp, y, y, ALU.mult))
                    own(nc.vector.scalar_tensor_tensor(tmp, tmp, -0.5, v, ALU.mult, ALU.mult))
                    last = nc.vector.scalar_tensor_tensor(y, tmp, 1.5, y, ALU.add, ALU.mult)
                    if k < 2:
                        own(last)
                return last

            dve.wait_ge(dma_mask, 16)
            nc.vector.tensor_scalar(madd[:, :, 0:S], mask_u8[:, :, :], 1.0, -NEG, ALU.subtract, ALU.mult).then_inc(mask_made, 1)

            def layer_norm_small(g):
                own(nc.vector.bn_stats(bst[:, :], hA[:, :]))
                own(nc.vector.bn_aggr(bmv[:, :], bst[:, :]))
                own(nc.vector.tensor_scalar(brs[:, 0:1], bmv[:, 1:2], EPS, None, ALU.add))
                own(rsqrt(brs[:, 1:2], brs[:, 0:1], brs[:, 2:3], own))
                own(nc.vector.tensor_scalar(hA[:, :], hA[:, :], bmv[:, 0:1], brs[:, 1:2], ALU.subtract, ALU.mult))
                nc.vector.tensor_tensor(hA[:, :], hA[:, :], mlp_r[:, g, :], ALU.mult).then_inc(mlp_normed, 1)


            ma, va, ta, ra = (stat[:, k, 0:NB] for k in range(4))
            dve.wait_ge(dma_x, 16)
            own(nc.vector.tensor_reduce(ma, xs[:, :, :], AX_X, ALU.add))
            own(nc.vector.tensor_scalar(ma, ma, 1.0 / D, None, ALU.mult))
            nc.vector.tensor_tensor(xn[:, :, :], xs[:, :, :], spread(ma, D), ALU.subtract).then_inc(x_centred, 1)
            dve.wait_ge(dma_mlp, 16 * MLP_DMAS)
            nc.vector.tensor_copy(bias[:, :, S], nullb[:, :]).then_inc(mask_made, 1)
            dve.wait_ge(const_made, CONSTS)
            own(nc.vector.scalar_tensor_tensor(hA[:, :], mlp_r[:, 4, :], pos[:, 0:1], mlp_r[:, 0, :], ALU.mult, ALU.add))
            layer_norm_small(1)
            dve.wait_ge(x_squared, 1)
            own(nc.vector.tensor_reduce(va, squares[:, :, :], AX_X, ALU.add))
            own(nc.vector.tensor_scalar(va, va, 1.0 / D, EPS, ALU.mult, ALU.add))
            own(rsqrt(ra, va, ta, own))
            for g in range(NB // 4):
                b = slice(4 * g, 4 * g + 4)
                nc.vector.tensor_tensor(xn[:, b, :], xn[:, b, :], spread(ra[:, b], D), ALU.mult).then_inc(x_normed, 1)

            dve.wait_ge(mlp_turned, 1)
            nc.vector.tensor_copy(hB[:, :], bank[7][:, 0:P]).then_inc(mlp_kept, 1)
            dve.wait_ge(mlp_made, 1)
            own(nc.vector.tensor_tensor(hA[:, :], bank[7][:, 0:P], mlp_r[:, 2, :], ALU.add))
            layer_norm_small(3)
            for g in range(NB // 4):
                dve.wait_ge(kv_made, g + 1)
                kv = bank[g % 4][:, :].rearrange("p (b n) -> p b n", b=4)
                nc.vector.tensor_copy(kraw[:, 4 * g:4 * g + 4, :], kv[:, :, 0:DH])
                nc.vector.tensor_copy(V1[:, 4 * g:4 * g + 4, 0:DH], kv[:, :, DH:2 * DH]).then_inc(k_kept, 1)
            dve.wait_ge(mlp_turned, 2)
            nc.vector.tensor_copy(hB[:, :], bank[7][:, 0:P]).then_inc(mlp_kept, 1)
            dve.wait_ge(mlp_made, 2)
            nc.vector.tensor_tensor(hrev[:, :], bank[7][:, 0:H], b2r[:, :], ALU.add).then_inc(mlp_kept, 1)
            dve.wait_ge(mlp_turned, 3)
            nc.vector.tensor_copy(hrevT[:, 0:P], bank[7][0:H, 0:P]).then_inc(hrev_made, 1)

            dve.wait_ge(k_squared, 1)
            dve.wait_ge(dma_small, 16 * SMALL_DMAS)
            own(nc.vector.tensor_tensor(kq[:, 2, :], kq[:, 0, :], kq[:, 1, :], ALU.mult))
            vk, tk, rk = (stat[:, 4 + k, 0:NB + 1] for k in range(3))
            own(nc.vector.tensor_reduce(vk, ksq[:, :, :], AX_X, ALU.add))
            own(nc.vector.tensor_scalar(vk, vk, NORM_GUARD_SQ, None, ALU.max))
            own(rsqrt(rk, vk, tk, own))
            own(nc.vector.tensor_tensor(kraw[:, :, :], kraw[:, :, :], spread(rk, DH), ALU.mult))
            for g in range(NB // 4):
                b = slice(4 * g, 4 * g + 4 if g < NB // 4 - 1 else NB + 1)
                for k in range(2):
                    last = nc.vector.scalar_tensor_tensor(kdup[:, b, k, :], kraw[:, b, :], SCALE,
                                                          kq[:, 2:3, :].to_broadcast([P, b.stop - b.start, DH]), ALU.mult, ALU.mult)
                last.then_inc(k_normed, 1)
            for g in range(0, NB // 4, 2):
                dve.wait_ge(k_turned, g + 1)
                for k in range(2):
                    rows = slice(k * DH, (k + 1) * DH)
                    last = nc.vector.tensor_copy(KB[rows, 4 * g:4 * g + 4, k, 0:S],
                                                 bank[g % 4][rows, :].rearrange("p (b n) -> p b n", b=4))
                last.then_inc(kT_kept, 1)
            dve.wait_ge(k_turned, NB // 4 + 1)
            for k in range(2):
                rows = slice(k * DH, (k + 1) * DH)
                last = nc.vector.tensor_copy(KB[rows, :, k, S], bank[0][rows, 0:1].to_broadcast([DH, NB]))
            last.then_inc(kT_kept, 1)

            dve.wait_ge(dma_small, 16 * SMALL_DMAS)
            dve.wait_ge(null_made, 3)
            for at in (0, 2 * H, 4 * H):
                rows = slice(at, at + H)
                nc.vector.tensor_copy(NV[rows, :, :], null_v[rows, :, :]).then_inc(null_split, 1)
            rows = slice(2 * H, 3 * H)
            dve.wait_ge(null_split, 3)
            nc.vector.tensor_tensor(NV[rows, :, :], null_v[rows, :, :], NV[rows, :, :].bitcast(F32), ALU.subtract).then_inc(null_split, 1)

            def low_expert(e):
                for k in range(2):
                    dve.wait_ge(expert_kept, 2 * e + k + 1)
                    nc.vector.tensor_tensor(GL[:, e, k, :], bank[5 + k][:, 0:I], GH[:, e, k, :].bitcast(F32),
                                            ALU.subtract).then_inc(expert_low, 1)

            dve.wait_ge(expert_split, 4 * THIRD.start)

            def y_part(k):
                return slice(0, Y_FIRST) if k == 0 else slice(Y_FIRST, NB)

            def centre_y(k):
                b = y_part(k)
                dve.wait_ge(y_kept, b.stop)
                own(nc.vector.tensor_reduce(ma[:, b], y_sb[:, b, :], AX_X, ALU.add))
                own(nc.vector.tensor_scalar(ma[:, b], ma[:, b], 1.0 / D, None, ALU.mult))
                nc.vector.tensor_tensor(y_sb[:, b, :], y_sb[:, b, :], spread(ma[:, b], D), ALU.subtract).then_inc(y_centred, 1)

            def scale_y(k):
                b = y_part(k)
                dve.wait_ge(y_squared, k + 1)
                own(nc.vector.tensor_reduce(va[:, b], y_squares[:, b, :], AX_X, ALU.add))
                own(nc.vector.tensor_scalar(va[:, b], va[:, b], 1.0 / D, EPS, ALU.mult, ALU.add))
                own(rsqrt(ra[:, b], va[:, b], ta[:, b], own))
                own(nc.vector.tensor_tensor(y_sb[:, b, :], y_sb[:, b, :], spread(ra[:, b], D), ALU.mult))

            def gain_y(k):
                b = y_part(k)
                nc.vector.tensor_tensor(y_sb[:, b, :], y_sb[:, b, :], gor[:, :].unsqueeze(1).to_broadcast([P, b.stop - b.start, D]),
                                        ALU.mult).then_inc(y_normed, 1)

            def step(t, p, on):
                q = 1 - p

                def scores(c):
                    if on(1):
                        n = NCH * (t - 1) + c
                        dve.wait_ge(scored, n + 1)
                        dve.wait_ge(biasm_made, n + 1)
                        if c == 0:
                            dve.wait_ge(rnorm_made, t)
                            need(dve, p_turned, NCH * (t - 2))
                            need(dve, pn_split, t - 2)
                            need(dve, shifted, NCH * (t - 2))
                        for k in range(HC):
                            h = c * HC + k
                            src = bank[2 * (c % 2) + k // 2][:, (k % 2) * KEYS:(k % 2 + 1) * KEYS]
                            last = nc.vector.scalar_tensor_tensor(Pb[:, q, h, :], src, rn[:, q, h:h + 1],
                                                                  biasm[:, q, h, :], ALU.mult, ALU.add)
                        last.then_inc(biased, 1)
                        dve.wait_ge(biased, n + 1)
                        nc.vector.tensor_reduce(mx[:, q, c * HC:(c + 1) * HC], Pb[:, q, c * HC:(c + 1) * HC, :],
                                                AX_X, ALU.max).then_inc(maxed, 1)

                def prepare(k):
                    if isinstance(t, int) and t == 0:
                        low_expert(THIRD[k])

                def split_pn():
                    if on(2):
                        dve.wait_ge(exped, NCH * (t - 1))
                        need(dve, pn_turned, t - 2)
                        nc.vector.tensor_copy(pn3[:, 0, :], Pb[:, p, :, S]).then_inc(pn_high, 1)
                        dve.wait_ge(pn_high, t - 1)
                        nc.vector.tensor_copy(pn3[:, 2, :], pn3[:, 0, :].bitcast(F32))
                        nc.vector.tensor_tensor(pn3[:, 4, :], Pb[:, p, :, S], pn3[:, 0, :].bitcast(F32),
                                                ALU.subtract).then_inc(pn_split, 1)

                def keep_o(c):
                    if on(2):
                        n = NCH * (t - 2) + c
                        dve.wait_ge(mixed, n + 1)
                        av = bank[6][:, 0:HC * VW].rearrange("p (h d) -> p h d", h=HC)
                        need(dve, o_kept, n)
                        nc.vector.reciprocal(inv_den[:, :], av[:, :, DH]).then_inc(den_made, 1)
                        dve.wait_ge(den_made, n + 1)
                        if isinstance(t, int) and t == 2:
                            dve.wait_ge(expert_turned, 3 * E)
                        if c == 0:
                            need(dve, o_turned, 2 * (t - 3))
                        nc.vector.tensor_tensor(o_sb[:, p, c * HC * DH:(c + 1) * HC * DH].rearrange("p (h d) -> p h d", h=HC),
                                                av[:, :, 0:DH], spread(inv_den[:, :], DH), ALU.mult).then_inc(o_kept, 1)

                def keep_y():
                    if on(4):
                        dve.wait_ge(y_made, t - 3)
                        nc.vector.tensor_copy(y_sb[:, bass.ds(t - 4, 1), :].rearrange("p a d -> p (a d)"),
                                              bank[7][:, 0:D]).then_inc(y_kept, 1)

                def norms():
                    if on(0):
                        links = 0

                        def link(ins):
                            nonlocal links
                            links += 1
                            ins.then_inc(rnorm_step, 1)
                            dve.wait_ge(rnorm_step, CHAIN * t + links)

                        dve.wait_ge(sums_turned, t + 1)
                        sums = bank[7][:, P:2 * P].rearrange("p (j m) -> p j m", j=GROUPS)[:, :, 0:H // GROUPS]
                        link(nc.vector.tensor_scalar(norm_in[:, 0, 0:H].rearrange("p (i j r) -> p i j r", j=GROUPS, r=2),
                                                     sums.rearrange("p j (i r) -> p i j r", r=2), NORM_GUARD_SQ, None, ALU.max))
                        rsqrt(rn[:, p, :], norm_in[:, 0, 0:H], norm_in[:, 1, 0:H], link).then_inc(rnorm_made, 1)
                        assert links == CHAIN

                split_pn()
                if isinstance(t, int) and t == NB + 1:
                    centre_y(0)
                scores(0)
                scores(1)
                prepare(0)
                prepare(1)
                keep_o(0)
                keep_y()
                keep_o(1)
                scores(2)
                keep_o(2)
                scores(3)
                norms()
                prepare(2)
                keep_o(3)
                if isinstance(t, int) and t == NB + 1:
                    scale_y(0)
                if isinstance(t, int) and t == NB + 2:
                    gain_y(0)

            run_steps(dve, step)

            dve.wait_ge(router_turned, 1)
            nc.vector.tensor_copy(router_wT[:, 0:NE], bank[4][:, 0:NE]).then_inc(router_kept, 1)
            centre_y(1)
            scale_y(1)
            gain_y(1)

            for k in range(TOP):
                nc.vector.tensor_copy(send[k][:, :, DEST_AT].bitcast(I32), dest[:, k, :]).then_inc((send0_made, send1_made)[k], 1)
            dve.wait_ge(logits_made, 1)
            own(nc.vector.tensor_tensor(L[:, :, :], bank[5][:, 0:NB * NE].rearrange("p (b e) -> p b e", b=NB),
                                        rbr[:, :].unsqueeze(1).to_broadcast([P, NB, NE]), ALU.add))
            for k in range(TOP):
                own(nc.vector.tensor_reduce(best[:, k, :], L[:, :, :], AX_X, ALU.max))
                own(nc.vector.tensor_tensor(equal[:, :, :], L[:, :, :], spread(best[:, k, :], NE), ALU.is_equal))
                own(nc.vector.scalar_tensor_tensor(equal[:, :, :], equal[:, :, :], -float(NE),
                                                   iota7[:, :].unsqueeze(1).to_broadcast([P, NB, NE]), ALU.mult, ALU.add))
                own(nc.vector.tensor_reduce(share[:, 0, :], equal[:, :, :], AX_X, ALU.min))
                own(nc.vector.tensor_tensor(chosen[:, k, :, :], equal[:, :, :], spread(share[:, 0, :], NE), ALU.is_equal))
                if k == 0:
                    own(nc.vector.scalar_tensor_tensor(L[:, :, :], chosen[:, 0, :, :], 2 * NEG, L[:, :, :], ALU.mult, ALU.add))
            nc.vector.tensor_tensor(load[:, :, :], chosen[:, 0, :, :], chosen[:, 1, :, :], ALU.add).then_inc(load_made, 1)
            nc.vector.tensor_tensor(share[:, 3, :], best[:, 1, :], best[:, 0, :], ALU.subtract).then_inc(gap_made, 1)

            dve.wait_ge(sort_consts, 4)
            dve.wait_ge(ranks_made, 1)
            tot = bank[7][:, 0:NB * NE].rearrange("p (b e) -> p b e", b=NB)
            nc.vector.tensor_copy(totals[:, :, :], tot)
            own(nc.vector.tensor_copy(run_up[:, 0, PAD:PAD + NB, :], tot))
            own(nc.vector.tensor_tensor(place[:, :, :], bank[6][:, 0:NB * NE].rearrange("p (b e) -> p b e", b=NB),
                                        totals[:, :, :], ALU.subtract))
            side, far = 0, 1
            while far < NB:
                own(nc.vector.tensor_tensor(run_up[:, 1 - side, PAD:PAD + NB, :], run_up[:, side, PAD:PAD + NB, :],
                                            run_up[:, side, PAD - far:PAD - far + NB, :], ALU.add))
                side, far = 1 - side, 2 * far
            own(nc.vector.tensor_tensor(place[:, :, :], place[:, :, :], run_up[:, side, PAD:PAD + NB, :], ALU.add))
            own(nc.vector.tensor_scalar(tiles_int[:, 0, :], run_up[:, side, PAD + NB - 1, :], float(P - 1), None, ALU.add))
            own(nc.vector.tensor_scalar(tiles_int[:, 1, :], tiles_int[:, 0, :], P.bit_length() - 1, None, ALU.logical_shift_right))
            nc.vector.tensor_copy(tiles_of[:, :], tiles_int[:, 1, :])
            own(nc.vector.tensor_copy(tiles_up[:, 0, EPAD:EPAD + NE], tiles_int[:, 1, :]))
            side, far = 0, 1
            while far < NE:
                own(nc.vector.tensor_tensor(tiles_up[:, 1 - side, EPAD:EPAD + NE], tiles_up[:, side, EPAD:EPAD + NE],
                                            tiles_up[:, side, EPAD - far:EPAD - far + NE], ALU.add))
                side, far = 1 - side, 2 * far
            ends = tiles_up[:, side, EPAD:EPAD + NE]
            own(nc.vector.tensor_tensor(tiles_of[:, :], ends, tiles_of[:, :], ALU.subtract))
            own(nc.vector.scalar_tensor_tensor(place[:, :, :], tiles_of[:, :].unsqueeze(1).to_broadcast([P, NB, NE]), float(P),
                                               place[:, :, :], ALU.mult, ALU.add))
            for k in range(TOP):
                last = nc.vector.tensor_tensor(placed[:, k, :, :], chosen[:, k, :, :], place[:, :, :], ALU.mult)
            own(last)
            own(nc.vector.tensor_reduce(row_of[:, :, :], placed[:, :, :, :], AX_X, ALU.add))
            nc.vector.tensor_copy(row_index[:, :, :], row_of[:, :, :]).then_inc(row_index_made, 1)
            dve.wait_ge(gap_exped, 1)
            own(nc.vector.tensor_scalar(share[:, 2, :], share[:, 1, :], 1.0, None, ALU.add))
            own(nc.vector.reciprocal(share[:, 2, :], share[:, 2, :]))
            nc.vector.tensor_copy(send[0][:, :, SHARE_AT], share[:, 2, :]).then_inc(send0_made, 1)
            nc.vector.tensor_tensor(send[1][:, :, SHARE_AT], share[:, 2, :], share[:, 1, :], ALU.mult).then_inc(send1_made, 1)
            own(nc.vector.tensor_tensor(passed[:, :, :], spread(iota_tile[:, :], NE - 1),
                                        ends[:, 0:NE - 1].unsqueeze(1).to_broadcast([P, ROUTED, NE - 1]), ALU.is_ge))
            own(nc.vector.tensor_reduce(tile_float[:, :], passed[:, :, :], AX_X, ALU.add))
            nc.vector.tensor_scalar(tile_expert[:, RING:RING + ROUTED], tile_float[:, :], 1.0, None, ALU.add).then_inc(table_made, 1)

            own(nc.vector.memset(h_sb[:, :, I:ICH * IC], 0.0))

            def step(u, m, lap, kind):
                if kind(0):
                    if kind(0) == "routed":
                        r = u - NB
                        dve.wait_ge(rows_loaded[m], 16 * (lap - NB // RING + 1))
                        src = bank[6][:, 0:P]
                    else:
                        src = YT[:, bass.ds(u * P, P)]
                    dve.wait_ge(yh_made, u + 1)
                    nc.vector.tensor_tensor(yl[:, m % 2, :], src, yh[:, m % 2, :].bitcast(F32), ALU.subtract).then_inc(yl_made, 1)
                    if kind(0) == "routed":
                        nc.vector.tensor_copy(share_of[:, bass.ds(r, 1)], rows_in[:, m, SHARE_AT:DEST_AT])
                        nc.vector.tensor_copy(dest_of[:, bass.ds(r, 1)], rows_in[:, m, DEST_AT:ROW].bitcast(U32)).then_inc(dest_kept, 1)
                if kind(1):
                    n, q = u - 1, (m - 1) % 2
                    dve.wait_ge(silu_made, n + 1)
                    dve.wait_ge(up_made, n + 1)
                    need(dve, h_turned, n - 1)
                    up = bank[2 * q + 1][:, 0:I]
                    if kind(1) == "shared":
                        ins = nc.vector.tensor_tensor(h_sb[:, q, 0:I], act_sb[:, q, :], up, ALU.mult)
                    else:
                        dve.wait_ge(dest_kept, n - NB + 1)
                        ins = nc.vector.scalar_tensor_tensor(h_sb[:, q, 0:I], act_sb[:, q, :], share_of[:, bass.ds(n - NB, 1)],
                                                             up, ALU.mult, ALU.mult)
                    ins.then_inc(h_made, 1)
                if kind(3):
                    n, q = u - 3, (m - 3) % RING
                    dve.wait_ge(down_made, n + 1)
                    if kind(3) == "shared":
                        xb = xs[:, bass.ds(n, 1), :].rearrange("p a d -> p (a d)")
                        nc.vector.tensor_tensor(xb, bank[7][:, 0:D], xb, ALU.add).then_inc(down_kept, 1)
                    else:
                        lap_n = lap - (1 if m < 3 else 0)
                        need(dve, result_sent[q], 16 * (lap_n - NB // RING))
                        nc.vector.tensor_copy(result[:, q, :], bank[7][:, 0:D])
                        nc.vector.tensor_copy(dest_ring[:, q:q + 1], dest_of[:, bass.ds(n - NB, 1)]).then_inc(down_kept, 1)

            run_tiles(dve, step)

            dve.wait_ge(down_kept, TILES)
            for g in range(NB // 4):
                dve.wait_ge(result_loaded[g], 16 * TOP)
                xg = xs[:, 4 * g:4 * g + 4, :]
                own(nc.vector.tensor_tensor(xg, xg, result_in[0][:, 4 * g:4 * g + 4, :], ALU.add))
                nc.vector.tensor_tensor(xg, xg, result_in[1][:, 4 * g:4 * g + 4, :], ALU.add).then_inc(fin_made, 1)

        @block.tensor
        def _(pe):
            def turn(out, in_):
                n = in_.shape[0]
                return nc.tensor.transpose(out, in_, ident[0:n, 0:n])

            def mm(out, a, b, start, stop):
                return nc.tensor.matmul(out, a, b, start=start, stop=stop, skip_group_check=True)

            def bias_layer(k, w):
                pe.wait_ge(mlp_active, k + 1)
                turn(bank[7][:, 0:P], hA[:, :]).then_inc(mlp_turned, 1)
                pe.wait_ge(mlp_kept, k + 1)
                mm(bank[7][:, 0:w.shape[1]], hB[:, :], w, True, True).then_inc(mlp_made, 1)

            pe.wait_ge(const_made, CONSTS)
            pe.wait_ge(dma_mlp, 16 * MLP_DMAS)
            def expert(n):
                p, first = n % len(graw), n == 0
                pe.wait_ge(dma_expert[p], 16 * EXPERT_DMAS * (n // len(graw) + 1))
                for k in range(2):
                    if not first:
                        if n - 1 in THIRD:
                            pe.wait_ge(expert_low, 2 * (n - 1 - THIRD.start) + k + 1)
                        else:
                            pe.wait_ge(expert_kept, 2 * (n - 1) + k + 1)
                    for c in range(ICH):
                        w = min(IC, I - c * IC)
                        last = turn(bank[5 + k][:, c * IC:c * IC + w], graw[p][0:w, k, c, :])
                    last.then_inc(expert_turned, 1)
                if not first:
                    pe.wait_ge(expert_down, n)
                for c in range(ICH):
                    last = turn(bank[down_bank(n)][0:IC, c * P:(c + 1) * P], draw[p][:, c * IC:(c + 1) * IC])
                last.then_inc(expert_turned, 1)

            for n in FIRST:
                expert(n)
            bias_layer(0, mlp_w[:, 0, :])
            pe.wait_ge(w_scaled, 2)
            for g in range(NB // 4 + 1):
                if g < NB // 4:
                    pe.wait_ge(x_normed, g + 1)
                    for k in range(4):
                        last = turn(bank[g][:, k * P:(k + 1) * P], xn[:, 4 * g + k, :])
                    last.then_inc(x_turned, 1)
                if g > 0:
                    pe.wait_ge(xT_kept, g)
                    for b in range(4 * g - 4, 4 * g):
                        last = mm(bank[g - 1][:, (b % 4) * P:(b % 4 + 1) * P], xnT[:, b * P:(b + 1) * P], wkv_sb[:, :], True, True)
                    last.then_inc(kv_made, 1)
            bias_layer(1, w2_sb[:, :])
            pe.wait_ge(mlp_kept, 3)
            turn(bank[7][0:H, 0:P], hrev[:, :]).then_inc(mlp_turned, 1)
            for n in SECOND:
                expert(n)
            for b in range(NB + 1):
                if b < NB and b % 4 == 0:
                    pe.wait_ge(k_normed, b // 4 + 1)
                if b == NB:
                    pe.wait_ge(kT_kept, 1)
                last = turn(bank[b // 4 % 4][:, (b % 4) * P:(b % 4 + 1) * P], kdup[:, b, :, :].rearrange("p a d -> p (a d)"))
                if b % 4 == 3 or b == NB:
                    last.then_inc(k_turned, 1)

            pe.wait_ge(kT_kept, NB // 8 + 1)
            pe.wait_ge(kT_odd_kept, NB // 8)
            pe.wait_ge(null_split, 4)
            pe.wait_ge(dma_wo, 16)

            def step(t, p, on):
                q = 1 - p
                if isinstance(t, int) and t > NB:
                    pe.wait_ge(y_kept, t - 4)

                def scores(c):
                    if on(1):
                        n = NCH * (t - 1) + c
                        pe.wait_ge(q_kept, 2 * t)
                        if isinstance(t, int) and t == 1 and c == 1:
                            pe.wait_ge(expert_low, 2 * len(THIRD))
                            pe.wait_ge(expert_down, E)
                        need(pe, biased, n - 1)
                        for k in range(2):
                            tile = 2 * c + k
                            last = mm(bank[2 * (c % 2) + k][:, 0:2 * KEYS], qT[:, q, tile * P:(tile + 1) * P],
                                      KB[:, bass.ds(t - 1, 1), :, :].rearrange("p a k n -> p (a k n)"), True, True)
                        last.then_inc(scored, 1)

                def queries(c):
                    if on(0):
                        if c == 0:
                            need(pe, oT_kept, 2 * (t - 3))
                        else:
                            pe.wait_ge(q_kept, 2 * t + 1)
                        for k in range(HALF):
                            tile = c * HALF + k
                            last = mm(bank[4][:, k * P:(k + 1) * P], wq_sb[:, tile * P:(tile + 1) * P],
                                      xnT[:, bass.ds(t * P, P)], True, True)
                        last.then_inc(q_made, 1)

                def prepare(k):
                    if isinstance(t, int) and t == 0:
                        expert(THIRD[k])

                def turn_pn():
                    if on(2):
                        pe.wait_ge(pn_split, t - 1)
                        need(pe, rnorm_made, min(t, NB) if isinstance(t, int) else t)
                        turn(bank[7][0:NULL_ROWS, 0:P], pn3[:, :, :].rearrange("p a h -> p (a h)").bitcast(F32)).then_inc(pn_turned, 1)

                def turn_p(c):
                    if on(2):
                        n = NCH * (t - 2) + c
                        pe.wait_ge(exped, n + 1)
                        at = turned_bank(t, c)
                        if at == 5:
                            need(pe, p_kept, n)
                        for k in range(HC):
                            last = turn(bank[at][:, k * P:(k + 1) * P], Pb[:, p, c * HC + k, 0:S])
                        last.then_inc(p_turned, 1)

                def mix(c):
                    if on(2):
                        n = NCH * (t - 2) + c
                        pe.wait_ge(p_kept, n + 1)
                        pe.wait_ge(pn_kept, t - 1)
                        need(pe, o_kept, n)
                        mm(bank[6][:, 0:HC * VW], pnT[:, :],
                           NV[:, c * HC:(c + 1) * HC, :].rearrange("p h d -> p (h d)"), True, False)
                        for k in range(HC):
                            last = mm(bank[6][:, k * VW:(k + 1) * VW], pT[:, c % 2, k * P:(k + 1) * P],
                                      V1[:, bass.ds(t - 2, 1), :].rearrange("p a d -> p (a d)"), False, k == HC - 1)
                        last.then_inc(mixed, 1)

                def project():
                    if on(4):
                        if not isinstance(t, int) or t - 2 < NB:
                            pe.wait_ge(pn_kept, t - 1)
                        pe.wait_ge(oT_kept, 2 * (t - 3))
                        for k in range(QT):
                            last = mm(bank[7][:, 0:D], oT[:, p, k * P:(k + 1) * P], wo_sb[:, k, :], k == 0, k == QT - 1)
                        last.then_inc(y_made, 1)

                def sum_squares():
                    if on(0):
                        pe.wait_ge(q_squared, 2 * t + 2)
                        need(pe, y_kept, t - 3)
                        if not isinstance(t, int) or t >= 2:
                            pe.wait_ge(pn_kept, t - 1)
                        for k in range(QT):
                            i, j = divmod(k, GROUPS)
                            last = mm(bank[7][j * (P // GROUPS):(j + 1) * (P // GROUPS), 0:P], hsel[:, i, :],
                                      sq[:, k * P:(k + 1) * P], i == 0, k >= QT - GROUPS)
                        last.then_inc(sumsq_made, 1)

                def turn_sums():
                    if on(0):
                        pe.wait_ge(sums_kept, t + 1)
                        turn(bank[7][:, P:2 * P], sums_sb[:, :]).then_inc(sums_turned, 1)

                def turn_o(c):
                    if on(3):
                        if c == 0:
                            pe.wait_ge(o_kept, NCH * (t - 2))
                            pe.wait_ge(q_kept, 2 * t + 2 if not isinstance(t, int) or t < NB else 2 * NB)
                        need(pe, oT_kept, 2 * (t - 3) + c)
                        for k in range(HALF):
                            tile = c * HALF + k
                            last = turn(bank[4][:, k * P:(k + 1) * P], o_sb[:, q, tile * P:(tile + 1) * P])
                        last.then_inc(o_turned, 1)

                if isinstance(t, int) and t == NB + 1:
                    for c in range(NCH - 1):
                        turn_p(c)
                    turn_pn()
                    turn_p(NCH - 1)
                    mix(0)
                    mix(1)
                    project()
                    turn_o(0)
                    mix(2)
                    mix(3)
                    turn_o(1)
                    return
                scores(0)
                queries(0)
                turn_p(0)
                scores(1)
                turn_pn()
                prepare(0)
                queries(1)
                prepare(1)
                mix(0)
                turn_p(1)
                project()
                scores(2)
                mix(1)
                turn_p(2)
                sum_squares()
                scores(3)
                mix(2)
                turn_p(3)
                turn_o(0)
                turn_sums()
                prepare(2)
                mix(3)
                turn_o(1)

            run_steps(pe, step)

            turn(bank[4][:, 0:NE], router_sb[:, :]).then_inc(router_turned, 1)
            for batches in (range(Y_FIRST), range(Y_FIRST, NB)):
                pe.wait_ge(y_normed, 1 if batches.start == 0 else 2)
                for b in batches:
                    last = turn(bank[b // 4][:, (b % 4) * P:(b % 4 + 1) * P], y_sb[:, b, :])
                    if b % 4 == 3:
                        last.then_inc(y_turned, 1)
                pe.wait_ge(router_kept, 1)
                for b in batches:
                    if b % 4 == 0:
                        pe.wait_ge(yT_kept, b // 4 + 1)
                    last = mm(bank[5][:, b * NE:(b + 1) * NE], YT[:, b * P:(b + 1) * P], router_wT[:, 0:NE], True, True)
            last.then_inc(logits_made, 1)

            pe.wait_ge(load_made, 1)
            pe.wait_ge(sort_consts, 4)
            load_flat = load[:, :, :].rearrange("p b e -> p (b e)")
            mm(bank[6][:, 0:NB * NE], before[:, :], load_flat, True, True)
            mm(bank[7][:, 0:NB * NE], ones[:, :], load_flat, True, True).then_inc(ranks_made, 1)

            expert_of = {}
            expert_regs = [pe.alloc_register(f"expert_reg{k}") for k in range(2 * RING)]

            def step(u, m, lap, kind):
                if m == 0 and (not isinstance(u, int) or u >= NB) and kind(0) != "shared":
                    pe.load(expert_regs, tile_expert[0:1, bass.ds(u - NB, 2 * RING)])
                    for at in range(-3, RING - 1):
                        expert_of[at] = pe.snap(expert_regs[at + RING], min_val=1, max_val=NE)
                if kind(0) == "routed":
                    r = u - NB
                    pe.wait_ge(rows_loaded[m], 16 * (lap - NB // RING + 1))
                    pe.wait_ge(yl_made, u)
                    turn(bank[6][:, 0:P], rows_in[:, m, 0:D]).then_inc(tile_turned, 1)
                if kind(1):
                    n, q = u - 1, (m - 1) % 2
                    e = 0 if kind(1) == "shared" else expert_of[m - 1]
                    pe.wait_ge(yl_made, n + 1)
                    need(pe, h_made, n - 1)
                    for k, made in ((0, gate_made), (1, up_made)):
                        o = bank[2 * q + k][:, 0:I]
                        high, low = (w[:, bass.ds(e, 1), k, :].rearrange("p a i -> p (a i)") for w in (GH, GL))
                        mm(o, yh[:, q, :], high, True, False)
                        mm(o, yh[:, q, :], low, False, False)
                        mm(o, yl[:, q, :], high, False, True).then_inc(made, 1)
                if kind(3):
                    n, q = u - 3, (m - 3) % 2
                    e = 0 if kind(3) == "shared" else expert_of[m - 3]
                    pe.wait_ge(hT_kept, n + 1)
                    need(pe, down_kept, n)
                    for c in range(ICH):
                        last = mm(bank[7][:, 0:D], hT[:, q, c * P:(c + 1) * P],
                                  DT[:, bass.ds(e, 1), c, :].rearrange("p a d -> p (a d)"), c == 0, c == ICH - 1)
                    last.then_inc(down_made, 1)
                if kind(2):
                    n, q = u - 2, (m - 2) % 2
                    pe.wait_ge(h_made, n + 1)
                    need(pe, hT_kept, n - 1)
                    for c in range(ICH):
                        last = turn(bank[4 + q][0:IC, c * P:(c + 1) * P], h_sb[:, q, c * IC:(c + 1) * IC])
                    last.then_inc(h_turned, 1)

            pe.wait_ge(table_made, 1)
            pe.wait_ge(expert_split, 4 * THIRD.start)
            run_tiles(pe, step)


_INS = ['x', 'cond_64', 'mask_BxS_bf1', 'L0_cond_g_norm', 'L0_cond_Wq', 'L0_cond_Wkv', 'L0_cond_q_scale',
        'L0_cond_k_scale', 'L0_cond_null_attn_bias', 'L0_cond_w0', 'L0_cond_b0', 'L0_cond_g0', 'L0_cond_w1',
        'L0_cond_b1', 'L0_cond_g1', 'L0_cond_w2', 'L0_cond_b2', 'L0_cond_Wout', 'L0_cond_g_out', 'L0_ffn_sg',
        'L0_ffn_su', 'L0_ffn_sd', 'L0_ffn_rg', 'L0_ffn_ru', 'L0_ffn_rd', 'L0_ffn_wr', 'L0_ffn_rb']
_OUTS = [((16, 128, 128), 'float32')]


def kernel(**inputs):
    import numpy as _np
    import concourse.bacc as _bacc
    from concourse import mybir as _mybir
    from concourse.bass_utils import run_bass_kernel_spmd as _run

    nc = _bacc.Bacc("TRN2", target_bir_lowering=False, num_devices=1)
    arrays, args = {}, []
    for name in _INS:
        a = _np.ascontiguousarray(inputs[name])
        arrays[f"in_{name}_dram"] = a
        args.append(nc.dram_tensor(f"in_{name}_dram", a.shape, _mybir.dt.from_np(a.dtype), kind="ExternalInput").ap())
    for i, (shape, dtype) in enumerate(_OUTS):
        dt = _mybir.dt.from_np(_np.dtype(dtype))
        args.append(nc.dram_tensor(f"out_{i}_dram", shape, dt, kind="ExternalOutput").ap())
    adaln_ffn_kernel(nc, *args)
    r = _run(nc, [arrays], core_ids=[0])
    got = tuple(r.results[0][f"out_{i}_dram"] for i in range(len(_OUTS)))
    return got[0]
```
